# Optimizing a Trainium2 kernel written in Bass

```python
import numpy as np
import jax
import jax.numpy as jnp

def _softmax(x, axis=-1):
    return jax.nn.softmax(x, axis=axis)

def _gelu(x):
    return jax.nn.gelu(x, approximate=True)

def _silu(x):
    return jax.nn.silu(x)

def _sigmoid(x):
    return jax.nn.sigmoid(x)

def _layernorm(x, axis=-1, eps=1e-05):
    m = jnp.mean(x, axis=axis, keepdims=True)
    v = jnp.var(x, axis=axis, keepdims=True)
    return (x - m) / jnp.sqrt(v + eps)

def _scatter_add(tgt, idx, src, axis=0):
    return tgt.at[idx].add(src)

def _segment_sum(src, seg, n):
    return jax.ops.segment_sum(src, seg, n)
kernel_name = 'mk_xattn_seq_d2_seqx_r4_78b9ad'

def setup_inputs(seed: int=0):
    np.random.seed(seed)
    _w = jnp.asarray

    def _rec_inputs():
        import jax
        import jax.numpy as jnp
        _rk = jax.random.key(seed)
        x = -0.0002928 + 1 * jax.random.normal(jax.random.fold_in(_rk, 1), (16, 128, 512), jnp.float32)
        _lenS = 128 - jax.random.randint(jax.random.fold_in(_rk, 7), (16,), 0, max(1, 128 // 4) + 1, jnp.int32)
        _lenS2 = 128 - jax.random.randint(jax.random.fold_in(_rk, 8), (16,), 0, max(1, 128 // 4) + 1, jnp.int32)
        _ctx_2048P = jax.random.normal(jax.random.fold_in(_rk, 11), (16, 16, 512), jnp.float32)
        _ctx_2048c = jax.random.dirichlet(jax.random.fold_in(_rk, 511), 0.3 * jnp.ones((16,), jnp.float32), (16, 128))
        _ctx_2048t = jnp.einsum('bsk,bkd->bsd', _ctx_2048c, _ctx_2048P)
        _ctx_2048t = _ctx_2048t * jax.lax.rsqrt(jnp.mean(jnp.square(_ctx_2048t)) + 1e-12) * 0.953939
        ctx_2048 = 0.000189249 + 0.0999589 * (_ctx_2048t + 0.3 * jax.random.normal(jax.random.fold_in(_rk, 611), (16, 128, 512), jnp.float32))
        return (x, ctx_2048)
    x, ctx_2048 = _rec_inputs()

    def _L0_xattn_setup():
        import jax, jax.numpy as jnp
        import numpy as np
        B, L, E, H = (4, 128, 512, 32)
        S = E // H
        EXTRA_MAA, EXTRA_DECAY = (32, 64)
        EPS = 1e-05

        def _ln(x, w, b):
            m = jnp.mean(x, axis=-1, keepdims=True)
            v = jnp.mean((x - m) ** 2, axis=-1, keepdims=True)
            return (x - m) * jax.lax.rsqrt(v + EPS) * w + b

        def _token_shift(xn, prev_row):
            first = (prev_row - xn[:, 0])[:, None]
            rest = xn[:, :-1] - xn[:, 1:]
            return jnp.concatenate([first, rest], axis=1)
        key = jax.random.key(seed)
        ks = jax.random.split(key, 24)
        rn = lambda k, shp, s=1.0: jax.random.normal(k, shp, dtype=jnp.float32) * s
        return dict(x=rn(ks[0], (B, L, E)), state=rn(ks[1], (B, 2 + S, E), 0.1), ln1_w=jnp.ones((E,), jnp.float32), ln1_b=jnp.zeros((E,), jnp.float32), ln2_w=jnp.ones((E,), jnp.float32), ln2_b=jnp.zeros((E,), jnp.float32), maa_x=rn(ks[2], (E,), 0.02), maa_w1=rn(ks[3], (E, 5 * EXTRA_MAA), 0.02), maa_w2=rn(ks[4], (5, EXTRA_MAA, E), 0.02), maa_stack=rn(ks[5], (5, E), 0.02), time_decay=rn(ks[6], (E,), 0.5), decay_w1=rn(ks[7], (E, EXTRA_DECAY), 0.02), decay_w2=rn(ks[8], (EXTRA_DECAY, E), 0.02), faaaa=rn(ks[9], (H, S), 0.1), Wr=rn(ks[10], (E, E), 0.02), Wk=rn(ks[11], (E, E), 0.02), Wv=rn(ks[12], (E, E), 0.02), Wg=rn(ks[13], (E, E), 0.02), Wo=rn(ks[14], (E, E), 0.02), gn_w=jnp.ones((E,), jnp.float32), gn_b=jnp.zeros((E,), jnp.float32), ffn_maa_k=rn(ks[15], (E,), 0.02), ffn_maa_r=rn(ks[16], (E,), 0.02), ffn_Wk=rn(ks[17], (E, E), 0.02), ffn_Wr=rn(ks[18], (E, E), 0.02), ffn_Wv=rn(ks[19], (E, E), 0.02), i=0)
    _L0_xattn_all = _L0_xattn_setup()
    _L0_xattn_in = {k: v for k, v in _L0_xattn_all.items() if k in ('ln1_w', 'ln1_b', 'ln2_w', 'ln2_b', 'maa_x', 'maa_w1', 'maa_w2', 'maa_stack', 'time_decay', 'decay_w1', 'decay_w2', 'faaaa', 'Wr', 'Wk', 'Wv', 'Wg', 'Wo', 'gn_w', 'gn_b', 'ffn_maa_k', 'ffn_maa_r', 'ffn_Wk', 'ffn_Wr', 'ffn_Wv')}
    del _L0_xattn_all

    def _L1_xattn_setup():
        import jax, jax.numpy as jnp
        import numpy as np
        B, Q, S1, S2 = (4, 64, 512, 512)
        D, H, K, F = (512, 16, 128, 2048)
        LN_EPS = 1e-05

        def _layer_norm(x, scale, offset):
            mu = jnp.mean(x, axis=-1, keepdims=True)
            var = jnp.var(x, axis=-1, keepdims=True)
            return (x - mu) * jax.lax.rsqrt(var + LN_EPS) * scale + offset

        def _cross_attention(q_in, kv_in, wq, bq, wk, bk, wv, bv, wo, bo, bias_k, bias_v):
            b, q_len, _ = q_in.shape
            t = kv_in.shape[1]
            qh = (q_in @ wq + bq).reshape(b, q_len, H, K)
            kh = (kv_in @ wk + bk).reshape(b, t, H, K)
            vh = (kv_in @ wv + bv).reshape(b, t, H, K)
            kh = jnp.concatenate([kh, jnp.broadcast_to(bias_k, (b, 1, H, K))], axis=1)
            vh = jnp.concatenate([vh, jnp.broadcast_to(bias_v, (b, 1, H, K))], axis=1)
            scale = jnp.sqrt(jnp.asarray(K, q_in.dtype))
            logits = jnp.einsum('bqhk,bthk->bhqt', qh, kh) / scale
            weights = jax.nn.softmax(logits, axis=-1)
            ctx = jnp.einsum('bhqt,bthk->bqhk', weights, vh).reshape(b, q_len, H * K)
            return ctx @ wo + bo

        def _forward(x, xf_1, xf_2, ln1_scale, ln1_offset, wq1, bq1, wk1, bk1, wv1, bv1, wo1, bo1, bias_k1, bias_v1, ln2_scale, ln2_offset, wq2, bq2, wk2, bk2, wv2, bv2, wo2, bo2, bias_k2, bias_v2, ln_mlp_scale, ln_mlp_offset, w_fc1, b_fc1, w_fc2, b_fc2):
            res = x
            h = _layer_norm(x, ln1_scale, ln1_offset)
            x = res + _cross_attention(h, xf_1, wq1, bq1, wk1, bk1, wv1, bv1, wo1, bo1, bias_k1, bias_v1)
            res = x
            h = _layer_norm(x, ln2_scale, ln2_offset)
            x = res + _cross_attention(h, xf_2, wq2, bq2, wk2, bk2, wv2, bv2, wo2, bo2, bias_k2, bias_v2)
            h = _layer_norm(x, ln_mlp_scale, ln_mlp_offset)
            h = jax.nn.gelu(h @ w_fc1 + b_fc1, approximate=False) @ w_fc2 + b_fc2
            return x + h
        key = jax.random.key(seed)
        ks = iter(jax.random.split(key, 64))

        def rn(shape, s=0.02):
            return jax.random.normal(next(ks), shape, jnp.float32) * s
        inp = {'x': rn((B, Q, D), 1.0), 'xf_1': rn((B, S1, D), 1.0), 'xf_2': rn((B, S2, D), 1.0)}
        for i in (1, 2):
            inp[f'ln{i}_scale'] = jnp.ones((D,), jnp.float32)
            inp[f'ln{i}_offset'] = jnp.zeros((D,), jnp.float32)
            inp[f'wq{i}'] = rn((D, H * K))
            inp[f'bq{i}'] = jnp.zeros((H * K,), jnp.float32)
            inp[f'wk{i}'] = rn((D, H * K))
            inp[f'bk{i}'] = jnp.zeros((H * K,), jnp.float32)
            inp[f'wv{i}'] = rn((D, H * K))
            inp[f'bv{i}'] = jnp.zeros((H * K,), jnp.float32)
            inp[f'wo{i}'] = rn((H * K, D))
            inp[f'bo{i}'] = jnp.zeros((D,), jnp.float32)
            inp[f'bias_k{i}'] = rn((1, 1, H, K))
            inp[f'bias_v{i}'] = rn((1, 1, H, K))
        inp['ln_mlp_scale'] = jnp.ones((D,), jnp.float32)
        inp['ln_mlp_offset'] = jnp.zeros((D,), jnp.float32)
        inp['w_fc1'] = rn((D, F))
        inp['b_fc1'] = jnp.zeros((F,), jnp.float32)
        inp['w_fc2'] = rn((F, D))
        inp['b_fc2'] = jnp.zeros((D,), jnp.float32)
        return inp
    _L1_xattn_all = _L1_xattn_setup()
    _L1_xattn_in = {k: v for k, v in _L1_xattn_all.items() if k in ('ln1_scale', 'ln1_offset', 'wq1', 'bq1', 'wk1', 'bk1', 'wv1', 'bv1', 'wo1', 'bo1', 'bias_k1', 'bias_v1', 'ln2_scale', 'ln2_offset', 'wq2', 'bq2', 'wk2', 'bk2', 'wv2', 'bv2', 'wo2', 'bo2', 'bias_k2', 'bias_v2', 'ln_mlp_scale', 'ln_mlp_offset', 'w_fc1', 'b_fc1', 'w_fc2', 'b_fc2')}
    del _L1_xattn_all
    return {'x': x, 'ctx_2048': ctx_2048, 'L0_xattn_ln1_w': _L0_xattn_in['ln1_w'], 'L0_xattn_ln1_b': _L0_xattn_in['ln1_b'], 'L0_xattn_ln2_w': _L0_xattn_in['ln2_w'], 'L0_xattn_ln2_b': _L0_xattn_in['ln2_b'], 'L0_xattn_maa_x': _L0_xattn_in['maa_x'], 'L0_xattn_maa_w1': _L0_xattn_in['maa_w1'], 'L0_xattn_maa_w2': _L0_xattn_in['maa_w2'], 'L0_xattn_maa_stack': _L0_xattn_in['maa_stack'], 'L0_xattn_time_decay': _L0_xattn_in['time_decay'], 'L0_xattn_decay_w1': _L0_xattn_in['decay_w1'], 'L0_xattn_decay_w2': _L0_xattn_in['decay_w2'], 'L0_xattn_faaaa': _L0_xattn_in['faaaa'], 'L0_xattn_Wr': _L0_xattn_in['Wr'], 'L0_xattn_Wk': _L0_xattn_in['Wk'], 'L0_xattn_Wv': _L0_xattn_in['Wv'], 'L0_xattn_Wg': _L0_xattn_in['Wg'], 'L0_xattn_Wo': _L0_xattn_in['Wo'], 'L0_xattn_gn_w': _L0_xattn_in['gn_w'], 'L0_xattn_gn_b': _L0_xattn_in['gn_b'], 'L0_xattn_ffn_maa_k': _L0_xattn_in['ffn_maa_k'], 'L0_xattn_ffn_maa_r': _L0_xattn_in['ffn_maa_r'], 'L0_xattn_ffn_Wk': _L0_xattn_in['ffn_Wk'], 'L0_xattn_ffn_Wr': _L0_xattn_in['ffn_Wr'], 'L0_xattn_ffn_Wv': _L0_xattn_in['ffn_Wv'], 'L1_xattn_ln1_scale': _L1_xattn_in['ln1_scale'], 'L1_xattn_ln1_offset': _L1_xattn_in['ln1_offset'], 'L1_xattn_wq1': _L1_xattn_in['wq1'], 'L1_xattn_bq1': _L1_xattn_in['bq1'], 'L1_xattn_wk1': _L1_xattn_in['wk1'], 'L1_xattn_bk1': _L1_xattn_in['bk1'], 'L1_xattn_wv1': _L1_xattn_in['wv1'], 'L1_xattn_bv1': _L1_xattn_in['bv1'], 'L1_xattn_wo1': _L1_xattn_in['wo1'], 'L1_xattn_bo1': _L1_xattn_in['bo1'], 'L1_xattn_bias_k1': _L1_xattn_in['bias_k1'], 'L1_xattn_bias_v1': _L1_xattn_in['bias_v1'], 'L1_xattn_ln2_scale': _L1_xattn_in['ln2_scale'], 'L1_xattn_ln2_offset': _L1_xattn_in['ln2_offset'], 'L1_xattn_wq2': _L1_xattn_in['wq2'], 'L1_xattn_bq2': _L1_xattn_in['bq2'], 'L1_xattn_wk2': _L1_xattn_in['wk2'], 'L1_xattn_bk2': _L1_xattn_in['bk2'], 'L1_xattn_wv2': _L1_xattn_in['wv2'], 'L1_xattn_bv2': _L1_xattn_in['bv2'], 'L1_xattn_wo2': _L1_xattn_in['wo2'], 'L1_xattn_bo2': _L1_xattn_in['bo2'], 'L1_xattn_bias_k2': _L1_xattn_in['bias_k2'], 'L1_xattn_bias_v2': _L1_xattn_in['bias_v2'], 'L1_xattn_ln_mlp_scale': _L1_xattn_in['ln_mlp_scale'], 'L1_xattn_ln_mlp_offset': _L1_xattn_in['ln_mlp_offset'], 'L1_xattn_w_fc1': _L1_xattn_in['w_fc1'], 'L1_xattn_b_fc1': _L1_xattn_in['b_fc1'], 'L1_xattn_w_fc2': _L1_xattn_in['w_fc2'], 'L1_xattn_b_fc2': _L1_xattn_in['b_fc2']}

def reference(x, ctx_2048, L0_xattn_ln1_w, L0_xattn_ln1_b, L0_xattn_ln2_w, L0_xattn_ln2_b, L0_xattn_maa_x, L0_xattn_maa_w1, L0_xattn_maa_w2, L0_xattn_maa_stack, L0_xattn_time_decay, L0_xattn_decay_w1, L0_xattn_decay_w2, L0_xattn_faaaa, L0_xattn_Wr, L0_xattn_Wk, L0_xattn_Wv, L0_xattn_Wg, L0_xattn_Wo, L0_xattn_gn_w, L0_xattn_gn_b, L0_xattn_ffn_maa_k, L0_xattn_ffn_maa_r, L0_xattn_ffn_Wk, L0_xattn_ffn_Wr, L0_xattn_ffn_Wv, L1_xattn_ln1_scale, L1_xattn_ln1_offset, L1_xattn_wq1, L1_xattn_bq1, L1_xattn_wk1, L1_xattn_bk1, L1_xattn_wv1, L1_xattn_bv1, L1_xattn_wo1, L1_xattn_bo1, L1_xattn_bias_k1, L1_xattn_bias_v1, L1_xattn_ln2_scale, L1_xattn_ln2_offset, L1_xattn_wq2, L1_xattn_bq2, L1_xattn_wk2, L1_xattn_bk2, L1_xattn_wv2, L1_xattn_bv2, L1_xattn_wo2, L1_xattn_bo2, L1_xattn_bias_k2, L1_xattn_bias_v2, L1_xattn_ln_mlp_scale, L1_xattn_ln_mlp_offset, L1_xattn_w_fc1, L1_xattn_b_fc1, L1_xattn_w_fc2, L1_xattn_b_fc2):
    import jax
    import jax.numpy as jnp

    def _L0_xattn_ref(x, state, ln1_w, ln1_b, ln2_w, ln2_b, maa_x, maa_w1, maa_w2, maa_stack, time_decay, decay_w1, decay_w2, faaaa, Wr, Wk, Wv, Wg, Wo, gn_w, gn_b, ffn_maa_k, ffn_maa_r, ffn_Wk, ffn_Wr, ffn_Wv, i):
        import jax, jax.numpy as jnp
        import numpy as np
        B, L, E, H = (4, 128, 512, 32)
        S = E // H
        EXTRA_MAA, EXTRA_DECAY = (32, 64)
        EPS = 1e-05

        def _ln(x, w, b):
            m = jnp.mean(x, axis=-1, keepdims=True)
            v = jnp.mean((x - m) ** 2, axis=-1, keepdims=True)
            return (x - m) * jax.lax.rsqrt(v + EPS) * w + b

        def _token_shift(xn, prev_row):
            first = (prev_row - xn[:, 0])[:, None]
            rest = xn[:, :-1] - xn[:, 1:]
            return jnp.concatenate([first, rest], axis=1)
        b, l = (x.shape[0], x.shape[1])
        i0 = (2 + S) * i + 0
        i1 = (2 + S) * i + 1
        xn = _ln(x, ln1_w, ln1_b)
        sx = _token_shift(xn, state[:, i1])
        xxx = jnp.tanh((xn + sx * maa_x) @ maa_w1).reshape(b, l, 5, 1, EXTRA_MAA)
        xxx = jnp.matmul(xxx, maa_w2).reshape(b, l, 5, E)
        x5 = xn[:, :, None] + sx[:, :, None] * (maa_stack + xxx)
        w = jnp.exp(-jnp.exp(time_decay + jnp.tanh(x5[:, :, 1] @ decay_w1) @ decay_w2))
        w = w.reshape(b, l, H, S)
        r = (x5[:, :, 3] @ Wr.T).reshape(b, l, H, S)
        k = (x5[:, :, 0] @ Wk.T).reshape(b, l, H, S)
        v = (x5[:, :, 2] @ Wv.T).reshape(b, l, H, S)
        g = jax.nn.silu(x5[:, :, 4] @ Wg.T)
        s0 = state[:, (2 + S) * i + 2:(2 + S) * (i + 1)].reshape(b, H, S, S)
        u = faaaa[None, :, :, None]

        def step(s, rkvw):
            r_t, k_t, v_t, w_t = rkvw
            a = k_t[:, :, :, None] * v_t[:, :, None, :]
            out = jnp.einsum('bhk,bhkd->bhd', r_t, u * a + s)
            return (a + w_t[:, :, :, None] * s, out)
        xs = tuple((jnp.moveaxis(t, 1, 0) for t in (r, k, v, w)))
        _, outs = jax.lax.scan(step, s0, xs)
        att = jnp.moveaxis(outs, 0, 1).reshape(b, l, E)
        a4 = att.reshape(b, l, H, S)
        m = jnp.mean(a4, axis=-1, keepdims=True)
        var = jnp.mean((a4 - m) ** 2, axis=-1, keepdims=True)
        att = ((a4 - m) * jax.lax.rsqrt(var + EPS)).reshape(b, l, E) * gn_w + gn_b
        x = x + att * g @ Wo.T
        xn2 = _ln(x, ln2_w, ln2_b)
        sx2 = _token_shift(xn2, state[:, i0])
        xk = xn2 + sx2 * ffn_maa_k
        xr = xn2 + sx2 * ffn_maa_r
        rr = jax.nn.sigmoid(xr @ ffn_Wr.T)
        kk = jnp.square(jax.nn.relu(xk @ ffn_Wk.T))
        x = x + rr * (kk @ ffn_Wv.T)
        return x

    def _L1_xattn_ref(x, xf_1, xf_2, ln1_scale, ln1_offset, wq1, bq1, wk1, bk1, wv1, bv1, wo1, bo1, bias_k1, bias_v1, ln2_scale, ln2_offset, wq2, bq2, wk2, bk2, wv2, bv2, wo2, bo2, bias_k2, bias_v2, ln_mlp_scale, ln_mlp_offset, w_fc1, b_fc1, w_fc2, b_fc2):
        import jax, jax.numpy as jnp
        import numpy as np
        B, Q, S1, S2 = (4, 64, 512, 512)
        D, H, K, F = (512, 16, 128, 2048)
        LN_EPS = 1e-05

        def _layer_norm(x, scale, offset):
            mu = jnp.mean(x, axis=-1, keepdims=True)
            var = jnp.var(x, axis=-1, keepdims=True)
            return (x - mu) * jax.lax.rsqrt(var + LN_EPS) * scale + offset

        def _cross_attention(q_in, kv_in, wq, bq, wk, bk, wv, bv, wo, bo, bias_k, bias_v):
            b, q_len, _ = q_in.shape
            t = kv_in.shape[1]
            qh = (q_in @ wq + bq).reshape(b, q_len, H, K)
            kh = (kv_in @ wk + bk).reshape(b, t, H, K)
            vh = (kv_in @ wv + bv).reshape(b, t, H, K)
            kh = jnp.concatenate([kh, jnp.broadcast_to(bias_k, (b, 1, H, K))], axis=1)
            vh = jnp.concatenate([vh, jnp.broadcast_to(bias_v, (b, 1, H, K))], axis=1)
            scale = jnp.sqrt(jnp.asarray(K, q_in.dtype))
            logits = jnp.einsum('bqhk,bthk->bhqt', qh, kh) / scale
            weights = jax.nn.softmax(logits, axis=-1)
            ctx = jnp.einsum('bhqt,bthk->bqhk', weights, vh).reshape(b, q_len, H * K)
            return ctx @ wo + bo

        def _forward(x, xf_1, xf_2, ln1_scale, ln1_offset, wq1, bq1, wk1, bk1, wv1, bv1, wo1, bo1, bias_k1, bias_v1, ln2_scale, ln2_offset, wq2, bq2, wk2, bk2, wv2, bv2, wo2, bo2, bias_k2, bias_v2, ln_mlp_scale, ln_mlp_offset, w_fc1, b_fc1, w_fc2, b_fc2):
            res = x
            h = _layer_norm(x, ln1_scale, ln1_offset)
            x = res + _cross_attention(h, xf_1, wq1, bq1, wk1, bk1, wv1, bv1, wo1, bo1, bias_k1, bias_v1)
            res = x
            h = _layer_norm(x, ln2_scale, ln2_offset)
            x = res + _cross_attention(h, xf_2, wq2, bq2, wk2, bk2, wv2, bv2, wo2, bo2, bias_k2, bias_v2)
            h = _layer_norm(x, ln_mlp_scale, ln_mlp_offset)
            h = jax.nn.gelu(h @ w_fc1 + b_fc1, approximate=False) @ w_fc2 + b_fc2
            return x + h
        return _forward(x, xf_1, xf_2, ln1_scale, ln1_offset, wq1, bq1, wk1, bk1, wv1, bv1, wo1, bo1, bias_k1, bias_v1, ln2_scale, ln2_offset, wq2, bq2, wk2, bk2, wv2, bv2, wo2, bo2, bias_k2, bias_v2, ln_mlp_scale, ln_mlp_offset, w_fc1, b_fc1, w_fc2, b_fc2)
    x = _L0_xattn_ref(x, ctx_2048, L0_xattn_ln1_w, L0_xattn_ln1_b, L0_xattn_ln2_w, L0_xattn_ln2_b, L0_xattn_maa_x, L0_xattn_maa_w1, L0_xattn_maa_w2, L0_xattn_maa_stack, L0_xattn_time_decay, L0_xattn_decay_w1, L0_xattn_decay_w2, L0_xattn_faaaa, L0_xattn_Wr, L0_xattn_Wk, L0_xattn_Wv, L0_xattn_Wg, L0_xattn_Wo, L0_xattn_gn_w, L0_xattn_gn_b, L0_xattn_ffn_maa_k, L0_xattn_ffn_maa_r, L0_xattn_ffn_Wk, L0_xattn_ffn_Wr, L0_xattn_ffn_Wv, 0)
    x = _L1_xattn_ref(x, ctx_2048, ctx_2048, L1_xattn_ln1_scale, L1_xattn_ln1_offset, L1_xattn_wq1, L1_xattn_bq1, L1_xattn_wk1, L1_xattn_bk1, L1_xattn_wv1, L1_xattn_bv1, L1_xattn_wo1, L1_xattn_bo1, L1_xattn_bias_k1, L1_xattn_bias_v1, L1_xattn_ln2_scale, L1_xattn_ln2_offset, L1_xattn_wq2, L1_xattn_bq2, L1_xattn_wk2, L1_xattn_bk2, L1_xattn_wv2, L1_xattn_bv2, L1_xattn_wo2, L1_xattn_bo2, L1_xattn_bias_k2, L1_xattn_bias_v2, L1_xattn_ln_mlp_scale, L1_xattn_ln_mlp_offset, L1_xattn_w_fc1, L1_xattn_b_fc1, L1_xattn_w_fc2, L1_xattn_b_fc2)
    return x

_drawn_inputs = setup_inputs


def setup_inputs(seed=0):
    import zlib

    import numpy as np

    out = dict(_drawn_inputs(seed))
    spreads = {'L0_xattn_ln1_w': (1.0, 0.2),
     'L0_xattn_ln1_b': (0.0, 0.27),
     'L0_xattn_ln2_w': (1.0, 0.6),
     'L0_xattn_ln2_b': (0.0, 0.8),
     'L0_xattn_gn_w': (1.0, 0.6),
     'L0_xattn_gn_b': (0.0, 0.692),
     'L1_xattn_ln1_scale': (1.0, 0.6),
     'L1_xattn_ln1_offset': (0.0, 0.8),
     'L1_xattn_bq1': (0.0, 2.0),
     'L1_xattn_bk1': (0.0, 0.8),
     'L1_xattn_bv1': (0.0, 0.1),
     'L1_xattn_bo1': (0.0, 0.1),
     'L1_xattn_ln2_scale': (1.0, 0.6),
     'L1_xattn_ln2_offset': (0.0, 0.8),
     'L1_xattn_bq2': (0.0, 2.0),
     'L1_xattn_bk2': (0.0, 0.8),
     'L1_xattn_bv2': (0.0, 0.1),
     'L1_xattn_bo2': (0.0, 0.1),
     'L1_xattn_ln_mlp_scale': (1.0, 0.2),
     'L1_xattn_ln_mlp_offset': (0.0, 0.34),
     'L1_xattn_b_fc1': (0.0, 0.1),
     'L1_xattn_b_fc2': (0.0, 0.1)}
    factors = {'L0_xattn_maa_x': 8.0,
     'L0_xattn_maa_w1': 2.94,
     'L0_xattn_maa_w2': 2.962,
     'L0_xattn_maa_stack': 6.472,
     'L0_xattn_decay_w1': 8.0,
     'L0_xattn_decay_w2': 8.0,
     'L0_xattn_faaaa': 3.024,
     'L0_xattn_ffn_maa_k': 8.0,
     'L0_xattn_ffn_maa_r': 8.0,
     'L0_xattn_ffn_Wr': 4.22,
     'L1_xattn_wq1': 8.0,
     'L1_xattn_wk1': 8.0,
     'L1_xattn_wv1': 2.801,
     'L1_xattn_bias_k1': 38.905,
     'L1_xattn_bias_v1': 8.0,
     'L1_xattn_wq2': 8.0,
     'L1_xattn_wk2': 8.0,
     'L1_xattn_wv2': 2.853,
     'L1_xattn_bias_k2': 31.212,
     'L1_xattn_bias_v2': 8.0}
    for name, (base, spread) in spreads.items():
        noise = np.random.default_rng([zlib.crc32(name.encode()), seed]).standard_normal(out[name].shape)
        drawn = base * np.exp(spread * noise) if base else spread * noise
        out[name] = jnp.asarray(drawn.astype(out[name].dtype))
    for name, factor in factors.items():
        out[name] = (out[name] * factor).astype(out[name].dtype)
    return out
```

```python
from contextlib import ExitStack

import numpy as np
import concourse.bass as bass
from concourse import mybir

ALU = mybir.AluOpType
ACT = mybir.ActivationFunctionType
AX = mybir.AxisListType.X
F32 = mybir.dt.float32
FR = mybir.dt.float32r

P = 128
B, L, E = 16, 128, 512
EC = E // P
NQ = B // 4
QT = 4 * L
HS = 16
EPS = 1e-5
NH, KD = 16, 128
F = 2048
SCALE = float(KD) ** -0.5
LORA = 32

VEC_NAMES = ["ln1_w", "ln1_b", "ln2_w", "ln2_b", "maa_x", "stack0", "stack1", "stack2", "stack3", "stack4",
             "time_decay", "faaaa", "gn_w", "gn_b", "ffn_maa_k", "ffn_maa_r",
             "s1", "o1", "s2", "o2", "s3", "o3"]
VEC = {n: i * EC for i, n in enumerate(VEC_NAMES)}
NV = len(VEC_NAMES) * EC


class Steps:

    def __init__(self, engine, sem, base=0):
        self.engine, self.sem, self.base, self.n = engine, sem, base, 0

    def link(self, instruction):
        self.n += 1
        instruction.then_inc(self.sem, 1)
        self.engine.wait_ge(self.sem, self.base + self.n)


def mm3(pe, out, lhs, rhs, first, last):
    pe.matmul(out, lhs[0], rhs[0], start=first, stop=False)
    pe.matmul(out, lhs[0], rhs[1], start=False, stop=False)
    return pe.matmul(out, lhs[1], rhs[0], start=False, stop=last)


def layernorm_dve(v, x4, xn4, stats, mv, std, rstd, bn_done, stats_ready, std_ready, xn0_ready, n, link):
    for b in range(4):
        v.bn_stats(stats[:, b, :], x4[:, b, :]).then_inc(bn_done, 1)
    v.wait_ge(bn_done, 4 * n + 4)
    v.memset(rstd[:, :], 1.0)
    for b in range(4):
        ins = v.bn_aggr(mv[:, b, :], stats[:, b, :])
    ins.then_inc(stats_ready, 1)
    v.wait_ge(std_ready, n + 1)
    link(v.reciprocal(rstd[:, :], std[:, :]))
    for b in range(4):
        v.tensor_scalar(xn4[:, b, :], x4[:, b, :], mv[:, b, 0:1], rstd[:, b:b + 1], ALU.subtract,
                        ALU.mult).then_inc(xn0_ready, 1)


def time_mix(nc, io, x2):
    J = 6
    MIX = [None, 1, 3, 0, 2, 4]
    PJ_USES = 2 + 1 + 4 + 16
    MX_USES = 20 + 4 + 4
    with ExitStack() as ctx:
        def sb(n, s, d=F32):
            return ctx.enter_context(nc.sbuf_tensor("tm_" + n, s, d))

        def ps(n, s):
            return ctx.enter_context(nc.psum_tensor("tm_" + n, s, F32))

        def sem(n):
            return ctx.enter_context(nc.semaphore("tm_" + n))

        vec = sb("vec", [P, NV])
        ident = sb("ident", [P, P])
        head_sum = sb("head_sum", [P, P])
        head_mean = sb("head_mean", [P, P])
        pick_k = sb("pick_k", [P, P + HS - 1])
        spread_v = sb("spread_v", [P, HS, P], FR)
        prev = sb("prev", [P, EC, B])
        s0 = sb("s0", [P, EC, HS, B])
        eps = sb("eps", [P, 1])
        w_hi = sb("w_hi", [P, 5, EC, E], FR)
        w_lo = sb("w_lo", [P, 5, EC, E], FR)
        lora1 = (sb("lora1_hi", [P, EC, 160], FR), sb("lora1_lo", [P, EC, 160], FR))
        dec1 = (sb("dec1_hi", [P, EC, 64], FR), sb("dec1_lo", [P, EC, 64], FR))
        lora2 = sb("lora2", [P, E])
        lora2e = sb("lora2e", [LORA, E])
        dec2 = sb("dec2", [64, E])
        xq = sb("xq", [P, 4, E])
        stats = sb("stats", [P, 4, 6])
        mv = sb("mv", [P, 4, 2])
        std = sb("std", [P, 4])
        rstd = sb("rstd", [P, 4])
        xn = sb("xn", [P, EC, 4, L + 1])
        sx = sb("sx", [P, EC, QT])
        xf = sb("xf", [P, EC, QT])
        x_hi = sb("x_hi", [P, EC, QT], FR)
        x_lo = sb("x_lo", [P, EC, QT], FR)
        h5 = sb("h5", [P, QT])
        h5e = sb("h5e", [LORA, QT])
        dh = sb("dh", [64, QT])
        ew = sb("ew", [P, QT])
        wd = sb("wd", [P, EC, 4, L])
        rr = sb("rr", [P, EC, QT])
        kk = sb("kk", [P, EC, 4, L + 1])
        vv = sb("vv", [P, EC, 4, L + 1])
        gg = sb("gg", [P, EC, QT])
        pj = [ps("pj0", [P, QT]), ps("pj1", [P, QT])]
        mx = [ps("mx0", [P, QT]), ps("mx1", [P, QT])]
        vb = ps("vb", [P, 4, QT])

        const_in, small_in, w_in, w_hi_ready, w_ready = sem("const_in"), sem("small_in"), [sem("w_in0"), sem("w_in1")], sem("w_hi_ready"), sem("w_ready")
        x_in, x2_out, quad_done = sem("x_in"), sem("x2_out"), sem("quad_done")
        bn_done = sem("bn_done")
        stats_ready, std_ready, xn0_ready = sem("stats_ready"), sem("std_ready"), sem("xn0_ready")
        xnT_full, xn_ready, prev_ready = sem("xnT_full"), sem("xn_ready"), sem("prev_ready")
        xf_ready, hi_ready, split_ready = sem("xf_ready"), sem("hi_ready"), sem("split_ready")
        pj_full, pj_free, mx_full, mx_free = sem("pj_full"), sem("pj_free"), sem("mx_full"), sem("mx_free")
        h5_ready, dh_ready, ew_ready = sem("h5_ready"), sem("dh_ready"), sem("ew_ready")
        proj_used = sem("proj_used")
        dve_step, v_hi_ready, v_split_ready = sem("dve_step"), sem("v_hi_ready"), sem("v_split_ready")
        ruk_ready = sem("ruk_ready")
        vb_full, scanned, rs_ready, rs_used = sem("vb_full"), sem("scanned"), sem("rs_ready"), sem("rs_used")
        mean_full, cent_ready = sem("mean_full"), sem("cent_ready")
        sq_ready, var_full, gstd_ready = sem("sq_ready"), sem("var_full"), sem("gstd_ready")
        y_ready, y_hi_ready, y_split_ready, wo_full = sem("y_ready"), sem("y_hi_ready"), sem("y_split_ready"), sem("wo_full")
        ready = sem("ready")

        state = xn[:, :, :, :].rearrange("p a b c -> p (a b c)")[:, 0:4 * QT].rearrange("p (a b) -> p a b", a=4)
        prod = [sx, xf]
        DVE_STEPS = 1 + 4 + 16 + 1 + 8 + 3
        block = ctx.enter_context(nc.Block())

        @block.sync
        def _(sp):
            for tile, name in ((vec, "vec"), (ident, "ident"), (head_sum, "head_sum"), (head_mean, "head_mean"),
                               (pick_k, "pick_k"), (s0, "s0"), (prev, "prev1"), (dec2, "dec2")):
                sp.dma_start(tile[:], io[name]).then_inc(const_in, 16)
            sp.dma_start(lora2[:], io["lora2"][0:P, :]).then_inc(const_in, 16)
            sp.dma_start(lora2e[:], io["lora2"][P:160, :]).then_inc(const_in, 16)
            sp.dma_start(xf[:].rearrange("p a b -> p (a b)"), io["spread_v"]).then_inc(small_in, 16)
            sp.dma_start(sx[:, 0:2, :].rearrange("p a b -> p (a b)")[:, 0:640].rearrange("p (c m) -> p c m", c=EC), io["lora1"]).then_inc(small_in, 16)
            sp.dma_start(sx[:, 2, 0:256].rearrange("p (c m) -> p c m", c=EC), io["dec1"]).then_inc(small_in, 16)
            for j in range(5):
                if j >= 2:
                    sp.wait_ge(w_ready, 2 + j - 1)
                sp.dma_start((rr if j % 2 == 0 else gg)[:], io["l0w"][j]).then_inc(w_in[j % 2], 16)
            with sp.Fori(0, NQ) as q:
                sp.wait_ge(quad_done, q + 1)
                sp.wait_ge(x2_out, q * 16 + 16)
                sp.dma_start(xq[:], io["x"][bass.ds(q * 4, 4)].rearrange("b t e -> t b e")).then_inc(x_in, 16)
                sp.wait_ge(quad_done, q + 2)
                sp.dma_start(x2[bass.ds(q * 4, 4)].rearrange("b t e -> t b e"), xq[:]).then_inc(x2_out, 16)
            sp.wait_ge(x2_out, NQ * 16 + 16)

        @block.gpsimd
        def _(gp):
            gp.memset(eps[:], EPS).then_inc(ready, 1)
            gp.memset(wd[:], 0.0).then_inc(ready, 1)
            gp.memset(kk[:, :, :, 0:1], 1.0).then_inc(ready, 1)
            gp.memset(vv[:, :, :, 0:1], 0.0).then_inc(ready, 1)
            gp.memset(h5e[0:1, 0:1], 0.0).then_inc(x2_out, 16)

        @block.scalar
        def _(act):
            act.wait_ge(small_in, 48)
            act.activation(spread_v[:].rearrange("p a b -> p (a b)"), xf[:].rearrange("p a b -> p (a b)"), ACT.Copy).then_inc(w_hi_ready, 1)
            act.activation(lora1[0][:], sx[:, 0:2, :].rearrange("p a b -> p (a b)")[:, 0:640].rearrange("p (c m) -> p c m", c=EC), ACT.Copy).then_inc(w_hi_ready, 1)
            act.activation(dec1[0][:], sx[:, 2, 0:256].rearrange("p (c m) -> p c m", c=EC), ACT.Copy).then_inc(w_hi_ready, 1)
            for j in range(5):
                act.wait_ge(w_in[j % 2], 16 * (j // 2 + 1))
                act.activation(w_hi[:, j], (rr if j % 2 == 0 else gg)[:], ACT.Copy).then_inc(w_hi_ready, 1)
            act.wait_ge(ready, 4)
            act.wait_ge(const_in, 160)
            act.wait_ge(w_ready, 7)
            with act.Fori(0, NQ) as q:
                pj_used = 0

                def pj_wait():
                    act.wait_ge(pj_full, q * PJ_USES + pj_used + 1)

                act.wait_ge(stats_ready, q + 1)
                act.activation(std[:, :], mv[:, :, 1], ACT.Sqrt, bias=eps[:]).then_inc(std_ready, 1)
                act.wait_ge(xnT_full, q + 1)
                for c in range(EC):
                    act.activation(xn[:, c, :, 1:L + 1], vb[:, c, :].rearrange("p (b t) -> p b t", b=4), ACT.Identity,
                                   bias=vec[:, VEC["ln1_b"] + c:VEC["ln1_b"] + c + 1],
                                   scale=vec[:, VEC["ln1_w"] + c:VEC["ln1_w"] + c + 1]).then_inc(xn_ready, 1)
                for j in range(J):
                    for c in range(EC):
                        act.wait_ge(xf_ready, q * 4 * J + 4 * j + c + 1)
                        if j > 0 and c == 0:
                            act.wait_ge(proj_used, q * J + j)
                        act.activation(x_hi[:, c, :], xf[:, c, :], ACT.Copy).then_inc(hi_ready, 1)
                    if j == 0:
                        pj_wait()
                        act.activation(h5[:], pj[0][:], ACT.Tanh).then_inc(pj_free, 1)
                        pj_used += 1
                        pj_wait()
                        act.activation(h5e[:], pj[1][0:LORA, :], ACT.Tanh).then_inc(pj_free, 1)
                        pj_used += 1
                        continue
                    if j == 1:
                        pj_wait()
                        act.activation(dh[:], pj[pj_used % 2][0:64, :], ACT.Tanh).then_inc(pj_free, 1)
                        pj_used += 1
                    for f in range(EC):
                        pj_wait()
                        src = pj[pj_used % 2][:]
                        src3 = src.rearrange("p (b t) -> p b t", b=4)
                        if j == 1 and f > 0:
                            act.wait_ge(ew_ready, q * 4 + f)
                        if j == 1:
                            act.activation(ew[:], src, ACT.Exp, bias=vec[:, VEC["time_decay"] + f:VEC["time_decay"] + f + 1]).then_inc(pj_free, 1)
                            act.wait_ge(pj_free, q * PJ_USES + pj_used + 1)
                            act.activation(wd[:, f, :, 1:L], ew[:].rearrange("p (b t) -> p b t", b=4)[:, :, 0:L - 1],
                                           ACT.Exp, scale=-1.0).then_inc(ew_ready, 1)
                        elif j == 2:
                            act.activation(rr[:, f, :], src, ACT.Copy).then_inc(pj_free, 1)
                        elif j == 3:
                            act.activation(kk[:, f, :, 1:L + 1], src3, ACT.Copy).then_inc(pj_free, 1)
                        elif j == 4:
                            act.activation(vv[:, f, :, 1:L + 1], src3, ACT.Copy).then_inc(pj_free, 1)
                        else:
                            act.activation(gg[:, f, :], src, ACT.Silu).then_inc(pj_free, 1)
                        pj_used += 1
                assert pj_used == PJ_USES
                act.wait_ge(pj_free, q * PJ_USES + PJ_USES)
                for c in range(EC):
                    act.activation(x_hi[:, c, :].rearrange("p (b t) -> p b t", b=4), vv[:, c, :, 0:L], ACT.Copy).then_inc(v_hi_ready, 1)
                act.wait_ge(cent_ready, q + 1)
                act.activation(xf[:].rearrange("p c (b t) -> p (c b) t", b=4), vv[:, :, :, 1:L + 1].rearrange("p c b t -> p (c b) t"), ACT.Square).then_inc(sq_ready, 1)
                act.wait_ge(var_full, q + 1)
                act.activation(sx[:].rearrange("p a b -> p (a b)"), vb[:].rearrange("p a b -> p (a b)"), ACT.Sqrt, bias=eps[:]).then_inc(gstd_ready, 1)
                for c in range(EC):
                    act.wait_ge(y_ready, q * 4 + c + 1)
                    act.activation(x_hi[:, c, :], xf[:, c, :], ACT.Copy).then_inc(y_hi_ready, 1)

        @block.vector
        def _(v):
            v.memset(std[:], 1.0).then_inc(quad_done, 1)
            v.wait_ge(w_hi_ready, 3)
            v.tensor_tensor(lora1[1][:], sx[:, 0:2, :].rearrange("p a b -> p (a b)")[:, 0:640].rearrange("p (c m) -> p c m", c=EC), lora1[0][:], ALU.subtract).then_inc(w_ready, 1)
            v.tensor_tensor(dec1[1][:], sx[:, 2, 0:256].rearrange("p (c m) -> p c m", c=EC), dec1[0][:], ALU.subtract).then_inc(w_ready, 1)
            for j in range(5):
                v.wait_ge(w_hi_ready, 3 + j + 1)
                v.tensor_tensor(w_lo[:, j], (rr if j % 2 == 0 else gg)[:], w_hi[:, j], ALU.subtract).then_inc(w_ready, 1)
            v.wait_ge(ready, 4)
            v.wait_ge(const_in, 160)
            with v.Fori(0, NQ) as q:
                steps = Steps(v, dve_step, q * DVE_STEPS)
                link = steps.link
                v.wait_ge(x_in, q * 16 + 16)
                layernorm_dve(v, xq, xf, stats, mv, std, rstd, bn_done, stats_ready, std_ready, xn0_ready, q, link)
                v.tensor_copy(xn[:, :, :, 0], prev[:, :, bass.ds(q * 4, 4)]).then_inc(prev_ready, 1)
                v.wait_ge(prev_ready, q + 1)
                for c in range(EC):
                    v.wait_ge(xn_ready, q * 4 + c + 1)
                    link(v.tensor_tensor(sx[:, c, :].rearrange("p (b t) -> p b t", b=4), xn[:, c, :, 0:L],
                                         xn[:, c, :, 1:L + 1], ALU.subtract))
                mx_used = 0
                for j in range(J):
                    for c in range(EC):
                        xc = xf[:, c, :].rearrange("p (b t) -> p b t", b=4)
                        sc = sx[:, c, :].rearrange("p (b t) -> p b t", b=4)
                        if j == 0:
                            if c == 0:
                                v.wait_ge(xnT_full, q + 1)
                            v.scalar_tensor_tensor(out=xc, in0=sc, scalar=vec[:, VEC["maa_x"] + c:VEC["maa_x"] + c + 1],
                                                   in1=xn[:, c, :, 1:L + 1], op0=ALU.mult, op1=ALU.add).then_inc(xf_ready, 1)
                        else:
                            s = VEC["stack%d" % MIX[j]] + c
                            v.wait_ge(split_ready, q * 4 * J + 4 * (j - 1) + c + 1)
                            v.wait_ge(mx_full, q * MX_USES + mx_used + 1)
                            v.scalar_tensor_tensor(out=xf[:, c, :], in0=mx[mx_used % 2][:], scalar=vec[:, s:s + 1],
                                                   in1=sx[:, c, :], op0=ALU.add, op1=ALU.mult).then_inc(mx_free, 1)
                            mx_used += 1
                            v.wait_ge(mx_free, q * MX_USES + mx_used)
                            v.tensor_tensor(xc, xc, xn[:, c, :, 1:L + 1], ALU.add).then_inc(xf_ready, 1)
                    for c in range(EC):
                        v.wait_ge(hi_ready, q * 4 * J + 4 * j + c + 1)
                        v.tensor_tensor(x_lo[:, c, :], xf[:, c, :], x_hi[:, c, :], ALU.subtract).then_inc(split_ready, 1)
                for c in range(EC):
                    v.wait_ge(v_hi_ready, q * 4 + c + 1)
                    v.tensor_tensor(x_lo[:, c, :].rearrange("p (b t) -> p b t", b=4), vv[:, c, :, 0:L],
                                    x_hi[:, c, :].rearrange("p (b t) -> p b t", b=4), ALU.subtract).then_inc(v_split_ready, 1)
                v.wait_ge(v_split_ready, q * 4 + 4)
                for c in range(EC):
                    u = VEC["faaaa"] + c
                    v.scalar_tensor_tensor(out=sx[:, c, :].rearrange("p (b t) -> p b t", b=4),
                                           in0=rr[:, c, :].rearrange("p (b t) -> p b t", b=4), scalar=vec[:, u:u + 1],
                                           in1=kk[:, c, :, 1:L + 1], op0=ALU.mult, op1=ALU.mult).then_inc(ruk_ready, 1)
                for c in range(EC):
                    v.wait_ge(mx_full, q * MX_USES + mx_used + 1)
                    v.tensor_tensor(vv[:, c, :, 1:L + 1], mx[mx_used % 2][:].rearrange("p (b t) -> p b t", b=4),
                                    vv[:, c, :, 1:L + 1], ALU.mult).then_inc(mx_free, 1)
                    mx_used += 1
                v.wait_ge(mx_free, q * MX_USES + mx_used)

                def add_bonus(g):
                    v.wait_ge(mx_full, q * MX_USES + 24 + g + 1)
                    v.tensor_tensor(vv[:, g, :, 1:L + 1], mx[g % 2][:].rearrange("p (b t) -> p b t", b=4),
                                    vv[:, g, :, 1:L + 1], ALU.add).then_inc(mx_free, 1)

                for i in range(16):
                    g = i // 4
                    v.wait_ge(vb_full, q * 16 + i + 1)
                    link(v.tensor_tensor(vb[:].rearrange("p d (b t) -> p d b t", b=4), vb[:].rearrange("p d (b t) -> p d b t", b=4),
                                         kk[:, g:g + 1, :, 0:L].broadcast_to([P, 4, 4, L]), ALU.mult))
                    for d in range(4):
                        ins = v.tensor_tensor_scan(state[:, d, :], wd[:, g].rearrange("p b t -> p (b t)"), vb[:, d, :], 0.0,
                                                   ALU.mult, ALU.add)
                        ins.then_inc(scanned, 1)
                    v.wait_ge(scanned, q * 64 + i * 4 + 4)
                    if i >= 2:
                        v.wait_ge(rs_used, q * 16 + i - 1)
                    else:
                        v.wait_ge(mx_full, q * MX_USES + 24)
                    v.tensor_tensor(prod[i % 2][:], state, rr[:, g:g + 1, :].broadcast_to([P, 4, QT]), ALU.mult).then_inc(rs_ready, 1)
                    v.wait_ge(rs_ready, q * 16 + i + 1)
                    if i % 4 == 1 and i > 4:
                        add_bonus(g - 1)
                add_bonus(3)
                v.wait_ge(mean_full, q + 1)
                v.tensor_tensor(vv[:, :, :, 1:L + 1].rearrange("p c b t -> p (c b) t"), vv[:, :, :, 1:L + 1].rearrange("p c b t -> p (c b) t"),
                                vb[:].rearrange("p c (b t) -> p (c b) t", b=4), ALU.subtract).then_inc(cent_ready, 1)
                v.wait_ge(gstd_ready, q + 1)
                link(v.reciprocal(sx[:], sx[:]))
                v.wait_ge(var_full, q + 1)
                for c in range(EC):
                    link(v.tensor_tensor(xf[:, c, :].rearrange("p (b t) -> p b t", b=4), vv[:, c, :, 1:L + 1],
                                         sx[:, c, :].rearrange("p (b t) -> p b t", b=4), ALU.mult))
                    w, b_ = VEC["gn_w"] + c, VEC["gn_b"] + c
                    link(v.tensor_scalar(xf[:, c, :], xf[:, c, :], vec[:, w:w + 1], vec[:, b_:b_ + 1], ALU.mult, ALU.add))
                    v.tensor_tensor(xf[:, c, :], xf[:, c, :], gg[:, c, :], ALU.mult).then_inc(y_ready, 1)
                for c in range(EC):
                    v.wait_ge(y_hi_ready, q * 4 + c + 1)
                    v.tensor_tensor(x_lo[:, c, :], xf[:, c, :], x_hi[:, c, :], ALU.subtract).then_inc(y_split_ready, 1)
                for b in range(4):
                    v.wait_ge(wo_full, q * 4 + b + 1)
                    ins = v.tensor_tensor(xq[:, b, :], xq[:, b, :], vb[:, b, :], ALU.add)
                    if b < 3:
                        link(ins)
                ins.then_inc(quad_done, 1)
                assert steps.n == DVE_STEPS

        @block.tensor
        def _(pe):
            pe.wait_ge(const_in, 160)
            pe.wait_ge(w_ready, 7)
            with pe.Fori(0, NQ) as q:
                pj_used = 0
                mx_used = 0

                def mix(j):
                    nonlocal mx_used
                    m = MIX[j]
                    for c in range(EC):
                        if mx_used >= 2:
                            pe.wait_ge(mx_free, q * MX_USES + mx_used - 1)
                        if m < 4:
                            lhs, rhs = lora2[32 * m:32 * m + 32, c * P:(c + 1) * P], h5[32 * m:32 * m + 32, :]
                        else:
                            lhs, rhs = lora2e[:, c * P:(c + 1) * P], h5e[:]
                        pe.matmul(mx[mx_used % 2][:], lhs, rhs, start=True, stop=True).then_inc(mx_full, 1)
                        mx_used += 1

                def project(j, w, m, rows):
                    nonlocal pj_used
                    if pj_used >= 2:
                        pe.wait_ge(pj_free, q * PJ_USES + pj_used - 1)
                    for c in range(EC):
                        pe.wait_ge(split_ready, q * 4 * J + 4 * j + c + 1)
                        ins = mm3(pe, pj[pj_used % 2][0:rows, :], (w[0][:, c, m:m + rows], w[1][:, c, m:m + rows]),
                                  (x_hi[:, c, :], x_lo[:, c, :]), c == 0, c == EC - 1)
                    ins.then_inc(pj_full, 1)
                    pj_used += 1

                for b in range(4):
                    pe.wait_ge(xn0_ready, q * 4 + b + 1)
                    for c in range(EC):
                        ins = pe.transpose(vb[:, c, b * P:(b + 1) * P], xf[:, b, c * P:(c + 1) * P], ident[:])
                ins.then_inc(xnT_full, 1)
                project(0, lora1, 0, P)
                project(0, lora1, P, LORA)
                pe.nop().then_inc(proj_used, 1)
                pe.wait_ge(pj_free, q * PJ_USES + 2)
                mix(1)
                for j in range(1, J):
                    if j + 1 < J:
                        mix(j + 1)
                    if j == 1:
                        project(1, dec1, 0, 64)
                        pe.nop().then_inc(proj_used, 1)
                        pe.wait_ge(pj_free, q * PJ_USES + pj_used)
                        for f in range(EC):
                            pe.wait_ge(pj_free, q * PJ_USES + pj_used - 1)
                            pe.matmul(pj[pj_used % 2][:], dec2[:, f * P:(f + 1) * P], dh[:], start=True, stop=True).then_inc(pj_full, 1)
                            pj_used += 1
                    else:
                        for f in range(EC):
                            project(j, (w_hi[:, j - 2], w_lo[:, j - 2]), f * P, P)
                        pe.nop().then_inc(proj_used, 1)
                for c in range(EC):
                    pe.wait_ge(ruk_ready, q * 4 + c + 1)
                    pe.wait_ge(mx_free, q * MX_USES + mx_used - 1)
                    pe.matmul(mx[mx_used % 2][:], head_sum[:], sx[:, c, :], start=True, stop=True).then_inc(mx_full, 1)
                    mx_used += 1

                def spread(i):
                    g = i // 4
                    if i > 0:
                        pe.wait_ge(scanned, q * 64 + 4 * i)
                    for e in range(4):
                        d = (i % 4) * 4 + e
                        pe.matmul(vb[:, e, :], spread_v[:, d, :], x_hi[:, g, :], start=True, stop=False)
                        pe.matmul(vb[:, e, :], spread_v[:, d, :], x_lo[:, g, :], start=False, stop=False)
                        ins = pe.matmul(vb[:, e, 0:QT:L], ident[:], s0[:, g, d, bass.ds(q * 4, 4)], start=False, stop=True)
                    ins.then_inc(vb_full, 1)

                pe.wait_ge(v_split_ready, q * 4 + 4)
                spread(0)
                for i in range(16):
                    if i + 1 < 16:
                        spread(i + 1)
                    g = i // 4
                    if i % 4 == 0:
                        pe.wait_ge(mx_free, q * MX_USES + 24 + g - 1)
                    pe.wait_ge(rs_ready, q * 16 + i + 1)
                    for e in range(4):
                        d = (i % 4) * 4 + e
                        ins = pe.matmul(mx[g % 2][:], pick_k[:, HS - 1 - d:HS - 1 - d + P], prod[i % 2][:, e, :], start=d == 0, stop=d == 15)
                    if i % 4 == 3:
                        ins.then_inc(mx_full, 1)
                        pe.nop().then_inc(rs_used, 1)
                    else:
                        ins.then_inc(rs_used, 1)
                pe.wait_ge(mx_free, q * MX_USES + MX_USES)
                for c in range(EC):
                    ins = pe.matmul(vb[:, c, :], head_mean[:], vv[:, c, :, 1:L + 1], start=True, stop=True)
                ins.then_inc(mean_full, 1)
                pe.wait_ge(sq_ready, q + 1)
                for c in range(EC):
                    ins = pe.matmul(vb[:, c, :], head_mean[:], xf[:, c, :], start=True, stop=True)
                ins.then_inc(var_full, 1)
                pe.wait_ge(gstd_ready, q + 1)
                for b in range(4):
                    for c in range(EC):
                        pe.wait_ge(y_split_ready, q * 4 + c + 1)
                        ins = mm3(pe, vb[:, b, :], (x_hi[:, c, b * P:(b + 1) * P], x_lo[:, c, b * P:(b + 1) * P]),
                                  (w_hi[:, 4, c, :], w_lo[:, 4, c, :]), c == 0, c == EC - 1)
                    ins.then_inc(wo_full, 1)


def channel_mix(nc, io, x2, x3):
    with ExitStack() as ctx:
        def sb(n, s, d=F32):
            return ctx.enter_context(nc.sbuf_tensor("cm_" + n, s, d))

        def ps(n, s):
            return ctx.enter_context(nc.psum_tensor("cm_" + n, s, F32))

        def sem(n):
            return ctx.enter_context(nc.semaphore("cm_" + n))

        vec = sb("vec", [P, NV])
        ident = sb("ident", [P, P])
        prev = sb("prev", [P, EC, B])
        eps = sb("eps", [P, 1])
        w_hi = sb("w_hi", [P, 3, EC, E], FR)
        w_lo = sb("w_lo", [P, 3, EC, E], FR)
        xq = sb("xq", [P, 4, E])
        stats = sb("stats", [P, 4, 6])
        mv = sb("mv", [P, 4, 2])
        std = sb("std", [P, 4])
        rstd = sb("rstd", [P, 4])
        xn = sb("xn", [P, EC, 4, L + 1])
        sx = sb("sx", [P, EC, QT])
        xf = [sb("xk", [P, EC, QT]), sb("xr", [P, EC, QT])]
        x_hi = [sb("xk_hi", [P, EC, QT], FR), sb("xr_hi", [P, EC, QT], FR)]
        x_lo = [sb("xk_lo", [P, EC, QT], FR), sb("xr_lo", [P, EC, QT], FR)]
        gate = sb("gate", [P, 4, E])
        tr = ps("tr", [P, 4, QT])
        mm = ps("mm", [P, 4, QT])

        const_in, w_in, w_hi_ready, w_ready = sem("const_in"), [sem("w_in%d" % j) for j in range(3)], sem("w_hi_ready"), sem("w_ready")
        x_in, x3_out, quad_done, ready = sem("x_in"), sem("x3_out"), sem("quad_done"), sem("ready")
        bn_done, stats_ready, std_ready, xn0_ready = sem("bn_done"), sem("stats_ready"), sem("std_ready"), sem("xn0_ready")
        xnT_full, xn_ready, prev_ready = sem("xnT_full"), sem("xn_ready"), sem("prev_ready")
        xf_ready, hi_ready, split_ready = sem("xf_ready"), sem("hi_ready"), sem("split_ready")
        k_full, r_full, y_full = sem("k_full"), sem("r_full"), sem("y_full")
        k2_ready, k2_hi_ready, k2_split_ready = sem("k2_ready"), sem("k2_hi_ready"), sem("k2_split_ready")
        gate_ready, gated, dve_step = sem("gate_ready"), sem("gated"), sem("dve_step")
        DVE_STEPS = 1 + 4 + 4 + 3
        block = ctx.enter_context(nc.Block())

        @block.sync
        def _(sp):
            raw = [gate, xf[0], xf[1]]
            for tile, name in ((vec, "vec"), (ident, "ident"), (prev, "prev0")):
                sp.dma_start(tile[:], io[name]).then_inc(const_in, 16)
            for j in range(3):
                sp.dma_start(raw[j][:], io["l0w"][5 + j]).then_inc(w_in[j], 16)
            with sp.Fori(0, NQ) as q:
                sp.wait_ge(quad_done, q + 1)
                sp.wait_ge(x3_out, q * 16 + 16)
                sp.dma_start(xq[:], x2[bass.ds(q * 4, 4)].rearrange("b t e -> t b e")).then_inc(x_in, 16)
                sp.wait_ge(quad_done, q + 2)
                sp.dma_start(x3[bass.ds(q * 4, 4)].rearrange("b t e -> t b e"), xq[:]).then_inc(x3_out, 16)
            sp.wait_ge(x3_out, NQ * 16 + 16)

        @block.gpsimd
        def _(gp):
            gp.memset(eps[:], EPS).then_inc(ready, 1)
            gp.memset(sx[0:1, 0, 0:1], 0.0).then_inc(x3_out, 16)

        @block.scalar
        def _(act):
            raw = [gate, xf[0], xf[1]]
            for j in range(3):
                act.wait_ge(w_in[j], 16)
                act.activation(w_hi[:, j], raw[j][:], ACT.Copy).then_inc(w_hi_ready, 1)
            act.wait_ge(const_in, 48)
            act.wait_ge(ready, 1)
            act.wait_ge(w_ready, 3)
            with act.Fori(0, NQ) as q:
                act.wait_ge(stats_ready, q + 1)
                act.activation(std[:, :], mv[:, :, 1], ACT.Sqrt, bias=eps[:]).then_inc(std_ready, 1)
                act.wait_ge(xnT_full, q + 1)
                for c in range(EC):
                    act.activation(xn[:, c, :, 1:L + 1], tr[:, c, :].rearrange("p (b t) -> p b t", b=4), ACT.Identity,
                                   bias=vec[:, VEC["ln2_b"] + c:VEC["ln2_b"] + c + 1],
                                   scale=vec[:, VEC["ln2_w"] + c:VEC["ln2_w"] + c + 1]).then_inc(xn_ready, 1)
                for j in range(2):
                    for c in range(EC):
                        act.wait_ge(xf_ready, q * 8 + 4 * j + c + 1)
                        act.activation(x_hi[j][:, c, :], xf[j][:, c, :], ACT.Copy).then_inc(hi_ready, 1)
                for c in range(EC):
                    act.wait_ge(k2_ready, q * 4 + c + 1)
                    act.activation(x_hi[0][:, c, :], xf[0][:, c, :], ACT.Copy).then_inc(k2_hi_ready, 1)
                for b in range(4):
                    act.wait_ge(r_full, q * 4 + b + 1)
                    act.activation(gate[:, b, :], tr[:, b, :], ACT.Sigmoid).then_inc(gate_ready, 1)

        @block.vector
        def _(v):
            raw = [gate, xf[0], xf[1]]
            v.memset(std[:], 1.0).then_inc(quad_done, 1)
            for j in range(3):
                v.wait_ge(w_hi_ready, j + 1)
                v.tensor_tensor(w_lo[:, j], raw[j][:], w_hi[:, j], ALU.subtract).then_inc(w_ready, 1)
            v.wait_ge(const_in, 48)
            v.wait_ge(w_ready, 3)
            with v.Fori(0, NQ) as q:
                steps = Steps(v, dve_step, q * DVE_STEPS)
                link = steps.link
                v.wait_ge(x_in, q * 16 + 16)
                layernorm_dve(v, xq, xf[0], stats, mv, std, rstd, bn_done, stats_ready, std_ready, xn0_ready, q, link)
                v.tensor_copy(xn[:, :, :, 0], prev[:, :, bass.ds(q * 4, 4)]).then_inc(prev_ready, 1)
                v.wait_ge(prev_ready, q + 1)
                for c in range(EC):
                    v.wait_ge(xn_ready, q * 4 + c + 1)
                    link(v.tensor_tensor(sx[:, c, :].rearrange("p (b t) -> p b t", b=4), xn[:, c, :, 0:L],
                                         xn[:, c, :, 1:L + 1], ALU.subtract))
                for j, name in ((0, "ffn_maa_k"), (1, "ffn_maa_r")):
                    for c in range(EC):
                        if j == 0 and c == 0:
                            v.wait_ge(xnT_full, q + 1)
                        m = VEC[name] + c
                        v.scalar_tensor_tensor(out=xf[j][:, c, :].rearrange("p (b t) -> p b t", b=4),
                                               in0=sx[:, c, :].rearrange("p (b t) -> p b t", b=4), scalar=vec[:, m:m + 1],
                                               in1=xn[:, c, :, 1:L + 1], op0=ALU.mult, op1=ALU.add).then_inc(xf_ready, 1)
                    for c in range(EC):
                        v.wait_ge(hi_ready, q * 8 + 4 * j + c + 1)
                        v.tensor_tensor(x_lo[j][:, c, :], xf[j][:, c, :], x_hi[j][:, c, :], ALU.subtract).then_inc(split_ready, 1)
                v.wait_ge(k_full, q * 4 + 4)
                for c in range(EC):
                    link(v.tensor_copy(sx[:, c, :], mm[:, c, :]))
                    v.scalar_tensor_tensor(out=xf[0][:, c, :], in0=mm[:, c, :], scalar=0.0, in1=sx[:, c, :],
                                           op0=ALU.max, op1=ALU.mult).then_inc(k2_ready, 1)
                for c in range(EC):
                    v.wait_ge(k2_hi_ready, q * 4 + c + 1)
                    v.tensor_tensor(x_lo[0][:, c, :], xf[0][:, c, :], x_hi[0][:, c, :], ALU.subtract).then_inc(k2_split_ready, 1)
                for b in range(4):
                    v.wait_ge(gate_ready, q * 4 + b + 1)
                    v.wait_ge(y_full, q * 4 + b + 1)
                    v.tensor_tensor(sx[:, b, :], gate[:, b, :], mm[:, b, :], ALU.mult).then_inc(gated, 1)
                    v.wait_ge(gated, q * 4 + b + 1)
                    ins = v.tensor_tensor(xq[:, b, :], xq[:, b, :], sx[:, b, :], ALU.add)
                    if b < 3:
                        link(ins)
                ins.then_inc(quad_done, 1)
                assert steps.n == DVE_STEPS

        @block.tensor
        def _(pe):
            pe.wait_ge(const_in, 48)
            pe.wait_ge(w_ready, 3)
            with pe.Fori(0, NQ) as q:
                for b in range(4):
                    pe.wait_ge(xn0_ready, q * 4 + b + 1)
                    for c in range(EC):
                        ins = pe.transpose(tr[:, c, b * P:(b + 1) * P], xf[0][:, b, c * P:(c + 1) * P], ident[:])
                ins.then_inc(xnT_full, 1)
                for f in range(EC):
                    for c in range(EC):
                        pe.wait_ge(split_ready, q * 8 + c + 1)
                        ins = mm3(pe, mm[:, f, :], (w_hi[:, 0, c, f * P:(f + 1) * P], w_lo[:, 0, c, f * P:(f + 1) * P]),
                                  (x_hi[0][:, c, :], x_lo[0][:, c, :]), c == 0, c == EC - 1)
                    ins.then_inc(k_full, 1)
                pe.wait_ge(xn_ready, q * 4 + 4)
                for b in range(4):
                    for c in range(EC):
                        pe.wait_ge(split_ready, q * 8 + 4 + c + 1)
                        ins = mm3(pe, tr[:, b, :], (x_hi[1][:, c, b * P:(b + 1) * P], x_lo[1][:, c, b * P:(b + 1) * P]),
                                  (w_hi[:, 1, c, :], w_lo[:, 1, c, :]), c == 0, c == EC - 1)
                    ins.then_inc(r_full, 1)
                for b in range(4):
                    for c in range(EC):
                        pe.wait_ge(k2_split_ready, q * 4 + (c + 1 if b == 0 else 4))
                        ins = mm3(pe, mm[:, b, :], (x_hi[0][:, c, b * P:(b + 1) * P], x_lo[0][:, c, b * P:(b + 1) * P]),
                                  (w_hi[:, 2, c, :], w_lo[:, 2, c, :]), c == 0, c == EC - 1)
                    ins.then_inc(y_full, 1)


def cross_attend(nc, io, x3, out):
    HT = 8
    G = NH // 2
    RING = 2
    STAGE = 6 * 16 + 4 * 16 + HT
    HALF = 2 * STAGE + 4 * 16
    KW = L + 2
    BANK_TR, BANK_SC, BANK_PV, BANK_BV = 2, 4, 6, 7
    HV = {"bq": 0, "bk": 1, "bv": 2, "bias_k": 3, "bias_v": 4}
    with ExitStack() as ctx:
        def sb(n, s, d=F32):
            return ctx.enter_context(nc.sbuf_tensor("ca_" + n, s, d))

        def two(n, s):
            return (sb(n + "_hi", s, FR), sb(n + "_lo", s, FR))

        def sem(n):
            return ctx.enter_context(nc.semaphore("ca_" + n))

        vec = sb("vec", [P, NV])
        hv = sb("hv", [P, 11 * NH])
        ident = sb("ident", [P, P])
        eps = sb("eps", [P, 1])
        bo = sb("bo", [P, 3, E])
        bias_k = two("bias_k", [P, 2 * NH])
        c2 = two("ctx", [P, EC, HT * L])
        h2 = two("h", [P, EC, HT * L])
        xres = sb("xres", [P, HT, E])
        lt = sb("lt", [P, 4, E])
        lh = sb("lh", [P, EC, QT])
        stats = sb("stats", [P, 4, 6])
        mv = sb("mv", [P, 4, 2])
        std = sb("std", [P, 4])
        rstd = sb("rstd", [P, 4])
        sq, sk, sv = sb("sq", [P, EC, 256]), sb("sk", [P, EC, 256]), sb("sv", [P, EC, 256])
        so = sb("so", [P, 2, E])
        wq, wk, wv = two("wq", [P, EC, 256]), two("wk", [P, EC, 256]), two("wv", [P, EC, 256])
        wo = two("wo", [P, 2, E])
        qT = [two("q%d" % i, [P, QT]) for i in range(2)]
        kT = [two("k%d" % i, [P, 4, KW]) for i in range(2)]
        vT = two("v", [P, 4, 256])
        pr = [sb("pr%d" % i, [P, 4, KW]) for i in range(2)]
        pT = [two("pt%d" % i, [P, QT]) for i in range(2)]
        cT = [two("ct%d" % i, [P, QT]) for i in range(2)]
        mxs = [sb("mx%d" % i, [P, 4]) for i in range(2)]
        nbs = [sb("nb%d" % i, [P, 4]) for i in range(2)]
        sms = [sb("sm%d" % i, [P, 4]) for i in range(2)]
        rss = [sb("rs%d" % i, [P, 4]) for i in range(2)]
        pb = sb("pb", [P, HT, NH])
        dbias = sb("dbias", [P, NH, NH])
        db = two("db", [P, 2, NH])
        bvs = sb("bvs", [NH, E])
        pbT = sb("pbT", [NH, HT * L])
        ps = ctx.enter_context(nc.psum_tensor("ca_ps", [P, 8, QT], F32))

        const_in, ready, bk_hi, bk_split = sem("const_in"), sem("ready"), sem("bk_hi"), sem("bk_split")
        x_in, c_in, c_hi, c_split, out_done = sem("x_in"), [sem("c_in0"), sem("c_in1")], sem("c_hi"), sem("c_split"), sem("out_done")
        wq_in, wk_in, wv_in, wo_in = sem("wq_in"), sem("wk_in"), sem("wv_in"), sem("wo_in")
        wq_hi, wk_hi, wv_hi, wo_hi = sem("wq_hi"), sem("wk_hi"), sem("wv_hi"), sem("wo_hi")
        wq_split, wk_split, wv_split, wo_split = sem("wq_split"), sem("wk_split"), sem("wv_split"), sem("wo_split")
        bn_done, stats_ready, std_ready, xn0_ready = sem("bn_done"), sem("stats_ready"), sem("std_ready"), sem("xn0_ready")
        ln_step, lnT_full, lh_ready, h_hi, h_split = sem("ln_step"), sem("lnT_full"), sem("lh_ready"), sem("h_hi"), sem("h_split")
        bo_added, dbias_ready = sem("bo_added"), sem("dbias_ready")
        ring_full, evacuated, p_hi = sem("ring_full"), sem("evacuated"), sem("p_hi")
        sc_full, mx_done, max_done, exp_done = sem("sc_full"), sem("mx_done"), sem("max_done"), sem("exp_done")
        rs_done, pn_done, norm_done = sem("rs_done"), sem("pn_done"), sem("norm_done")
        tr_full, pt_hi, pt_split = sem("tr_full"), sem("pt_hi"), sem("pt_split")
        pv_full, ct_hi, ct_split = sem("pv_full"), sem("ct_hi"), sem("ct_split")
        act_waited = sem("act_waited")
        db_hi, db_ready, pbT_full, pbT_ready = sem("db_hi"), sem("db_ready"), sem("pbT_full"), sem("pbT_ready")
        fc1_full, gelu_ready, u_hi, u_split = sem("fc1_full"), sem("gelu_ready"), sem("u_hi"), sem("u_split")

        class Slot:

            def __init__(self, h, st, g, quad, proj=True, attn=True):
                self.h, self.st, self.g, self.quad, self.proj, self.attn = h, st, g, quad, proj, attn
                s = g * 2 + quad
                self.s = s
                self.n = h * 32 + (st * 16 + s)
                self.gu = g if quad else g - 1
                self.qu = 1 - quad
                self.ring = h * HALF + (st * STAGE + s * 10 - (4 if attn else 0))
                self.projected = self.ring - (0 if isinstance(g, int) and s <= 1 else 4)
                if not proj:
                    self.out0 = self.ring
                else:
                    self.out0 = self.ring + 6
                self.gq = h * 24 + (st * 8 + g)
                self.gk = h * 16 + (st * 8 + g)

        def attention_slots(engine, h, st, slot):
            slot(Slot(h, st, 0, 0, attn=False))
            slot(Slot(h, st, 0, 1))
            with engine.Fori(1, G) as g:
                slot(Slot(h, st, g, 0))
                slot(Slot(h, st, g, 1))
            slot(Slot(h, st, G, 0, proj=False))

        class MlpSlot:
            def __init__(self, h, g, quad, proj=True, outp=True):
                self.h, self.g, self.quad, self.proj, self.outp = h, g, quad, proj, outp
                s = g * 2 + quad
                self.n = h * 16 + s
                self.out0 = h * HALF + (2 * STAGE + s * 4 - 4)
                self.gq = h * 24 + (16 + g)
                self.u = pT if quad == 0 else cT
                self.u_last = cT if quad == 0 else pT

        def mlp_slots(engine, h, slot):
            slot(MlpSlot(h, 0, 0, outp=False))
            slot(MlpSlot(h, 0, 1))
            with engine.Fori(1, G) as g:
                slot(MlpSlot(h, g, 0))
                slot(MlpSlot(h, g, 1))
            slot(MlpSlot(h, G, 0, proj=False))

        def wait_apart(act):
            act.sem_inc(act_waited, 1)

        def head_col(st, kind, g, hd):
            return hv[:, bass.ds(g * 2 + ((st * 5 + HV[kind]) * NH + hd), 1)]

        block = ctx.enter_context(nc.Block())

        @block.sync
        def _(sp):
            for tile, name in ((vec, "vec"), (ident, "ident"), (hv, "head_vec"), (bo, "bo")):
                sp.dma_start(tile[:], io[name]).then_inc(const_in, 16)
            sp.dma_start(sq[:], io["wq"][0]).then_inc(wq_in, 16)
            sp.dma_start(sk[:], io["wk"][0]).then_inc(wk_in, 16)
            with sp.Fori(0, 2) as h:
                sp.wait_ge(out_done, h * 16 + 16)
                for quad, tile in ((0, lt), (1, lh)):
                    sp.dma_start(tile[:], io["ctxT"][:, :, bass.ds(h * (HT * L) + quad * QT, QT)]).then_inc(c_in[quad], 16)
                sp.dma_start(xres[:], x3[bass.ds(h * HT, HT)].rearrange("b t e -> t b e")).then_inc(x_in, 16)
                for st in range(2):
                    with sp.Fori(0, G) as g:
                        gq, gk = h * 24 + (st * 8 + g), h * 16 + (st * 8 + g)
                        sp.wait_ge(wv_split, gk + 1)
                        sp.dma_start(sv[:], io["wv"][bass.ds(g + st * 8, 1)].rearrange("a p c m -> (a p) c m")).then_inc(wv_in, 16)
                        sp.wait_ge(wo_split, gq + 1)
                        sp.dma_start(so[:], io["wo"][bass.ds(g + st * 8, 1)].rearrange("a p c m -> (a p) c m")).then_inc(wo_in, 16)
                        sp.wait_ge(wq_split, (gq + 1) * 2)
                        sp.dma_start(sq[:], io["wq"][bass.ds(g + (st * 8 + 1), 1)].rearrange("a p c m -> (a p) c m")).then_inc(wq_in, 16)
                        sp.wait_ge(wk_split, gk + 1)
                        sp.dma_start(sk[:], io["wk"][bass.ds(g + (st * 8 + 1), 1)].rearrange("a p c m -> (a p) c m")).then_inc(wk_in, 16)
                with sp.Fori(0, G) as g:
                    gq = h * 24 + (16 + g)
                    sp.wait_ge(wo_split, gq + 1)
                    sp.dma_start(so[:], io["wo"][bass.ds(g + 16, 1)].rearrange("a p c m -> (a p) c m")).then_inc(wo_in, 16)
                    sp.wait_ge(wq_split, (gq + 1) * 2)
                    sp.dma_start(sq[:], io["wq"][bass.ds(g + 17, 1)].rearrange("a p c m -> (a p) c m")).then_inc(wq_in, 16)
                sp.wait_ge(evacuated, h * HALF + (HALF + RING))
                sp.dma_start(out[bass.ds(h * HT, HT)].rearrange("b t e -> t b e"), xres[:]).then_inc(out_done, 16)
            sp.wait_ge(out_done, 3 * 16)

        @block.gpsimd
        def _(gp):
            gp.memset(eps[:], EPS).then_inc(ready, 1)
            gp.memset(dbias[:], 0.0).then_inc(ready, 1)
            for hd in range(2):
                gp.memset(kT[hd][0][:, :, L + 1:KW].bitcast(F32), 0.0).then_inc(ready, 1)
                gp.memset(kT[hd][1][:, :, L + 1:KW].bitcast(F32), 0.0).then_inc(ready, 1)
            for s, n in ((out_done, 16), (wv_split, 1), (wo_split, 1), (evacuated, RING), (exp_done, 1),
                         (ct_split, 1), (tr_full, 2)):
                gp.memset(pb[0:1, 0, 0:1], 0.0).then_inc(s, n)
                gp.drain()
            gp.wait_ge(const_in, 64)
            with gp.Fori(0, 2) as h:
                for st in range(3):
                    gp.wait_ge(xn0_ready, (h * 3 + st) * 8 + 8)
                    for b in range(HT):
                        ins = gp.tensor_tensor(xres[:, b, :], xres[:, b, :], bo[:, st, :], ALU.add)
                    ins.then_inc(bo_added, 1)

        @block.scalar
        def _(act):
            def split_q(gq, k):
                act.wait_ge(wq_in, (gq + 1) * 16)
                act.activation(wq[0][:, :, k * P:(k + 1) * P], sq[:, :, k * P:(k + 1) * P], ACT.Copy).then_inc(wq_hi, 1)

            def split_one(w, raw, w_in, w_hi, g):
                act.wait_ge(w_in, (g + 1) * 16)
                act.activation(w[0][:], raw[:], ACT.Copy).then_inc(w_hi, 1)

            def slot(S):
                st = S.st

                def project_hi(k):
                    act.wait_ge(ring_full, S.ring + (k + 1))
                    src = ps[:, k % RING, :]
                    if k >= 4:
                        act.activation(vT[0][:, (k - 4) * 2:(k - 4) * 2 + 2, :].rearrange("p b m -> p (b m)"), src, ACT.Copy).then_inc(p_hi, 1)
                        return
                    hd = k // 2
                    wait_apart(act)
                    if k % 2 == 0:
                        act.activation(qT[hd][0][:], src, ACT.Identity, bias=head_col(st, "bq", S.g, hd)).then_inc(p_hi, 1)
                    else:
                        act.activation(kT[hd][0][:, :, 0:L], src.rearrange("p (b t) -> p b t", b=4), ACT.Identity,
                                       bias=head_col(st, "bk", S.g, hd)).then_inc(p_hi, 1)

                def exps(hd):
                    act.wait_ge(max_done, S.n * 2 + (hd - 1))
                    act.wait_ge(tr_full, S.n * 2 + (hd - 1))
                    for b in range(4):
                        o = (b % 2) * KW
                        ins = act.activation(pr[hd][:, b, 0:L + 1], ps[:, BANK_SC + b // 2, o:o + L + 1], ACT.Exp,
                                             bias=nbs[hd][:, b:b + 1], scale=SCALE, accum_out=sms[hd][:, b:b + 1])
                    ins.then_inc(exp_done, 1)

                def probs_hi(hd):
                    act.wait_ge(tr_full, S.n * 2 + (hd - 1 + 2))
                    act.activation(pT[hd][0][:], ps[:, BANK_TR + hd, :], ACT.Copy).then_inc(pt_hi, 1)

                def context_hi(hd):
                    act.wait_ge(pv_full, S.n * 2 + (hd - 1))
                    wait_apart(act)
                    act.activation(cT[hd][0][:], ps[:, BANK_PV, :], ACT.Identity, bias=head_col(st, "bv", S.gu, hd)).then_inc(ct_hi, 1)

                if S.attn:
                    act.wait_ge(ring_full, S.ring)
                if S.proj and S.quad == 0:
                    split_one(wv, sv, wv_in, wv_hi, S.gk)
                if S.proj and S.quad == 1:
                    split_one(wo, so, wo_in, wo_hi, S.gq)
                if S.attn:
                    exps(0)
                if S.proj:
                    project_hi(0)
                if S.attn:
                    exps(1)
                if S.proj:
                    project_hi(1)
                if S.attn:
                    probs_hi(0)
                if S.proj:
                    project_hi(2)
                    if S.quad == 1:
                        split_q(S.gq + 1, 0)
                if S.attn:
                    probs_hi(1)
                    context_hi(0)
                if S.proj:
                    project_hi(3)
                    if S.quad == 1:
                        split_q(S.gq + 1, 1)
                if S.attn:
                    context_hi(1)
                if S.proj:
                    project_hi(4)
                    if S.quad == 1:
                        split_one(wk, sk, wk_in, wk_hi, S.gk + 1)
                    project_hi(5)

            def mlp_slot(S):
                if S.outp:
                    act.wait_ge(ring_full, S.out0)
                if S.proj and S.quad == 1:
                    split_one(wo, so, wo_in, wo_hi, S.gq)
                if S.proj:
                    for k in range(2):
                        act.wait_ge(fc1_full, S.n * 2 + (k + 1))
                        act.wait_ge(u_split, S.n * 2 + (k + 1))
                        wait_apart(act)
                        act.activation(lt[:, k, :], ps[:, BANK_SC + k, :], ACT.Gelu,
                                       bias=hv[:, bass.ds(S.g * 2 + (10 * NH + k), 1)]).then_inc(gelu_ready, 1)
                        if S.quad == 1:
                            split_q(S.gq + 1, k)
                        act.wait_ge(gelu_ready, S.n * 2 + (k + 1))
                        act.activation(S.u[k][0][:], lt[:, k, :], ACT.Copy).then_inc(u_hi, 1)

            act.wait_ge(const_in, 64)
            act.activation(bias_k[0][:].rearrange("p (s h) -> p s h", s=2),
                           hv[:, 0:10 * NH].rearrange("p (s k h) -> p s k h", s=2, k=5)[:, :, HV["bias_k"], :], ACT.Copy).then_inc(bk_hi, 1)
            act.wait_ge(ready, 6)
            split_q(0, 0)
            split_q(0, 1)
            split_one(wk, sk, wk_in, wk_hi, 0)
            with act.Fori(0, 2) as h:
                for quad, tile in ((0, lt), (1, lh)):
                    act.wait_ge(c_in[quad], h * 16 + 16)
                    act.activation(c2[0][:, :, quad * QT:(quad + 1) * QT], tile[:], ACT.Copy).then_inc(c_hi, 1)
                for st in range(3):
                    for quad in range(2):
                        r = (h * 3 + st) * 2 + quad
                        act.wait_ge(stats_ready, r + 1)
                        act.activation(std[:, :], mv[:, :, 1], ACT.Sqrt, bias=eps[:]).then_inc(std_ready, 1)
                        for c in range(EC):
                            act.wait_ge(lh_ready, r * 4 + (c + 1))
                            act.activation(h2[0][:, c, quad * QT:(quad + 1) * QT], lh[:, c, :], ACT.Copy).then_inc(h_hi, 1)
                    if st < 2:
                        attention_slots(act, h, st, slot)
                        act.wait_ge(pbT_full, h * 2 + (st + 1))
                        act.activation(bvs[:], ps[0:NH, BANK_BV, :], ACT.Copy)
                        act.activation(pbT[:], ps[0:NH, BANK_TR:BANK_TR + 2, :].rearrange("p a b -> p (a b)"), ACT.Copy).then_inc(pbT_ready, 1)
                    else:
                        mlp_slots(act, h, mlp_slot)

        @block.vector
        def _(v):
            def split_q(gq, k):
                v.wait_ge(wq_hi, gq * 2 + (k + 1))
                v.tensor_tensor(wq[1][:, :, k * P:(k + 1) * P], sq[:, :, k * P:(k + 1) * P], wq[0][:, :, k * P:(k + 1) * P],
                                ALU.subtract).then_inc(wq_split, 1)

            def split_one(w, raw, w_hi, w_split, g):
                v.wait_ge(w_hi, g + 1)
                v.tensor_tensor(w[1][:], raw[:], w[0][:], ALU.subtract).then_inc(w_split, 1)

            def add_output(idx, b, bank):
                v.wait_ge(ring_full, idx + 1)
                v.tensor_tensor(xres[:, b, :], xres[:, b, :], ps[:, bank, :], ALU.add).then_inc(evacuated, 1)

            def slot(S):
                st = S.st

                def project_lo(k):
                    v.wait_ge(p_hi, S.n * 6 + (k + 1))
                    src = ps[:, k % RING, :]
                    if k >= 4:
                        tiles = [t[:, (k - 4) * 2:(k - 4) * 2 + 2, :].rearrange("p b m -> p (b m)") for t in vT]
                        v.tensor_tensor(tiles[1], src, tiles[0], ALU.subtract).then_inc(evacuated, 1)
                        return
                    hd = k // 2
                    if k % 2 == 0:
                        v.scalar_tensor_tensor(out=qT[hd][1][:], in0=src, scalar=head_col(st, "bq", S.g, hd),
                                               in1=qT[hd][0][:], op0=ALU.add, op1=ALU.subtract).then_inc(evacuated, 1)
                    else:
                        for t in range(2):
                            v.tensor_scalar(kT[hd][t][:, :, L:L + 1],
                                            bias_k[t][:, bass.ds(S.g * 2 + (st * NH + hd), 1)].rearrange("p (a b) -> p a b", b=1).broadcast_to([P, 4, 1]),
                                            1.0, None, ALU.mult)
                        v.scalar_tensor_tensor(out=kT[hd][1][:, :, 0:L], in0=src.rearrange("p (b t) -> p b t", b=4),
                                               scalar=head_col(st, "bk", S.g, hd), in1=kT[hd][0][:, :, 0:L],
                                               op0=ALU.add, op1=ALU.subtract).then_inc(evacuated, 1)

                def row_max(hd):
                    v.wait_ge(sc_full, S.n * 2 + (hd - 1))
                    sc = ps[:, BANK_SC:BANK_SC + 2, 0:2 * KW].rearrange("p a (b k) -> p a b k", b=2)[:, :, :, 0:L + 1]
                    v.tensor_reduce(mxs[hd][:].rearrange("p (a b) -> p a b", a=2), sc, AX, ALU.max).then_inc(mx_done, 1)
                    v.wait_ge(mx_done, S.n * 2 + (hd - 1))
                    v.tensor_scalar(nbs[hd][:], mxs[hd][:], -SCALE, None, ALU.mult).then_inc(max_done, 1)

                def normalise(hd):
                    v.wait_ge(exp_done, S.n * 2 + (hd - 1 + 1))
                    v.reciprocal(rss[hd][:], sms[hd][:]).then_inc(rs_done, 1)
                    v.wait_ge(rs_done, S.n * 2 + (hd - 1))
                    v.tensor_tensor(pr[hd][:, :, 0:L + 1], pr[hd][:, :, 0:L + 1],
                                    rss[hd][:].rearrange("p (a b) -> p a b", b=1).broadcast_to([P, 4, L + 1]), ALU.mult).then_inc(pn_done, 1)
                    v.wait_ge(pn_done, S.n * 2 + (hd - 1))
                    v.tensor_scalar(pb[:, S.qu * 4:S.qu * 4 + 4, bass.ds(S.gu * 2 + hd, 1)], pr[hd][:, :, L:L + 1], 1.0, None,
                                    ALU.mult).then_inc(norm_done, 1)

                def probs_lo(hd):
                    v.wait_ge(pt_hi, S.n * 2 + (hd - 1))
                    v.tensor_tensor(pT[hd][1][:], ps[:, BANK_TR + hd, :], pT[hd][0][:], ALU.subtract).then_inc(pt_split, 1)

                def context_lo(hd):
                    v.wait_ge(ct_hi, S.n * 2 + (hd - 1))
                    v.scalar_tensor_tensor(out=cT[hd][1][:], in0=ps[:, BANK_PV, :], scalar=head_col(st, "bv", S.gu, hd),
                                           in1=cT[hd][0][:], op0=ALU.add, op1=ALU.subtract).then_inc(ct_split, 1)

                if S.proj and S.quad == 0:
                    split_one(wv, sv, wv_hi, wv_split, S.gk)
                if S.proj and S.quad == 1:
                    split_one(wo, so, wo_hi, wo_split, S.gq)
                    v.tensor_scalar(db[0][:], dbias[:, bass.ds(S.g * 2, 2), :], 1.0, None, ALU.mult).then_inc(db_hi, 1)
                    v.wait_ge(db_hi, S.gk + 1)
                    v.tensor_tensor(db[1][:], dbias[:, bass.ds(S.g * 2, 2), :], db[0][:], ALU.subtract).then_inc(db_ready, 1)
                if S.attn:
                    row_max(0)
                if S.proj:
                    project_lo(0)
                if S.attn:
                    normalise(0)
                    row_max(1)
                if S.proj:
                    project_lo(1)
                if S.attn:
                    normalise(1)
                    probs_lo(0)
                if S.proj:
                    project_lo(2)
                    if S.quad == 1:
                        split_q(S.gq + 1, 0)
                if S.attn:
                    probs_lo(1)
                    context_lo(0)
                if S.proj:
                    project_lo(3)
                    if S.quad == 1:
                        split_q(S.gq + 1, 1)
                if S.attn:
                    context_lo(1)
                if S.proj:
                    project_lo(4)
                    if S.quad == 1:
                        split_one(wk, sk, wk_hi, wk_split, S.gk + 1)
                    project_lo(5)
                if S.attn:
                    v.wait_ge(bo_added, S.h * 3 + (st + 1))
                    for b in range(4):
                        add_output(S.out0 + b, S.qu * 4 + b, b % RING)

            def mlp_slot(S):
                if S.proj and S.quad == 1:
                    split_one(wo, so, wo_hi, wo_split, S.gq)
                if S.proj:
                    for k in range(2):
                        if S.quad == 1:
                            split_q(S.gq + 1, k)
                        v.wait_ge(u_hi, S.n * 2 + (k + 1))
                        v.tensor_tensor(S.u[k][1][:], lt[:, k, :], S.u[k][0][:], ALU.subtract).then_inc(u_split, 1)
                if S.outp:
                    v.wait_ge(bo_added, S.h * 3 + 3)
                    for b in range(4):
                        add_output(S.out0 + b, (1 - S.quad) * 4 + b, b % RING)

            v.wait_ge(bk_hi, 1)
            v.tensor_tensor(bias_k[1][:].rearrange("p (s h) -> p s h", s=2),
                            hv[:, 0:10 * NH].rearrange("p (s k h) -> p s k h", s=2, k=5)[:, :, HV["bias_k"], :],
                            bias_k[0][:].rearrange("p (s h) -> p s h", s=2), ALU.subtract).then_inc(bk_split, 1)
            v.memset(std[:], 1.0).then_inc(u_split, 2)
            v.wait_ge(bk_split, 1)
            v.wait_ge(ready, 6)
            split_q(0, 0)
            split_q(0, 1)
            split_one(wk, sk, wk_hi, wk_split, 0)
            with v.Fori(0, 2) as h:
                for quad, tile in ((0, lt), (1, lh)):
                    v.wait_ge(c_hi, h * 2 + (quad + 1))
                    v.tensor_tensor(c2[1][:, :, quad * QT:(quad + 1) * QT], tile[:], c2[0][:, :, quad * QT:(quad + 1) * QT],
                                    ALU.subtract).then_inc(c_split, 1)
                v.wait_ge(c_split, h * 2 + 2)
                v.wait_ge(x_in, h * 16 + 16)
                for st in range(3):
                    if st < 2:
                        col = (st * 5 + HV["bias_v"]) * NH, (st * 5 + HV["bv"]) * NH
                        v.tensor_tensor(dbias[:].rearrange("p a b -> p (a b)")[:, 0:NH * NH:NH + 1], hv[:, col[0]:col[0] + NH],
                                        hv[:, col[1]:col[1] + NH], ALU.subtract).then_inc(dbias_ready, 1)
                        v.wait_ge(dbias_ready, h * 2 + (st + 1))
                    for quad in range(2):
                        r = (h * 3 + st) * 2 + quad
                        step = [0]

                        def link(ins):
                            step[0] += 1
                            assert step[0] == 1
                            ins.then_inc(ln_step, 1)
                            v.wait_ge(ln_step, r + 1)

                        if quad == 1:
                            v.wait_ge(lnT_full, r)
                            v.wait_ge(h_split, r * 4)
                        layernorm_dve(v, xres[:, quad * 4:quad * 4 + 4, :], lt, stats, mv, std, rstd, bn_done,
                                      stats_ready, std_ready, xn0_ready, r, link)
                        v.wait_ge(xn0_ready, r * 4 + 4)
                        v.wait_ge(lnT_full, r + 1)
                        for c in range(EC):
                            w, b_ = VEC["s%d" % (st + 1)] + c, VEC["o%d" % (st + 1)] + c
                            v.tensor_scalar(lh[:, c, :], ps[:, c, :], vec[:, w:w + 1], vec[:, b_:b_ + 1], ALU.mult, ALU.add).then_inc(lh_ready, 1)
                        for c in range(EC):
                            v.wait_ge(h_hi, r * 4 + (c + 1))
                            v.tensor_tensor(h2[1][:, c, quad * QT:(quad + 1) * QT], lh[:, c, :], h2[0][:, c, quad * QT:(quad + 1) * QT],
                                            ALU.subtract).then_inc(h_split, 1)
                    if st < 2:
                        attention_slots(v, h, st, slot)
                        base = h * HALF + (st * STAGE + 160)
                        for b in range(HT):
                            add_output(base + b, b, b % RING)
                        v.wait_ge(evacuated, base + (HT + RING))
                    else:
                        mlp_slots(v, h, mlp_slot)
                        v.wait_ge(evacuated, h * HALF + (HALF + RING))

        @block.tensor
        def _(pe):
            def ring_wait(idx):
                pe.wait_ge(evacuated, idx + 1)

            def slot(S):
                st = S.st
                cols = slice(S.quad * QT, (S.quad + 1) * QT)

                def project(k):
                    ring_wait(S.ring + k)
                    if k < 4:
                        hd = k // 2
                        w, x = (wq, h2) if k % 2 == 0 else (wk, c2)
                        if k % 2 == 0:
                            pe.wait_ge(wq_split, S.gq * 2 + (hd + 1))
                        else:
                            pe.wait_ge(wk_split, S.gk + 1)
                        for c in range(EC):
                            ins = mm3(pe, ps[:, k % RING, :], [t[:, c, hd * P:(hd + 1) * P] for t in w],
                                      [t[:, c, cols] for t in x], c == 0, c == EC - 1)
                    else:
                        pe.wait_ge(wv_split, S.gk + 2)
                        for b in range(2):
                            t0 = S.quad * QT + ((k - 4) * 2 + b) * L
                            for c in range(EC):
                                ins = mm3(pe, ps[:, k % RING, b * 256:(b + 1) * 256], [t[:, c, t0:t0 + L] for t in c2],
                                          [t[:, c, :] for t in wv], c == 0, c == EC - 1)
                    ins.then_inc(ring_full, 1)

                def scores(hd):
                    if hd == 0:
                        pe.wait_ge(evacuated, S.projected + RING)
                    pe.wait_ge(exp_done, S.n * 2 + (hd - 1))
                    for b in range(4):
                        o = (b % 2) * KW
                        ins = mm3(pe, ps[:, BANK_SC + b // 2, o:o + KW], [t[:, b * L:(b + 1) * L] for t in qT[hd]],
                                  [t[:, b, :] for t in kT[hd]], True, True)
                    ins.then_inc(sc_full, 1)

                def transpose(hd):
                    pe.wait_ge(norm_done, S.n * 2 + (hd - 1))
                    for b in range(4):
                        ins = pe.transpose(ps[:, BANK_TR + hd, b * L:(b + 1) * L], pr[hd][:, b, 0:L], ident[:])
                    ins.then_inc(tr_full, 1)

                def context(hd):
                    pe.wait_ge(pt_split, S.n * 2 + (hd - 1))
                    pe.wait_ge(ct_split, S.n * 2 + (hd - 1))
                    for b in range(4):
                        ins = mm3(pe, ps[:, BANK_PV, b * L:(b + 1) * L], [t[:, b, hd * P:(hd + 1) * P] for t in vT],
                                  [t[:, b * L:(b + 1) * L] for t in pT[hd]], True, True)
                    ins.then_inc(pv_full, 1)

                def outputs():
                    pe.wait_ge(ct_split, S.n * 2 + 1)
                    for b in range(4):
                        ring_wait(S.out0 + b)
                        for hd in range(2):
                            ins = mm3(pe, ps[:, b % RING, :], [t[:, b * L:(b + 1) * L] for t in cT[hd]],
                                      [t[:, hd, :] for t in wo], hd == 0, hd == 1)
                        ins.then_inc(ring_full, 1)

                if S.attn:
                    scores(0)
                if S.proj:
                    project(0)
                if S.attn:
                    scores(1)
                if S.proj:
                    project(1)
                if S.attn:
                    transpose(0)
                if S.proj:
                    project(2)
                if S.attn:
                    transpose(1)
                    context(0)
                if S.proj:
                    project(3)
                if S.attn:
                    context(1)
                if S.proj:
                    project(4)
                    project(5)
                    if S.quad == 1:
                        pe.wait_ge(wo_split, S.gq + 2)
                        pe.wait_ge(db_ready, S.gk + 1)
                        for hd in range(2):
                            for i, (a, b) in enumerate(((0, 0), (0, 1), (1, 0))):
                                pe.matmul(ps[0:NH, BANK_BV, :], db[a][:, hd, :], wo[b][:, hd, :],
                                          start=isinstance(S.g, int) and hd == 0 and i == 0, stop=False, skip_group_check=True)
                if S.attn:
                    outputs()

            def mlp_slot(S):
                if S.proj:
                    for k in range(2):
                        pe.wait_ge(wq_split, S.gq * 2 + (k + 1))
                        if S.outp:
                            pe.wait_ge(gelu_ready, S.n * 2 + (k - 1))
                        for c in range(EC):
                            ins = mm3(pe, ps[:, BANK_SC + k, :], [t[:, c, k * P:(k + 1) * P] for t in wq],
                                      [t[:, c, S.quad * QT:(S.quad + 1) * QT] for t in h2], c == 0, c == EC - 1)
                        ins.then_inc(fc1_full, 1)
                if S.outp:
                    pe.wait_ge(u_split, S.n * 2 + 2)
                    pe.wait_ge(wo_split, (S.gq + 2) if S.quad == 1 else (S.gq + 1))
                    for b in range(4):
                        ring_wait(S.out0 + b)
                        for k in range(2):
                            ins = mm3(pe, ps[:, b % RING, :], [t[:, b * L:(b + 1) * L] for t in S.u_last[k]],
                                      [t[:, k, :] for t in wo], k == 0, k == 1)
                        ins.then_inc(ring_full, 1)

            pe.wait_ge(const_in, 64)
            with pe.Fori(0, 2) as h:
                for st in range(3):
                    for quad in range(2):
                        r = (h * 3 + st) * 2 + quad
                        if quad == 1:
                            pe.wait_ge(lh_ready, r * 4)
                        for b in range(4):
                            pe.wait_ge(xn0_ready, r * 4 + (b + 1))
                            for c in range(EC):
                                ins = pe.transpose(ps[:, c, b * P:(b + 1) * P], lt[:, b, c * P:(c + 1) * P], ident[:])
                        ins.then_inc(lnT_full, 1)
                    pe.wait_ge(h_split, (h * 3 + st) * 8 + 8)
                    if st == 0:
                        pe.wait_ge(c_split, h * 2 + 2)
                        pe.wait_ge(ready, 6)
                    if st < 2:
                        attention_slots(pe, h, st, slot)
                        for b in range(HT):
                            ins = pe.transpose(ps[0:NH, BANK_TR + b // 4, (b % 4) * P:(b % 4 + 1) * P], pb[:, b, :], ident[:])
                        ins.then_inc(pbT_full, 1)
                        pe.wait_ge(pbT_ready, h * 2 + (st + 1))
                        base = h * HALF + (st * STAGE + 160)
                        for b in range(HT):
                            ring_wait(base + b)
                            pe.matmul(ps[:, b % RING, :], pbT[:, b * P:(b + 1) * P], bvs[:], start=True, stop=True).then_inc(ring_full, 1)
                    else:
                        mlp_slots(pe, h, mlp_slot)


def build(nc, io, out):
    x2 = nc.dram_tensor("x2_dram", (B, L, E), F32, kind="Internal").ap()
    time_mix(nc, io, x2)
    x3 = nc.dram_tensor("x3_dram", (B, L, E), F32, kind="Internal").ap()
    channel_mix(nc, io, x2, x3)
    cross_attend(nc, io, x3, out)


def vec_table(a):
    return np.ascontiguousarray(a.reshape(-1, EC, P).transpose(2, 0, 1).reshape(P, -1))


def w_tiles(w, m):
    k, n = w.shape
    return np.ascontiguousarray(w.reshape(k // P, P, n // m, m).transpose(2, 1, 0, 3))


def layouts(i):
    a = {}
    p = "L0_xattn_"
    a["x"] = i["x"]
    ctx = i["ctx_2048"]
    vecs = [i[p + n] for n in ("ln1_w", "ln1_b", "ln2_w", "ln2_b", "maa_x")] + [i[p + "maa_stack"][m] for m in range(5)]
    vecs += [i[p + "time_decay"], i[p + "faaaa"].reshape(E), i[p + "gn_w"], i[p + "gn_b"], i[p + "ffn_maa_k"], i[p + "ffn_maa_r"]]
    vecs += [i["L1_xattn_" + n] for n in ("ln1_scale", "ln1_offset", "ln2_scale", "ln2_offset", "ln_mlp_scale", "ln_mlp_offset")]
    a["vec"] = vec_table(np.stack(vecs))
    a["ident"] = np.eye(P, dtype=np.float32)
    same = np.kron(np.eye(8, dtype=np.float32), np.ones((HS, HS), np.float32))
    a["head_sum"] = same
    a["head_mean"] = same / HS
    pick = np.zeros((P, P + HS - 1), np.float32)
    pick[np.arange(P), np.arange(P) // HS * HS + HS - 1] = 1
    a["pick_k"] = pick
    spread = np.zeros((P, HS, P), np.float32)
    for d in range(HS):
        spread[:, d, :] = same * (np.arange(P)[:, None] % HS == d)
    a["spread_v"] = spread.reshape(P, HS * P)
    a["prev1"] = np.ascontiguousarray(ctx[:, 1, :].reshape(B, EC, P).transpose(2, 1, 0))
    a["prev0"] = np.ascontiguousarray(ctx[:, 0, :].reshape(B, EC, P).transpose(2, 1, 0))
    a["s0"] = np.ascontiguousarray(ctx[:, 2:2 + HS, :].reshape(B, EC, P, HS).transpose(2, 1, 3, 0))
    a["l0w"] = np.stack([w_tiles(i[p + n].T, E)[0] for n in ("Wr", "Wk", "Wv", "Wg", "Wo", "ffn_Wk", "ffn_Wr", "ffn_Wv")])
    a["lora1"] = w_tiles(i[p + "maa_w1"], 160)[0]
    a["dec1"] = w_tiles(i[p + "decay_w1"], 64)[0]
    a["lora2"] = i[p + "maa_w2"].reshape(160, E)
    a["dec2"] = i[p + "decay_w2"]
    p = "L1_xattn_"
    a["ctxT"] = ctx.reshape(B * L, EC, P).transpose(2, 1, 0)
    a["head_vec"] = np.stack([i[p + n + s].reshape(NH, KD) for s in "12" for n in ("bq", "bk", "bv", "bias_k", "bias_v")]
                             + [i[p + "b_fc1"].reshape(NH, P)]).transpose(2, 0, 1).reshape(P, -1)
    a["bo"] = np.broadcast_to(np.stack([i[p + "bo1"], i[p + "bo2"], i[p + "b_fc2"]]), (P, 3, E))
    q = [w_tiles(i[p + n], 256) for n in ("wq1", "wq2", "w_fc1")]
    a["wq"] = np.concatenate(q + [q[0][0:1]])
    k = [w_tiles(i[p + n], 256) for n in ("wk1", "wk2")]
    a["wk"] = np.concatenate(k + [k[0][0:1]])
    a["wv"] = np.concatenate([w_tiles(i[p + n], 256) for n in ("wv1", "wv2")])
    a["wo"] = np.concatenate([i[p + n].reshape(NH // 2, 2, P, E).transpose(0, 2, 1, 3) for n in ("wo1", "wo2", "w_fc2")])
    return {k: np.ascontiguousarray(v) for k, v in a.items()}


def kernel(**inputs):
    import concourse.bacc as _bacc
    from concourse.bass_utils import run_bass_kernel_spmd as _run

    nc = _bacc.Bacc("TRN2", target_bir_lowering=False, num_devices=1)
    arrays = layouts({k: np.asarray(v) for k, v in inputs.items()})
    io = {n: nc.dram_tensor(f"in_{n}", a.shape, mybir.dt.from_np(a.dtype), kind="ExternalInput").ap() for n, a in arrays.items()}
    out = nc.dram_tensor("out_dram", (B, L, E), F32, kind="ExternalOutput").ap()
    build(nc, io, out)
    r = _run(nc, [{f"in_{n}": a for n, a in arrays.items()}], core_ids=[0])
    return r.results[0]["out_dram"]
```

```python
from contextlib import ExitStack

import numpy as np
import concourse.bass as bass
from concourse import mybir

ALU = mybir.AluOpType
ACT = mybir.ActivationFunctionType
AX = mybir.AxisListType.X
F32 = mybir.dt.float32
FR = mybir.dt.float32r

P = 128
B, L, E = 16, 128, 512
EC = E // P
NQ = B // 4
QT = 4 * L
HS = 16
EPS = 1e-5
NH, KD = 16, 128
F = 2048
SCALE = float(KD) ** -0.5
LORA = 32

VEC_NAMES = ["ln1_w", "ln1_b", "ln2_w", "ln2_b", "maa_x", "stack0", "stack1", "stack2", "stack3", "stack4",
             "time_decay", "faaaa", "gn_w", "gn_b", "ffn_maa_k", "ffn_maa_r",
             "s1", "o1", "s2", "o2", "s3", "o3"]
VEC = {n: i * EC for i, n in enumerate(VEC_NAMES)}
NV = len(VEC_NAMES) * EC


class Steps:

    def __init__(self, engine, sem, base=0):
        self.engine, self.sem, self.base, self.n = engine, sem, base, 0

    def link(self, instruction):
        self.n += 1
        instruction.then_inc(self.sem, 1)
        self.engine.wait_ge(self.sem, self.base + self.n)


def mm3(pe, out, lhs, rhs, first, last):
    pe.matmul(out, lhs[0], rhs[0], start=first, stop=False)
    pe.matmul(out, lhs[0], rhs[1], start=False, stop=False)
    return pe.matmul(out, lhs[1], rhs[0], start=False, stop=last)


def layernorm_dve(v, x4, xn4, stats, mv, std, rstd, bn_done, stats_ready, std_ready, xn0_ready, n, link):
    for b in range(4):
        v.bn_stats(stats[:, b, :], x4[:, b, :]).then_inc(bn_done, 1)
    v.wait_ge(bn_done, 4 * n + 4)
    v.memset(rstd[:, :], 1.0)
    for b in range(4):
        ins = v.bn_aggr(mv[:, b, :], stats[:, b, :])
    ins.then_inc(stats_ready, 1)
    v.wait_ge(std_ready, n + 1)
    link(v.reciprocal(rstd[:, :], std[:, :]))
    for b in range(4):
        v.tensor_scalar(xn4[:, b, :], x4[:, b, :], mv[:, b, 0:1], rstd[:, b:b + 1], ALU.subtract,
                        ALU.mult).then_inc(xn0_ready, 1)


def time_mix(nc, io, x2):
    J = 6
    MIX = [None, 1, 3, 0, 2, 4]
    HALVES = 32
    with ExitStack() as ctx:
        def sb(n, s, d=F32):
            return ctx.enter_context(nc.sbuf_tensor("tm_" + n, s, d))

        def ps(n, s):
            return ctx.enter_context(nc.psum_tensor("tm_" + n, s, F32))

        def sem(n):
            return ctx.enter_context(nc.semaphore("tm_" + n))

        vec = sb("vec", [P, NV])
        ident = sb("ident", [P, P])
        head_sum = sb("head_sum", [P, P])
        head_mean = sb("head_mean", [P, P])
        head_mean4 = sb("head_mean4", [P, 32])
        unpack = sb("unpack", [P, EC, P])
        pick_k = sb("pick_k", [P, P + HS - 1])
        spread_v = sb("spread_v", [P, HS, P], FR)
        prev = sb("prev", [P, EC, B])
        eps = sb("eps", [P, 1])
        w_hi = sb("w_hi", [P, 5, EC, E], FR)
        w_lo = sb("w_lo", [P, 5, EC, E], FR)
        lora1 = (sb("lora1_hi", [P, EC, 160], FR), sb("lora1_lo", [P, EC, 160], FR))
        dec1 = (sb("dec1_hi", [P, EC, 64], FR), sb("dec1_lo", [P, EC, 64], FR))
        lora2 = sb("lora2", [P, E])
        lora2e = sb("lora2e", [LORA, E])
        dec2 = sb("dec2", [64, E])
        xq = sb("xq", [P, 4, E])
        stats = sb("stats", [P, 4, 6])
        mv = sb("mv", [P, 4, 2])
        std = sb("std", [P, 4])
        rstd = sb("rstd", [P, 4])
        s0 = sb("s0", [P, EC, HS, 4])
        xn = sb("xn", [P, EC, 4, L + 1])
        sx = sb("sx", [P, EC, QT])
        xf = sb("xf", [P, EC, QT])
        x_hi = sb("x_hi", [P, EC, QT], FR)
        x_lo = sb("x_lo", [P, EC, QT], FR)
        h5 = sb("h5", [P, QT])
        h5e = sb("h5e", [LORA, QT])
        dh = sb("dh", [64, QT])
        ew = sb("ew", [P, QT])
        wd = sb("wd", [P, EC, 4, L])
        rr = sb("rr", [P, EC, QT])
        kk = sb("kk", [P, EC, 4, L + 1])
        vv = sb("vv", [P, EC, 4, L + 1])
        gg = sb("gg", [P, EC, QT])
        pj = [ps("pj0", [P, QT]), ps("pj1", [P, QT])]
        mx = [ps("mx0", [P, QT]), ps("mx1", [P, QT])]
        vb = ps("vb", [P, 4, QT])

        const_in, small_in = sem("const_in"), sem("small_in")
        w_in, w_hi_ready, w_ready = [sem("w_in0"), sem("w_in1")], sem("w_hi_ready"), sem("w_ready")
        x_in, s0_in, res_in, x2_out, quad_done = sem("x_in"), sem("s0_in"), sem("res_in"), sem("x2_out"), sem("quad_done")
        bn_done = sem("bn_done")
        stats_ready, std_ready, xn0_ready = sem("stats_ready"), sem("std_ready"), sem("xn0_ready")
        xnT_full, xn_ready, prev_ready = sem("xnT_full"), sem("xn_ready"), sem("prev_ready")
        xf_ready, hi_ready, split_ready, x_used = sem("xf_ready"), sem("hi_ready"), sem("split_ready"), sem("x_used")
        pj_full, pj_free, mx_full, mx_free = sem("pj_full"), sem("pj_free"), sem("mx_full"), sem("mx_free")
        f_full, f_free = sem("f_full"), sem("f_free")
        h5_ready, dh_ready, ew_ready = sem("h5_ready"), sem("dh_ready"), sem("ew_ready")
        dve_step, v_hi_ready, v_split_ready = sem("dve_step"), sem("v_hi_ready"), sem("v_split_ready")
        ruk_ready, bonus_full, bonus_used = sem("ruk_ready"), sem("bonus_full"), sem("bonus_used")
        vb_full, s0_set, kv_ready, scanned = sem("vb_full"), sem("s0_set"), sem("kv_ready"), sem("scanned")
        rs_ready, rs_used, acc_full, att_ready = sem("rs_ready"), sem("rs_used"), sem("acc_full"), sem("att_ready")
        mean_full, cent_ready, sq_ready, var_full = sem("mean_full"), sem("cent_ready"), sem("sq_ready"), sem("var_full")
        gstd_ready, grstd_ready, unpacked = sem("gstd_ready"), sem("grstd_ready"), sem("unpacked")
        y_ready, y_hi_ready, y_split_ready, wo_full = sem("y_ready"), sem("y_hi_ready"), sem("y_split_ready"), sem("wo_full")
        ready = sem("ready")

        xn_flat = xn[:, :, :, :].rearrange("p a b c -> p (a b c)")[:, 0:4 * QT].rearrange("p (a b) -> p a b", a=4)
        state = [xn_flat[:, 0:2, :], xn_flat[:, 2:4, :]]
        prod = [sx[:, 0:2, :], sx[:, 2:4, :], xf[:, 0:2, :], xf[:, 2:4, :]]
        wo_bank = [mx[0], mx[1], pj[0], pj[1]]
        raw = [rr, gg]
        raw_spread = xf[:].rearrange("p a b -> p (a b)")
        raw_lora1 = sx[:, 0:2, :].rearrange("p a b -> p (a b)")[:, 0:640].rearrange("p (c m) -> p c m", c=EC)
        raw_dec1 = sx[:, 2, 0:256].rearrange("p (c m) -> p c m", c=EC)
        DVE_STEPS = 1 + 4 + 8 + 3
        CONSTS = (("vec", vec), ("ident", ident), ("head_sum", head_sum), ("head_mean", head_mean), ("head_mean4", head_mean4),
                  ("unpack", unpack), ("pick_k", pick_k), ("prev1", prev), ("dec2", dec2))
        N_CONST = 16 * (len(CONSTS) + 2)
        block = ctx.enter_context(nc.Block())

        def quad3(ap):
            return ap.rearrange("p (b t) -> p b t", b=4)

        def x_used_wait(engine, q, j, c):
            if c < EC - 1:
                engine.wait_ge(x_used, q * (J * 3) + (j * 3 + c + 1))
            elif j == 0:
                engine.wait_ge(pj_full, q * 7 + 2)
            elif j == 1:
                engine.wait_ge(pj_full, q * 7 + 3)
            else:
                engine.wait_ge(f_full, q * 16 + (j - 1) * 4)

        @block.sync
        def _(sp):
            for name, tile in CONSTS:
                sp.dma_start(tile[:], io[name]).then_inc(const_in, 16)
            sp.dma_start(lora2[:], io["lora2"][0:P, :]).then_inc(const_in, 16)
            sp.dma_start(lora2e[:], io["lora2"][P:160, :]).then_inc(const_in, 16)
            sp.dma_start(raw_spread, io["spread_v"]).then_inc(small_in, 16)
            sp.dma_start(raw_lora1, io["lora1"]).then_inc(small_in, 16)
            sp.dma_start(raw_dec1, io["dec1"]).then_inc(small_in, 16)
            sp.dma_start(xq[:], io["x"][0:4].rearrange("b t e -> t b e")).then_inc(x_in, 16)
            for j in range(5):
                if j >= 2:
                    sp.wait_ge(w_ready, 2 + j - 1)
                sp.dma_start(raw[j % 2][:], io["l0w"][j]).then_inc(w_in[j % 2], 16)

            def quad(q, last):
                if not isinstance(q, int) or q > 0:
                    sp.wait_ge(scanned, q * (2 * HALVES))
                sp.dma_start(s0[:], io["s0"][bass.ds(q, 1)].rearrange("a p c d b -> (a p) c d b")).then_inc(s0_in, 16)
                if not last:
                    sp.wait_ge(xn0_ready, q * 4 + 4)
                    sp.dma_start(xq[:], io["x"][bass.ds(q * 4 + 4, 4)].rearrange("b t e -> t b e")).then_inc(x_in, 16)
                sp.wait_ge(acc_full, q * 4 + 4)
                sp.dma_start(sx[:], io["x"][bass.ds(q * 4, 4)].rearrange("b t e -> t b e")).then_inc(res_in, 16)
                sp.wait_ge(quad_done, q + 1)
                sp.dma_start(x2[bass.ds(q * 4, 4)].rearrange("b t e -> t b e"), sx[:]).then_inc(x2_out, 16)

            quad(0, False)
            with sp.Fori(1, NQ - 1) as q:
                quad(q, False)
            quad(NQ - 1, True)
            sp.wait_ge(x2_out, NQ * 16 + 16)

        @block.gpsimd
        def _(gp):
            gp.memset(eps[:], EPS).then_inc(ready, 1)
            gp.memset(wd[:], 0.0).then_inc(ready, 1)
            gp.memset(kk[:, :, :, 0:1], 1.0).then_inc(ready, 1)
            gp.memset(vv[:, :, :, 0:1], 0.0).then_inc(ready, 1)
            gp.memset(h5e[0:1, 0:1], 0.0).then_inc(x2_out, 16)
            with gp.Fori(0, NQ) as q:
                for t in range(HALVES):
                    if t >= 4:
                        gp.wait_ge(rs_used, q * HALVES + (t - 3))
                    gp.wait_ge(scanned, q * (2 * HALVES) + 2 * (t + 1))
                    g = t // 8
                    gp.tensor_tensor(prod[t % 4], state[t % 2], rr[:, g:g + 1, :].broadcast_to([P, 2, QT]), ALU.mult).then_inc(rs_ready, 1)

        @block.scalar
        def _(act):
            act.wait_ge(small_in, 48)
            act.activation(spread_v[:].rearrange("p a b -> p (a b)"), raw_spread, ACT.Copy).then_inc(w_hi_ready, 1)
            act.activation(lora1[0][:], raw_lora1, ACT.Copy).then_inc(w_hi_ready, 1)
            act.activation(dec1[0][:], raw_dec1, ACT.Copy).then_inc(w_hi_ready, 1)
            for j in range(5):
                act.wait_ge(w_in[j % 2], 16 * (j // 2 + 1))
                act.activation(w_hi[:, j], raw[j % 2][:], ACT.Copy).then_inc(w_hi_ready, 1)
            act.wait_ge(ready, 4)
            act.wait_ge(const_in, N_CONST)
            act.wait_ge(w_ready, 7)
            with act.Fori(0, NQ) as q:
                def hi(j, c):
                    act.wait_ge(xf_ready, q * (4 * J) + (4 * j + c + 1))
                    if j > 0:
                        x_used_wait(act, q, j - 1, c)
                    act.activation(x_hi[:, c, :], xf[:, c, :], ACT.Copy).then_inc(hi_ready, 1)

                def decay(f):
                    act.wait_ge(pj_full, q * 7 + (3 + f + 1))
                    if f > 0:
                        act.wait_ge(ew_ready, q * 4 + f)
                    col = VEC["time_decay"] + f
                    act.activation(ew[:], pj[(3 + f) % 2][:], ACT.Exp, bias=vec[:, col:col + 1]).then_inc(pj_free, 1)
                    act.wait_ge(pj_free, q * 7 + (3 + f + 1))
                    act.activation(wd[:, f, :, 1:L], quad3(ew[:])[:, :, 0:L - 1], ACT.Exp, scale=-1.0).then_inc(ew_ready, 1)

                def evacuate(j):
                    for f in range(EC):
                        act.wait_ge(f_full, q * 16 + ((j - 2) * 4 + f + 1))
                        if j == 2:
                            ins = act.activation(rr[:, f, :], vb[:, f, :], ACT.Copy)
                        elif j == 3:
                            ins = act.activation(kk[:, f, :, 1:L + 1], quad3(vb[:, f, :]), ACT.Copy)
                        elif j == 4:
                            ins = act.activation(vv[:, f, :, 1:L + 1], quad3(vb[:, f, :]), ACT.Copy)
                        else:
                            ins = act.activation(gg[:, f, :], vb[:, f, :], ACT.Silu)
                        ins.then_inc(f_free, 1)

                act.wait_ge(stats_ready, q + 1)
                act.activation(std[:, :], mv[:, :, 1], ACT.Sqrt, bias=eps[:]).then_inc(std_ready, 1)
                for c in range(EC):
                    act.wait_ge(xnT_full, q * 4 + (c + 1))
                    act.activation(xn[:, c, :, 1:L + 1], quad3(vb[:, c, :]), ACT.Identity,
                                   bias=vec[:, VEC["ln1_b"] + c:VEC["ln1_b"] + c + 1],
                                   scale=vec[:, VEC["ln1_w"] + c:VEC["ln1_w"] + c + 1]).then_inc(xn_ready, 1)
                for c in range(EC):
                    hi(0, c)
                for k, tile in ((0, h5), (1, h5e)):
                    act.wait_ge(pj_full, q * 7 + (k + 1))
                    act.activation(tile[:], pj[k][0:tile.shape[0], :], ACT.Tanh).then_inc(pj_free, 1)
                for c in range(EC):
                    hi(1, c)
                for c in range(3):
                    hi(2, c)
                act.wait_ge(pj_full, q * 7 + 3)
                act.activation(dh[:], pj[0][0:64, :], ACT.Tanh).then_inc(pj_free, 1)
                hi(2, 3)
                for j in range(2, J):
                    for c in range(3):
                        if j + 1 < J:
                            hi(j + 1, c)
                        if j == 2:
                            decay(c)
                    evacuate(j)
                    if j + 1 < J:
                        hi(j + 1, 3)
                    if j == 2:
                        decay(3)
                act.wait_ge(f_free, q * 16 + 16)
                for c in range(EC):
                    act.activation(quad3(x_hi[:, c, :]), vv[:, c, :, 0:L], ACT.Copy).then_inc(v_hi_ready, 1)
                act.wait_ge(s0_in, q * 16 + 16)
                for t in range(HALVES):
                    act.wait_ge(vb_full, q * HALVES + (t + 1))
                    d = 2 * (t % 8)
                    act.activation(vb[:, 2 * (t % 2):2 * (t % 2) + 2, 0:QT:L], s0[:, t // 8, d:d + 2, :], ACT.Copy).then_inc(s0_set, 1)
                for c in range(EC):
                    act.wait_ge(cent_ready, q * 4 + (c + 1))
                    act.activation(quad3(xf[:, c, :]), vv[:, c, :, 1:L + 1], ACT.Square).then_inc(sq_ready, 1)
                act.wait_ge(var_full, q + 1)
                act.activation(ew[:], mx[0][:], ACT.Sqrt, bias=eps[:]).then_inc(gstd_ready, 1)
                for c in range(EC):
                    act.wait_ge(y_ready, q * 4 + (c + 1))
                    act.activation(x_hi[:, c, :], xf[:, c, :], ACT.Copy).then_inc(y_hi_ready, 1)

        @block.vector
        def _(v):
            v.wait_ge(w_hi_ready, 3)
            v.tensor_tensor(lora1[1][:], raw_lora1, lora1[0][:], ALU.subtract).then_inc(w_ready, 1)
            v.tensor_tensor(dec1[1][:], raw_dec1, dec1[0][:], ALU.subtract).then_inc(w_ready, 1)
            for j in range(5):
                v.wait_ge(w_hi_ready, 3 + j + 1)
                v.tensor_tensor(w_lo[:, j], raw[j % 2][:], w_hi[:, j], ALU.subtract).then_inc(w_ready, 1)
            v.wait_ge(ready, 4)
            v.wait_ge(const_in, N_CONST)
            v.wait_ge(w_ready, 7)
            with v.Fori(0, NQ) as q:
                steps = Steps(v, dve_step, q * DVE_STEPS)
                link = steps.link
                v.wait_ge(x_in, q * 16 + 16)
                layernorm_dve(v, xq, xf, stats, mv, std, rstd, bn_done, stats_ready, std_ready, xn0_ready, q, link)
                v.tensor_copy(xn[:, :, :, 0], prev[:, :, bass.ds(q * 4, 4)]).then_inc(prev_ready, 1)
                v.wait_ge(prev_ready, q + 1)
                v.wait_ge(x2_out, q * 16 + 16)
                for c in range(EC):
                    v.wait_ge(xn_ready, q * 4 + (c + 1))
                    link(v.tensor_tensor(quad3(sx[:, c, :]), xn[:, c, :, 0:L], xn[:, c, :, 1:L + 1], ALU.subtract))
                    if c == 0:
                        v.wait_ge(xnT_full, q * 4 + 4)
                    m = VEC["maa_x"] + c
                    v.scalar_tensor_tensor(out=quad3(xf[:, c, :]), in0=quad3(sx[:, c, :]), scalar=vec[:, m:m + 1],
                                           in1=xn[:, c, :, 1:L + 1], op0=ALU.mult, op1=ALU.add).then_inc(xf_ready, 1)

                def lo(j, c):
                    v.wait_ge(hi_ready, q * (4 * J) + (4 * j + c + 1))
                    v.tensor_tensor(x_lo[:, c, :], xf[:, c, :], x_hi[:, c, :], ALU.subtract).then_inc(split_ready, 1)

                for c in range(EC):
                    lo(0, c)
                for j in range(1, J):
                    for c in range(EC):
                        s = VEC["stack%d" % MIX[j]] + c
                        n = (j - 1) * 4 + c
                        v.wait_ge(split_ready, q * (4 * J) + (4 * (j - 1) + c + 1))
                        v.wait_ge(mx_full, q * 20 + (n + 1))
                        v.scalar_tensor_tensor(out=xf[:, c, :], in0=mx[n % 2][:], scalar=vec[:, s:s + 1],
                                               in1=sx[:, c, :], op0=ALU.add, op1=ALU.mult).then_inc(mx_free, 1)
                        if c > 0:
                            lo(j, c - 1)
                        v.wait_ge(mx_free, q * 20 + (n + 1))
                        v.tensor_tensor(quad3(xf[:, c, :]), quad3(xf[:, c, :]), xn[:, c, :, 1:L + 1], ALU.add).then_inc(xf_ready, 1)
                    lo(j, EC - 1)
                v.wait_ge(f_free, q * 16 + 8)
                for c in range(EC):
                    u = VEC["faaaa"] + c
                    v.scalar_tensor_tensor(out=quad3(sx[:, c, :]), in0=quad3(rr[:, c, :]), scalar=vec[:, u:u + 1],
                                           in1=kk[:, c, :, 1:L + 1], op0=ALU.mult, op1=ALU.mult).then_inc(ruk_ready, 1)
                for c in range(EC):
                    v.wait_ge(v_hi_ready, q * 4 + (c + 1))
                    v.tensor_tensor(quad3(x_lo[:, c, :]), vv[:, c, :, 0:L], quad3(x_hi[:, c, :]), ALU.subtract).then_inc(v_split_ready, 1)
                v.wait_ge(v_split_ready, q * 4 + 4)
                for c in range(EC):
                    v.wait_ge(bonus_full, q * 4 + (c + 1))
                    v.tensor_tensor(vv[:, c, :, 1:L + 1], quad3(pj[c % 2][:]), vv[:, c, :, 1:L + 1], ALU.mult).then_inc(bonus_used, 1)
                v.wait_ge(bonus_used, q * 4 + 4)

                def add_bonus(g):
                    v.wait_ge(acc_full, q * 4 + (g + 1))
                    v.tensor_tensor(vv[:, g, :, 1:L + 1], quad3(mx[g % 2][:]), vv[:, g, :, 1:L + 1], ALU.add).then_inc(att_ready, 1)

                for t in range(HALVES):
                    g = t // 8
                    pair = vb[:, 2 * (t % 2):2 * (t % 2) + 2, :]
                    pair4 = pair.rearrange("p d (b t) -> p d b t", b=4)
                    v.wait_ge(s0_set, q * HALVES + (t + 1))
                    v.tensor_tensor(pair4, pair4, kk[:, g:g + 1, :, 0:L].broadcast_to([P, 2, 4, L]), ALU.mult).then_inc(kv_ready, 1)
                    if t >= 2:
                        v.wait_ge(rs_ready, q * HALVES + (t - 1))
                    v.wait_ge(kv_ready, q * HALVES + (t + 1))
                    for d in range(2):
                        v.tensor_tensor_scan(state[t % 2][:, d, :], wd[:, g].rearrange("p b t -> p (b t)"), pair[:, d, :], 0.0,
                                             ALU.mult, ALU.add).then_inc(scanned, 1)
                    if t % 8 == 2 and t > 8:
                        add_bonus(g - 1)
                add_bonus(3)
                v.wait_ge(att_ready, q * 4 + 4)
                for c in range(EC):
                    v.wait_ge(mean_full, q * 4 + (c + 1))
                    v.tensor_tensor(vv[:, c, :, 1:L + 1], vv[:, c, :, 1:L + 1], quad3(pj[c % 2][:]), ALU.subtract).then_inc(cent_ready, 1)
                v.wait_ge(gstd_ready, q + 1)
                v.reciprocal(ew[:], ew[:]).then_inc(grstd_ready, 1)
                for c in range(EC):
                    v.wait_ge(unpacked, q * 4 + (c + 1))
                    link(v.tensor_tensor(quad3(xf[:, c, :]), vv[:, c, :, 1:L + 1], quad3(vb[:, c, :]), ALU.mult))
                    w, b_ = VEC["gn_w"] + c, VEC["gn_b"] + c
                    link(v.tensor_scalar(xf[:, c, :], xf[:, c, :], vec[:, w:w + 1], vec[:, b_:b_ + 1], ALU.mult, ALU.add))
                    v.tensor_tensor(xf[:, c, :], xf[:, c, :], gg[:, c, :], ALU.mult).then_inc(y_ready, 1)
                    if c > 0:
                        v.wait_ge(y_hi_ready, q * 4 + c)
                        v.tensor_tensor(x_lo[:, c - 1, :], xf[:, c - 1, :], x_hi[:, c - 1, :], ALU.subtract).then_inc(y_split_ready, 1)
                v.wait_ge(y_hi_ready, q * 4 + EC)
                v.tensor_tensor(x_lo[:, EC - 1, :], xf[:, EC - 1, :], x_hi[:, EC - 1, :], ALU.subtract).then_inc(y_split_ready, 1)
                v.wait_ge(res_in, q * 16 + 16)
                for b in range(4):
                    v.wait_ge(wo_full, q * 4 + (b + 1))
                    ins = v.tensor_tensor(sx[:, b, :], sx[:, b, :], wo_bank[b][:], ALU.add)
                    if b < 3:
                        link(ins)
                ins.then_inc(quad_done, 1)
                assert steps.n == DVE_STEPS

        @block.tensor
        def _(pe):
            pe.wait_ge(const_in, N_CONST)
            pe.wait_ge(w_ready, 7)
            with pe.Fori(0, NQ) as q:
                def mix(j, c):
                    if j >= J:
                        return
                    m, n = MIX[j], (j - 1) * 4 + c
                    if n >= 2:
                        pe.wait_ge(mx_free, q * 20 + (n - 1))
                    if m < 4:
                        lhs, rhs = lora2[32 * m:32 * m + 32, c * P:(c + 1) * P], h5[32 * m:32 * m + 32, :]
                    else:
                        lhs, rhs = lora2e[:, c * P:(c + 1) * P], h5e[:]
                    pe.matmul(mx[n % 2][:], lhs, rhs, start=True, stop=True).then_inc(mx_full, 1)

                def stage(j, c):
                    pe.wait_ge(split_ready, q * (4 * J) + (4 * j + c + 1))
                    x = (x_hi[:, c, :], x_lo[:, c, :])
                    first, last = c == 0, c == EC - 1
                    if j == 0:
                        for k, rows in ((0, P), (1, LORA)):
                            ins = mm3(pe, pj[k][0:rows, :], [t[:, c, k * P:k * P + rows] for t in lora1], x, first, last)
                            if last:
                                ins.then_inc(pj_full, 1)
                    elif j == 1:
                        if first:
                            pe.wait_ge(pj_free, q * 7 + 1)
                        ins = mm3(pe, pj[0][0:64, :], [t[:, c, :] for t in dec1], x, first, last)
                        if last:
                            ins.then_inc(pj_full, 1)
                    else:
                        for f in range(EC):
                            if first and j > 2:
                                pe.wait_ge(f_free, q * 16 + ((j - 3) * 4 + f + 1))
                            ins = mm3(pe, vb[:, f, :], [t[:, j - 2, c, f * P:(f + 1) * P] for t in (w_hi, w_lo)], x, first, last)
                            if last:
                                ins.then_inc(f_full, 1)
                    if not last:
                        ins.then_inc(x_used, 1)

                def decay(f):
                    pe.wait_ge(pj_free, q * 7 + (3 if f == 0 else 3 + f - 1))
                    pe.matmul(pj[(3 + f) % 2][:], dec2[:, f * P:(f + 1) * P], dh[:], start=True, stop=True).then_inc(pj_full, 1)

                for b in range(4):
                    pe.wait_ge(xn0_ready, q * 4 + (b + 1))
                    for c in range(EC):
                        ins = pe.transpose(vb[:, c, b * P:(b + 1) * P], xf[:, b, c * P:(c + 1) * P], ident[:])
                        if b == 3:
                            ins.then_inc(xnT_full, 1)
                for c in range(EC):
                    stage(0, c)
                pe.wait_ge(pj_free, q * 7 + 1)
                for c in range(EC):
                    mix(1, c)
                for j in range(1, J):
                    if j + 1 == J - 0:
                        pass
                    if MIX[j + 1 if j + 1 < J else j] == 4:
                        pe.wait_ge(pj_free, q * 7 + 2)
                    mix(j + 1, 0)
                    mix(j + 1, 1)
                    stage(j, 0)
                    if j == 2:
                        decay(0)
                    mix(j + 1, 2)
                    stage(j, 1)
                    if j == 2:
                        decay(1)
                    mix(j + 1, 3)
                    for c in (2, 3):
                        stage(j, c)
                        if j == 2:
                            decay(c)
                for c in range(EC):
                    pe.wait_ge(ruk_ready, q * 4 + (c + 1))
                    if c < 2:
                        pe.wait_ge(pj_free, q * 7 + 7)
                    else:
                        pe.wait_ge(bonus_used, q * 4 + (c - 1))
                    pe.matmul(pj[c % 2][:], head_sum[:], sx[:, c, :], start=True, stop=True).then_inc(bonus_full, 1)

                def spread(t):
                    if t >= HALVES:
                        return
                    g = t // 8
                    pe.wait_ge(v_split_ready, q * 4 + (g + 1))
                    if t >= 2:
                        pe.wait_ge(scanned, q * (2 * HALVES) + 2 * (t - 1))
                    for e in range(2):
                        d = 2 * (t % 8) + e
                        pe.matmul(vb[:, 2 * (t % 2) + e, :], spread_v[:, d, :], x_hi[:, g, :], start=True, stop=False)
                        ins = pe.matmul(vb[:, 2 * (t % 2) + e, :], spread_v[:, d, :], x_lo[:, g, :], start=False, stop=True)
                    ins.then_inc(vb_full, 1)

                def accumulate(t):
                    g = t // 8
                    if t % 8 == 0 and g >= 2:
                        pe.wait_ge(att_ready, q * 4 + (g - 1))
                    pe.wait_ge(rs_ready, q * HALVES + (t + 1))
                    for e in range(2):
                        d = 2 * (t % 8) + e
                        ins = pe.matmul(mx[g % 2][:], pick_k[:, HS - 1 - d:HS - 1 - d + P], prod[t % 4][:, e, :], start=d == 0, stop=d == 15)
                    ins.then_inc(rs_used, 1)
                    if t % 8 == 7:
                        pe.wait_ge(rs_used, q * HALVES + (t + 1))
                        pe.nop().then_inc(acc_full, 1)

                pe.wait_ge(f_free, q * 16 + 16)
                spread(0)
                spread(1)
                for t in range(HALVES):
                    spread(t + 2)
                    if t >= 1:
                        accumulate(t - 1)
                accumulate(HALVES - 1)
                for c in range(EC):
                    pe.wait_ge(att_ready, q * 4 + (c + 1))
                    if c >= 2:
                        pe.wait_ge(cent_ready, q * 4 + (c - 1))
                    pe.matmul(pj[c % 2][:], head_mean[:], vv[:, c, :, 1:L + 1], start=True, stop=True).then_inc(mean_full, 1)
                for c in range(EC):
                    pe.wait_ge(sq_ready, q * 4 + (c + 1))
                    ins = pe.matmul(mx[0][32 * c:32 * c + 32, :], head_mean4[:], xf[:, c, :], start=True, stop=True)
                ins.then_inc(var_full, 1)
                pe.wait_ge(grstd_ready, q + 1)
                for c in range(EC):
                    pe.matmul(vb[:, c, :], unpack[:, c, :], ew[:], start=True, stop=True).then_inc(unpacked, 1)
                for c in range(EC):
                    pe.wait_ge(y_split_ready, q * 4 + (c + 1))
                    for b in range(4):
                        ins = mm3(pe, wo_bank[b][:], (x_hi[:, c, b * P:(b + 1) * P], x_lo[:, c, b * P:(b + 1) * P]),
                                  (w_hi[:, 4, c, :], w_lo[:, 4, c, :]), c == 0, c == EC - 1)
                        if c == EC - 1:
                            ins.then_inc(wo_full, 1)


def channel_mix(nc, io, x2, x3):
    with ExitStack() as ctx:
        def sb(n, s, d=F32):
            return ctx.enter_context(nc.sbuf_tensor("cm_" + n, s, d))

        def ps(n, s):
            return ctx.enter_context(nc.psum_tensor("cm_" + n, s, F32))

        def sem(n):
            return ctx.enter_context(nc.semaphore("cm_" + n))

        vec = sb("vec", [P, NV])
        ident = sb("ident", [P, P])
        prev = sb("prev", [P, EC, B])
        eps = sb("eps", [P, 1])
        w_hi = sb("w_hi", [P, 3, EC, E], FR)
        w_lo = sb("w_lo", [P, 3, EC, E], FR)
        xq = sb("xq", [P, 4, E])
        stats = sb("stats", [P, 4, 6])
        mv = sb("mv", [P, 4, 2])
        std = sb("std", [P, 4])
        rstd = sb("rstd", [P, 4])
        xn = sb("xn", [P, EC, 4, L + 1])
        sx = sb("sx", [P, EC, QT])
        xf = [sb("xk", [P, EC, QT]), sb("xr", [P, EC, QT])]
        x_hi = [sb("xk_hi", [P, EC, QT], FR), sb("xr_hi", [P, EC, QT], FR)]
        x_lo = [sb("xk_lo", [P, EC, QT], FR), sb("xr_lo", [P, EC, QT], FR)]
        gate = sb("gate", [P, 4, E])
        tr = ps("tr", [P, 4, QT])
        mm = ps("mm", [P, 4, QT])

        const_in, w_in, w_hi_ready, w_ready = sem("const_in"), [sem("w_in%d" % j) for j in range(3)], sem("w_hi_ready"), sem("w_ready")
        x_in, x3_out, quad_done, ready = sem("x_in"), sem("x3_out"), sem("quad_done"), sem("ready")
        bn_done, stats_ready, std_ready, xn0_ready = sem("bn_done"), sem("stats_ready"), sem("std_ready"), sem("xn0_ready")
        xnT_full, xn_ready, prev_ready = sem("xnT_full"), sem("xn_ready"), sem("prev_ready")
        xf_ready, hi_ready, split_ready = sem("xf_ready"), sem("hi_ready"), sem("split_ready")
        k_full, r_full, y_full = sem("k_full"), sem("r_full"), sem("y_full")
        k2_ready, k2_hi_ready, k2_split_ready = sem("k2_ready"), sem("k2_hi_ready"), sem("k2_split_ready")
        gate_ready, gated, dve_step = sem("gate_ready"), sem("gated"), sem("dve_step")
        DVE_STEPS = 1 + 4 + 4 + 3
        block = ctx.enter_context(nc.Block())

        @block.sync
        def _(sp):
            raw = [gate, xf[0], xf[1]]
            for tile, name in ((vec, "vec"), (ident, "ident"), (prev, "prev0")):
                sp.dma_start(tile[:], io[name]).then_inc(const_in, 16)
            for j in range(3):
                sp.dma_start(raw[j][:], io["l0w"][5 + j]).then_inc(w_in[j], 16)
            with sp.Fori(0, NQ) as q:
                sp.wait_ge(quad_done, q + 1)
                sp.wait_ge(x3_out, q * 16 + 16)
                sp.dma_start(xq[:], x2[bass.ds(q * 4, 4)].rearrange("b t e -> t b e")).then_inc(x_in, 16)
                sp.wait_ge(quad_done, q + 2)
                sp.dma_start(x3[bass.ds(q * 4, 4)].rearrange("b t e -> t b e"), xq[:]).then_inc(x3_out, 16)
            sp.wait_ge(x3_out, NQ * 16 + 16)

        @block.gpsimd
        def _(gp):
            gp.memset(eps[:], EPS).then_inc(ready, 1)
            gp.memset(sx[0:1, 0, 0:1], 0.0).then_inc(x3_out, 16)

        @block.scalar
        def _(act):
            raw = [gate, xf[0], xf[1]]
            for j in range(3):
                act.wait_ge(w_in[j], 16)
                act.activation(w_hi[:, j], raw[j][:], ACT.Copy).then_inc(w_hi_ready, 1)
            act.wait_ge(const_in, 48)
            act.wait_ge(ready, 1)
            act.wait_ge(w_ready, 3)
            with act.Fori(0, NQ) as q:
                act.wait_ge(stats_ready, q + 1)
                act.activation(std[:, :], mv[:, :, 1], ACT.Sqrt, bias=eps[:]).then_inc(std_ready, 1)
                act.wait_ge(xnT_full, q + 1)
                for c in range(EC):
                    act.activation(xn[:, c, :, 1:L + 1], tr[:, c, :].rearrange("p (b t) -> p b t", b=4), ACT.Identity,
                                   bias=vec[:, VEC["ln2_b"] + c:VEC["ln2_b"] + c + 1],
                                   scale=vec[:, VEC["ln2_w"] + c:VEC["ln2_w"] + c + 1]).then_inc(xn_ready, 1)
                for j in range(2):
                    for c in range(EC):
                        act.wait_ge(xf_ready, q * 8 + 4 * j + c + 1)
                        act.activation(x_hi[j][:, c, :], xf[j][:, c, :], ACT.Copy).then_inc(hi_ready, 1)
                for c in range(EC):
                    act.wait_ge(k2_ready, q * 4 + c + 1)
                    act.activation(x_hi[0][:, c, :], xf[0][:, c, :], ACT.Copy).then_inc(k2_hi_ready, 1)
                for b in range(4):
                    act.wait_ge(r_full, q * 4 + b + 1)
                    act.activation(gate[:, b, :], tr[:, b, :], ACT.Sigmoid).then_inc(gate_ready, 1)

        @block.vector
        def _(v):
            raw = [gate, xf[0], xf[1]]
            v.memset(std[:], 1.0).then_inc(quad_done, 1)
            for j in range(3):
                v.wait_ge(w_hi_ready, j + 1)
                v.tensor_tensor(w_lo[:, j], raw[j][:], w_hi[:, j], ALU.subtract).then_inc(w_ready, 1)
            v.wait_ge(const_in, 48)
            v.wait_ge(w_ready, 3)
            with v.Fori(0, NQ) as q:
                steps = Steps(v, dve_step, q * DVE_STEPS)
                link = steps.link
                v.wait_ge(x_in, q * 16 + 16)
                layernorm_dve(v, xq, xf[0], stats, mv, std, rstd, bn_done, stats_ready, std_ready, xn0_ready, q, link)
                v.tensor_copy(xn[:, :, :, 0], prev[:, :, bass.ds(q * 4, 4)]).then_inc(prev_ready, 1)
                v.wait_ge(prev_ready, q + 1)
                for c in range(EC):
                    v.wait_ge(xn_ready, q * 4 + c + 1)
                    link(v.tensor_tensor(sx[:, c, :].rearrange("p (b t) -> p b t", b=4), xn[:, c, :, 0:L],
                                         xn[:, c, :, 1:L + 1], ALU.subtract))
                for j, name in ((0, "ffn_maa_k"), (1, "ffn_maa_r")):
                    for c in range(EC):
                        if j == 0 and c == 0:
                            v.wait_ge(xnT_full, q + 1)
                        m = VEC[name] + c
                        v.scalar_tensor_tensor(out=xf[j][:, c, :].rearrange("p (b t) -> p b t", b=4),
                                               in0=sx[:, c, :].rearrange("p (b t) -> p b t", b=4), scalar=vec[:, m:m + 1],
                                               in1=xn[:, c, :, 1:L + 1], op0=ALU.mult, op1=ALU.add).then_inc(xf_ready, 1)
                    for c in range(EC):
                        v.wait_ge(hi_ready, q * 8 + 4 * j + c + 1)
                        v.tensor_tensor(x_lo[j][:, c, :], xf[j][:, c, :], x_hi[j][:, c, :], ALU.subtract).then_inc(split_ready, 1)
                v.wait_ge(k_full, q * 4 + 4)
                for c in range(EC):
                    link(v.tensor_copy(sx[:, c, :], mm[:, c, :]))
                    v.scalar_tensor_tensor(out=xf[0][:, c, :], in0=mm[:, c, :], scalar=0.0, in1=sx[:, c, :],
                                           op0=ALU.max, op1=ALU.mult).then_inc(k2_ready, 1)
                for c in range(EC):
                    v.wait_ge(k2_hi_ready, q * 4 + c + 1)
                    v.tensor_tensor(x_lo[0][:, c, :], xf[0][:, c, :], x_hi[0][:, c, :], ALU.subtract).then_inc(k2_split_ready, 1)
                for b in range(4):
                    v.wait_ge(gate_ready, q * 4 + b + 1)
                    v.wait_ge(y_full, q * 4 + b + 1)
                    v.tensor_tensor(sx[:, b, :], gate[:, b, :], mm[:, b, :], ALU.mult).then_inc(gated, 1)
                    v.wait_ge(gated, q * 4 + b + 1)
                    ins = v.tensor_tensor(xq[:, b, :], xq[:, b, :], sx[:, b, :], ALU.add)
                    if b < 3:
                        link(ins)
                ins.then_inc(quad_done, 1)
                assert steps.n == DVE_STEPS

        @block.tensor
        def _(pe):
            pe.wait_ge(const_in, 48)
            pe.wait_ge(w_ready, 3)
            with pe.Fori(0, NQ) as q:
                for b in range(4):
                    pe.wait_ge(xn0_ready, q * 4 + b + 1)
                    for c in range(EC):
                        ins = pe.transpose(tr[:, c, b * P:(b + 1) * P], xf[0][:, b, c * P:(c + 1) * P], ident[:])
                ins.then_inc(xnT_full, 1)
                for f in range(EC):
                    for c in range(EC):
                        pe.wait_ge(split_ready, q * 8 + c + 1)
                        ins = mm3(pe, mm[:, f, :], (w_hi[:, 0, c, f * P:(f + 1) * P], w_lo[:, 0, c, f * P:(f + 1) * P]),
                                  (x_hi[0][:, c, :], x_lo[0][:, c, :]), c == 0, c == EC - 1)
                    ins.then_inc(k_full, 1)
                pe.wait_ge(xn_ready, q * 4 + 4)
                for b in range(4):
                    for c in range(EC):
                        pe.wait_ge(split_ready, q * 8 + 4 + c + 1)
                        ins = mm3(pe, tr[:, b, :], (x_hi[1][:, c, b * P:(b + 1) * P], x_lo[1][:, c, b * P:(b + 1) * P]),
                                  (w_hi[:, 1, c, :], w_lo[:, 1, c, :]), c == 0, c == EC - 1)
                    ins.then_inc(r_full, 1)
                for b in range(4):
                    for c in range(EC):
                        pe.wait_ge(k2_split_ready, q * 4 + (c + 1 if b == 0 else 4))
                        ins = mm3(pe, mm[:, b, :], (x_hi[0][:, c, b * P:(b + 1) * P], x_lo[0][:, c, b * P:(b + 1) * P]),
                                  (w_hi[:, 2, c, :], w_lo[:, 2, c, :]), c == 0, c == EC - 1)
                    ins.then_inc(y_full, 1)


def cross_attend(nc, io, x3, out):
    HT = 8
    G = NH // 2
    RING = 2
    STAGE = 6 * 16 + 4 * 16 + HT
    HALF = 2 * STAGE + 4 * 16
    KW = L + 2
    BANK_TR, BANK_SC, BANK_PV, BANK_BV = 2, 4, 6, 7
    HV = {"bq": 0, "bk": 1, "bv": 2, "bias_k": 3, "bias_v": 4}
    with ExitStack() as ctx:
        def sb(n, s, d=F32):
            return ctx.enter_context(nc.sbuf_tensor("ca_" + n, s, d))

        def two(n, s):
            return (sb(n + "_hi", s, FR), sb(n + "_lo", s, FR))

        def sem(n):
            return ctx.enter_context(nc.semaphore("ca_" + n))

        vec = sb("vec", [P, NV])
        hv = sb("hv", [P, 11 * NH])
        ident = sb("ident", [P, P])
        eps = sb("eps", [P, 1])
        bo = sb("bo", [P, 3, E])
        bias_k = two("bias_k", [P, 2 * NH])
        c2 = two("ctx", [P, EC, HT * L])
        h2 = two("h", [P, EC, HT * L])
        xres = sb("xres", [P, HT, E])
        lt = sb("lt", [P, 4, E])
        lh = sb("lh", [P, EC, QT])
        stats = sb("stats", [P, 4, 6])
        mv = sb("mv", [P, 4, 2])
        std = sb("std", [P, 4])
        rstd = sb("rstd", [P, 4])
        sq, sk, sv = sb("sq", [P, EC, 256]), sb("sk", [P, EC, 256]), sb("sv", [P, EC, 256])
        so = sb("so", [P, 2, E])
        wq, wk, wv = two("wq", [P, EC, 256]), two("wk", [P, EC, 256]), two("wv", [P, EC, 256])
        wo = two("wo", [P, 2, E])
        qT = [two("q%d" % i, [P, QT]) for i in range(2)]
        kT = [two("k%d" % i, [P, 4, KW]) for i in range(2)]
        vT = two("v", [P, 4, 256])
        pr = [sb("pr%d" % i, [P, 4, KW]) for i in range(2)]
        pT = [two("pt%d" % i, [P, QT]) for i in range(2)]
        cT = [two("ct%d" % i, [P, QT]) for i in range(2)]
        mxs = [sb("mx%d" % i, [P, 4]) for i in range(2)]
        nbs = [sb("nb%d" % i, [P, 4]) for i in range(2)]
        sms = [sb("sm%d" % i, [P, 4]) for i in range(2)]
        rss = [sb("rs%d" % i, [P, 4]) for i in range(2)]
        pb = sb("pb", [P, HT, NH])
        dbias = sb("dbias", [P, NH, NH])
        db = two("db", [P, 2, NH])
        bvs = sb("bvs", [NH, E])
        pbT = sb("pbT", [NH, HT * L])
        ps = ctx.enter_context(nc.psum_tensor("ca_ps", [P, 8, QT], F32))

        const_in, ready, bk_hi, bk_split = sem("const_in"), sem("ready"), sem("bk_hi"), sem("bk_split")
        x_in, c_in, c_hi, c_split, out_done = sem("x_in"), [sem("c_in0"), sem("c_in1")], sem("c_hi"), sem("c_split"), sem("out_done")
        wq_in, wk_in, wv_in, wo_in = sem("wq_in"), sem("wk_in"), sem("wv_in"), sem("wo_in")
        wq_hi, wk_hi, wv_hi, wo_hi = sem("wq_hi"), sem("wk_hi"), sem("wv_hi"), sem("wo_hi")
        wq_split, wk_split, wv_split, wo_split = sem("wq_split"), sem("wk_split"), sem("wv_split"), sem("wo_split")
        bn_done, stats_ready, std_ready, xn0_ready = sem("bn_done"), sem("stats_ready"), sem("std_ready"), sem("xn0_ready")
        ln_step, lnT_full, lh_ready, h_hi, h_split = sem("ln_step"), sem("lnT_full"), sem("lh_ready"), sem("h_hi"), sem("h_split")
        bo_added, dbias_ready = sem("bo_added"), sem("dbias_ready")
        ring_full, evacuated, p_hi = sem("ring_full"), sem("evacuated"), sem("p_hi")
        sc_full, mx_done, max_done, exp_done = sem("sc_full"), sem("mx_done"), sem("max_done"), sem("exp_done")
        rs_done, norm_done = sem("rs_done"), sem("norm_done")
        tr_full, pt_hi, pt_split = sem("tr_full"), sem("pt_hi"), sem("pt_split")
        pv_full, ct_hi, ct_split = sem("pv_full"), sem("ct_hi"), sem("ct_split")
        act_waited = sem("act_waited")
        db_hi, db_ready, pbT_full, pbT_ready = sem("db_hi"), sem("db_ready"), sem("pbT_full"), sem("pbT_ready")
        fc1_full, gelu_ready, u_hi, u_split = sem("fc1_full"), sem("gelu_ready"), sem("u_hi"), sem("u_split")

        class Slot:

            def __init__(self, h, st, g, quad, proj=True, attn=True):
                self.h, self.st, self.g, self.quad, self.proj, self.attn = h, st, g, quad, proj, attn
                s = g * 2 + quad
                self.s = s
                self.n = h * 32 + (st * 16 + s)
                self.gu = g if quad else g - 1
                self.qu = 1 - quad
                self.ring = h * HALF + (st * STAGE + s * 10 - (4 if attn else 0))
                self.projected = self.ring - (0 if isinstance(g, int) and s <= 1 else 4)
                if not proj:
                    self.out0 = self.ring
                else:
                    self.out0 = self.ring + 6
                self.gq = h * 24 + (st * 8 + g)
                self.gk = h * 16 + (st * 8 + g)

        def attention_slots(engine, h, st, slot):
            slot(Slot(h, st, 0, 0, attn=False))
            slot(Slot(h, st, 0, 1))
            with engine.Fori(1, G) as g:
                slot(Slot(h, st, g, 0))
                slot(Slot(h, st, g, 1))
            slot(Slot(h, st, G, 0, proj=False))

        class MlpSlot:
            def __init__(self, h, g, quad, proj=True, outp=True):
                self.h, self.g, self.quad, self.proj, self.outp = h, g, quad, proj, outp
                s = g * 2 + quad
                self.n = h * 16 + s
                self.out0 = h * HALF + (2 * STAGE + s * 4 - 4)
                self.gq = h * 24 + (16 + g)
                self.u = pT if quad == 0 else cT
                self.u_last = cT if quad == 0 else pT

        def mlp_slots(engine, h, slot):
            slot(MlpSlot(h, 0, 0, outp=False))
            slot(MlpSlot(h, 0, 1))
            with engine.Fori(1, G) as g:
                slot(MlpSlot(h, g, 0))
                slot(MlpSlot(h, g, 1))
            slot(MlpSlot(h, G, 0, proj=False))

        def wait_apart(act):
            act.sem_inc(act_waited, 1)

        def head_col(st, kind, g, hd):
            return hv[:, bass.ds(g * 2 + ((st * 5 + HV[kind]) * NH + hd), 1)]

        block = ctx.enter_context(nc.Block())

        @block.sync
        def _(sp):
            for tile, name in ((vec, "vec"), (ident, "ident"), (hv, "head_vec"), (bo, "bo")):
                sp.dma_start(tile[:], io[name]).then_inc(const_in, 16)
            sp.dma_start(sq[:], io["wq"][0]).then_inc(wq_in, 16)
            sp.dma_start(sk[:], io["wk"][0]).then_inc(wk_in, 16)
            with sp.Fori(0, 2) as h:
                sp.wait_ge(out_done, h * 16 + 16)
                for quad, tile in ((0, lt), (1, lh)):
                    sp.dma_start(tile[:], io["ctxT"][:, :, bass.ds(h * (HT * L) + quad * QT, QT)]).then_inc(c_in[quad], 16)
                sp.dma_start(xres[:], x3[bass.ds(h * HT, HT)].rearrange("b t e -> t b e")).then_inc(x_in, 16)
                for st in range(2):
                    with sp.Fori(0, G) as g:
                        gq, gk = h * 24 + (st * 8 + g), h * 16 + (st * 8 + g)
                        sp.wait_ge(wv_split, gk + 1)
                        sp.dma_start(sv[:], io["wv"][bass.ds(g + st * 8, 1)].rearrange("a p c m -> (a p) c m")).then_inc(wv_in, 16)
                        sp.wait_ge(wo_split, gq + 1)
                        sp.dma_start(so[:], io["wo"][bass.ds(g + st * 8, 1)].rearrange("a p c m -> (a p) c m")).then_inc(wo_in, 16)
                        sp.wait_ge(wq_split, (gq + 1) * 2)
                        sp.dma_start(sq[:], io["wq"][bass.ds(g + (st * 8 + 1), 1)].rearrange("a p c m -> (a p) c m")).then_inc(wq_in, 16)
                        sp.wait_ge(wk_split, gk + 1)
                        sp.dma_start(sk[:], io["wk"][bass.ds(g + (st * 8 + 1), 1)].rearrange("a p c m -> (a p) c m")).then_inc(wk_in, 16)
                with sp.Fori(0, G) as g:
                    gq = h * 24 + (16 + g)
                    sp.wait_ge(wo_split, gq + 1)
                    sp.dma_start(so[:], io["wo"][bass.ds(g + 16, 1)].rearrange("a p c m -> (a p) c m")).then_inc(wo_in, 16)
                    sp.wait_ge(wq_split, (gq + 1) * 2)
                    sp.dma_start(sq[:], io["wq"][bass.ds(g + 17, 1)].rearrange("a p c m -> (a p) c m")).then_inc(wq_in, 16)
                sp.wait_ge(evacuated, h * HALF + (HALF + RING))
                sp.dma_start(out[bass.ds(h * HT, HT)].rearrange("b t e -> t b e"), xres[:]).then_inc(out_done, 16)
            sp.wait_ge(out_done, 3 * 16)

        @block.gpsimd
        def _(gp):
            gp.memset(eps[:], EPS).then_inc(ready, 1)
            gp.memset(dbias[:], 0.0).then_inc(ready, 1)
            for hd in range(2):
                gp.memset(kT[hd][0][:, :, L + 1:KW].bitcast(F32), 0.0).then_inc(ready, 1)
                gp.memset(kT[hd][1][:, :, L + 1:KW].bitcast(F32), 0.0).then_inc(ready, 1)
            for s, n in ((out_done, 16), (wv_split, 1), (wo_split, 1), (evacuated, RING), (exp_done, 1),
                         (ct_split, 1), (tr_full, 2)):
                gp.memset(pb[0:1, 0, 0:1], 0.0).then_inc(s, n)
                gp.drain()
            gp.wait_ge(const_in, 64)
            with gp.Fori(0, 2) as h:
                for st in range(3):
                    gp.wait_ge(xn0_ready, (h * 3 + st) * 8 + 8)
                    for b in range(HT):
                        ins = gp.tensor_tensor(xres[:, b, :], xres[:, b, :], bo[:, st, :], ALU.add)
                    ins.then_inc(bo_added, 1)

        @block.scalar
        def _(act):
            def split_q(gq, k):
                act.wait_ge(wq_in, (gq + 1) * 16)
                act.activation(wq[0][:, :, k * P:(k + 1) * P], sq[:, :, k * P:(k + 1) * P], ACT.Copy).then_inc(wq_hi, 1)

            def split_one(w, raw, w_in, w_hi, g):
                act.wait_ge(w_in, (g + 1) * 16)
                act.activation(w[0][:], raw[:], ACT.Copy).then_inc(w_hi, 1)

            def slot(S):
                st = S.st

                def project_hi(k):
                    act.wait_ge(ring_full, S.ring + (k + 1))
                    src = ps[:, k % RING, :]
                    if k >= 4:
                        act.activation(vT[0][:, (k - 4) * 2:(k - 4) * 2 + 2, :].rearrange("p b m -> p (b m)"), src, ACT.Copy).then_inc(p_hi, 1)
                        return
                    hd = k // 2
                    wait_apart(act)
                    if k % 2 == 0:
                        act.activation(qT[hd][0][:], src, ACT.Identity, bias=head_col(st, "bq", S.g, hd)).then_inc(p_hi, 1)
                    else:
                        act.activation(kT[hd][0][:, :, 0:L], src.rearrange("p (b t) -> p b t", b=4), ACT.Identity,
                                       bias=head_col(st, "bk", S.g, hd)).then_inc(p_hi, 1)

                def exps(hd):
                    act.wait_ge(max_done, S.n * 2 + (hd - 1))
                    act.wait_ge(tr_full, S.n * 2 + (hd - 1))
                    for b in range(4):
                        o = (b % 2) * KW
                        ins = act.activation(pr[hd][:, b, 0:L + 1], ps[:, BANK_SC + b // 2, o:o + L + 1], ACT.Exp,
                                             bias=nbs[hd][:, b:b + 1], scale=SCALE, accum_out=sms[hd][:, b:b + 1])
                    ins.then_inc(exp_done, 1)

                def probs_hi(hd):
                    act.wait_ge(tr_full, S.n * 2 + (hd - 1 + 2))
                    act.activation(pT[hd][0][:], ps[:, BANK_TR + hd, :], ACT.Copy).then_inc(pt_hi, 1)

                def context_hi(hd):
                    act.wait_ge(pv_full, S.n * 2 + (hd - 1))
                    wait_apart(act)
                    act.activation(cT[hd][0][:], ps[:, BANK_PV, :], ACT.Identity, bias=head_col(st, "bv", S.gu, hd)).then_inc(ct_hi, 1)

                if S.attn:
                    act.wait_ge(ring_full, S.ring)
                if S.attn:
                    exps(0)
                if S.proj:
                    project_hi(0)
                    if S.quad == 0:
                        split_one(wv, sv, wv_in, wv_hi, S.gk)
                    else:
                        split_one(wo, so, wo_in, wo_hi, S.gq)
                if S.attn:
                    exps(1)
                if S.proj:
                    project_hi(1)
                if S.attn:
                    probs_hi(0)
                if S.proj:
                    project_hi(2)
                    if S.quad == 1:
                        split_q(S.gq + 1, 0)
                if S.attn:
                    probs_hi(1)
                    context_hi(0)
                if S.proj:
                    project_hi(3)
                    if S.quad == 1:
                        split_q(S.gq + 1, 1)
                if S.attn:
                    context_hi(1)
                if S.proj:
                    project_hi(4)
                    if S.quad == 1:
                        split_one(wk, sk, wk_in, wk_hi, S.gk + 1)
                    project_hi(5)

            def mlp_slot(S):
                if S.outp:
                    act.wait_ge(ring_full, S.out0)
                if S.proj and S.quad == 1:
                    split_one(wo, so, wo_in, wo_hi, S.gq)
                if S.proj:
                    for k in range(2):
                        act.wait_ge(fc1_full, S.n * 2 + (k + 1))
                        act.wait_ge(u_split, S.n * 2 + (k + 1))
                        wait_apart(act)
                        act.activation(lt[:, k, :], ps[:, BANK_SC + k, :], ACT.Gelu,
                                       bias=hv[:, bass.ds(S.g * 2 + (10 * NH + k), 1)]).then_inc(gelu_ready, 1)
                        if S.quad == 1:
                            split_q(S.gq + 1, k)
                        act.wait_ge(gelu_ready, S.n * 2 + (k + 1))
                        act.activation(S.u[k][0][:], lt[:, k, :], ACT.Copy).then_inc(u_hi, 1)

            act.wait_ge(const_in, 64)
            act.activation(bias_k[0][:].rearrange("p (s h) -> p s h", s=2),
                           hv[:, 0:10 * NH].rearrange("p (s k h) -> p s k h", s=2, k=5)[:, :, HV["bias_k"], :], ACT.Copy).then_inc(bk_hi, 1)
            act.wait_ge(ready, 6)
            split_q(0, 0)
            split_q(0, 1)
            split_one(wk, sk, wk_in, wk_hi, 0)
            with act.Fori(0, 2) as h:
                for quad, tile in ((0, lt), (1, lh)):
                    act.wait_ge(c_in[quad], h * 16 + 16)
                    act.activation(c2[0][:, :, quad * QT:(quad + 1) * QT], tile[:], ACT.Copy).then_inc(c_hi, 1)
                for st in range(3):
                    for quad in range(2):
                        r = (h * 3 + st) * 2 + quad
                        act.wait_ge(stats_ready, r + 1)
                        act.activation(std[:, :], mv[:, :, 1], ACT.Sqrt, bias=eps[:]).then_inc(std_ready, 1)
                        for c in range(EC):
                            act.wait_ge(lh_ready, r * 4 + (c + 1))
                            act.activation(h2[0][:, c, quad * QT:(quad + 1) * QT], lh[:, c, :], ACT.Copy).then_inc(h_hi, 1)
                    if st < 2:
                        attention_slots(act, h, st, slot)
                        act.wait_ge(pbT_full, h * 2 + (st + 1))
                        act.activation(bvs[:], ps[0:NH, BANK_BV, :], ACT.Copy)
                        act.activation(pbT[:], ps[0:NH, BANK_TR:BANK_TR + 2, :].rearrange("p a b -> p (a b)"), ACT.Copy).then_inc(pbT_ready, 1)
                    else:
                        mlp_slots(act, h, mlp_slot)

        @block.vector
        def _(v):
            def split_q(gq, k):
                v.wait_ge(wq_hi, gq * 2 + (k + 1))
                v.tensor_tensor(wq[1][:, :, k * P:(k + 1) * P], sq[:, :, k * P:(k + 1) * P], wq[0][:, :, k * P:(k + 1) * P],
                                ALU.subtract).then_inc(wq_split, 1)

            def split_one(w, raw, w_hi, w_split, g):
                v.wait_ge(w_hi, g + 1)
                v.tensor_tensor(w[1][:], raw[:], w[0][:], ALU.subtract).then_inc(w_split, 1)

            def add_output(idx, b, bank):
                v.wait_ge(ring_full, idx + 1)
                v.tensor_tensor(xres[:, b, :], xres[:, b, :], ps[:, bank, :], ALU.add).then_inc(evacuated, 1)

            def slot(S):
                st = S.st

                def project_lo(k):
                    v.wait_ge(p_hi, S.n * 6 + (k + 1))
                    src = ps[:, k % RING, :]
                    if k >= 4:
                        tiles = [t[:, (k - 4) * 2:(k - 4) * 2 + 2, :].rearrange("p b m -> p (b m)") for t in vT]
                        v.tensor_tensor(tiles[1], src, tiles[0], ALU.subtract).then_inc(evacuated, 1)
                        return
                    hd = k // 2
                    if k % 2 == 0:
                        v.scalar_tensor_tensor(out=qT[hd][1][:], in0=src, scalar=head_col(st, "bq", S.g, hd),
                                               in1=qT[hd][0][:], op0=ALU.add, op1=ALU.subtract).then_inc(evacuated, 1)
                    else:
                        for t in range(2):
                            v.tensor_scalar(kT[hd][t][:, :, L:L + 1],
                                            bias_k[t][:, bass.ds(S.g * 2 + (st * NH + hd), 1)].rearrange("p (a b) -> p a b", b=1).broadcast_to([P, 4, 1]),
                                            1.0, None, ALU.mult)
                        v.scalar_tensor_tensor(out=kT[hd][1][:, :, 0:L], in0=src.rearrange("p (b t) -> p b t", b=4),
                                               scalar=head_col(st, "bk", S.g, hd), in1=kT[hd][0][:, :, 0:L],
                                               op0=ALU.add, op1=ALU.subtract).then_inc(evacuated, 1)

                def row_max(hd):
                    v.wait_ge(sc_full, S.n * 2 + (hd - 1))
                    sc = ps[:, BANK_SC:BANK_SC + 2, 0:2 * KW].rearrange("p a (b k) -> p a b k", b=2)[:, :, :, 0:L + 1]
                    v.tensor_reduce(mxs[hd][:].rearrange("p (a b) -> p a b", a=2), sc, AX, ALU.max).then_inc(mx_done, 1)
                    v.wait_ge(mx_done, S.n * 2 + (hd - 1))
                    v.tensor_scalar(nbs[hd][:], mxs[hd][:], -SCALE, None, ALU.mult).then_inc(max_done, 1)

                def normalise(hd):
                    v.wait_ge(exp_done, S.n * 2 + (hd - 1 + 1))
                    v.reciprocal(rss[hd][:], sms[hd][:]).then_inc(rs_done, 1)
                    v.wait_ge(rs_done, S.n * 2 + (hd - 1))
                    v.tensor_tensor(pr[hd][:, :, 0:L + 1], pr[hd][:, :, 0:L + 1],
                                    rss[hd][:].rearrange("p (a b) -> p a b", b=1).broadcast_to([P, 4, L + 1]), ALU.mult).then_inc(norm_done, 1)
                    v.wait_ge(norm_done, S.n * 2 + (hd - 1))
                    v.tensor_scalar(pb[:, S.qu * 4:S.qu * 4 + 4, bass.ds(S.gu * 2 + hd, 1)], pr[hd][:, :, L:L + 1], 1.0, None,
                                    ALU.mult)

                def probs_lo(hd):
                    v.wait_ge(pt_hi, S.n * 2 + (hd - 1))
                    v.tensor_tensor(pT[hd][1][:], ps[:, BANK_TR + hd, :], pT[hd][0][:], ALU.subtract).then_inc(pt_split, 1)

                def context_lo(hd):
                    v.wait_ge(ct_hi, S.n * 2 + (hd - 1))
                    v.scalar_tensor_tensor(out=cT[hd][1][:], in0=ps[:, BANK_PV, :], scalar=head_col(st, "bv", S.gu, hd),
                                           in1=cT[hd][0][:], op0=ALU.add, op1=ALU.subtract).then_inc(ct_split, 1)

                if S.attn:
                    row_max(0)
                    normalise(0)
                if S.proj:
                    project_lo(0)
                if S.attn:
                    row_max(1)
                if S.proj and S.quad == 0:
                    split_one(wv, sv, wv_hi, wv_split, S.gk)
                if S.proj and S.quad == 1:
                    split_one(wo, so, wo_hi, wo_split, S.gq)
                    v.tensor_scalar(db[0][:], dbias[:, bass.ds(S.g * 2, 2), :], 1.0, None, ALU.mult).then_inc(db_hi, 1)
                    v.wait_ge(db_hi, S.gk + 1)
                    v.tensor_tensor(db[1][:], dbias[:, bass.ds(S.g * 2, 2), :], db[0][:], ALU.subtract).then_inc(db_ready, 1)
                if S.attn:
                    normalise(1)
                if S.proj:
                    project_lo(1)
                if S.attn:
                    probs_lo(0)
                if S.proj:
                    project_lo(2)
                    if S.quad == 1:
                        split_q(S.gq + 1, 0)
                if S.attn:
                    probs_lo(1)
                    context_lo(0)
                if S.proj:
                    project_lo(3)
                    if S.quad == 1:
                        split_q(S.gq + 1, 1)
                if S.attn:
                    context_lo(1)
                if S.proj:
                    project_lo(4)
                    if S.quad == 1:
                        split_one(wk, sk, wk_hi, wk_split, S.gk + 1)
                    project_lo(5)
                if S.attn:
                    v.wait_ge(bo_added, S.h * 3 + (st + 1))
                    for b in range(4):
                        add_output(S.out0 + b, S.qu * 4 + b, b % RING)

            def mlp_slot(S):
                if S.proj and S.quad == 1:
                    split_one(wo, so, wo_hi, wo_split, S.gq)
                if S.proj:
                    for k in range(2):
                        if S.quad == 1:
                            split_q(S.gq + 1, k)
                        v.wait_ge(u_hi, S.n * 2 + (k + 1))
                        v.tensor_tensor(S.u[k][1][:], lt[:, k, :], S.u[k][0][:], ALU.subtract).then_inc(u_split, 1)
                if S.outp:
                    v.wait_ge(bo_added, S.h * 3 + 3)
                    for b in range(4):
                        add_output(S.out0 + b, (1 - S.quad) * 4 + b, b % RING)

            v.wait_ge(bk_hi, 1)
            v.tensor_tensor(bias_k[1][:].rearrange("p (s h) -> p s h", s=2),
                            hv[:, 0:10 * NH].rearrange("p (s k h) -> p s k h", s=2, k=5)[:, :, HV["bias_k"], :],
                            bias_k[0][:].rearrange("p (s h) -> p s h", s=2), ALU.subtract).then_inc(bk_split, 1)
            v.memset(std[:], 1.0).then_inc(u_split, 2)
            v.wait_ge(bk_split, 1)
            v.wait_ge(ready, 6)
            split_q(0, 0)
            split_q(0, 1)
            split_one(wk, sk, wk_hi, wk_split, 0)
            with v.Fori(0, 2) as h:
                for quad, tile in ((0, lt), (1, lh)):
                    v.wait_ge(c_hi, h * 2 + (quad + 1))
                    v.tensor_tensor(c2[1][:, :, quad * QT:(quad + 1) * QT], tile[:], c2[0][:, :, quad * QT:(quad + 1) * QT],
                                    ALU.subtract).then_inc(c_split, 1)
                v.wait_ge(c_split, h * 2 + 2)
                v.wait_ge(x_in, h * 16 + 16)
                for st in range(3):
                    if st < 2:
                        col = (st * 5 + HV["bias_v"]) * NH, (st * 5 + HV["bv"]) * NH
                        v.tensor_tensor(dbias[:].rearrange("p a b -> p (a b)")[:, 0:NH * NH:NH + 1], hv[:, col[0]:col[0] + NH],
                                        hv[:, col[1]:col[1] + NH], ALU.subtract).then_inc(dbias_ready, 1)
                        v.wait_ge(dbias_ready, h * 2 + (st + 1))
                    for quad in range(2):
                        r = (h * 3 + st) * 2 + quad
                        step = [0]

                        def link(ins):
                            step[0] += 1
                            assert step[0] == 1
                            ins.then_inc(ln_step, 1)
                            v.wait_ge(ln_step, r + 1)

                        if quad == 1:
                            v.wait_ge(lnT_full, r)
                            v.wait_ge(h_split, r * 4)
                        layernorm_dve(v, xres[:, quad * 4:quad * 4 + 4, :], lt, stats, mv, std, rstd, bn_done,
                                      stats_ready, std_ready, xn0_ready, r, link)
                        v.wait_ge(xn0_ready, r * 4 + 4)
                        v.wait_ge(lnT_full, r + 1)
                        for c in range(EC):
                            w, b_ = VEC["s%d" % (st + 1)] + c, VEC["o%d" % (st + 1)] + c
                            v.tensor_scalar(lh[:, c, :], ps[:, c, :], vec[:, w:w + 1], vec[:, b_:b_ + 1], ALU.mult, ALU.add).then_inc(lh_ready, 1)
                        for c in range(EC):
                            v.wait_ge(h_hi, r * 4 + (c + 1))
                            v.tensor_tensor(h2[1][:, c, quad * QT:(quad + 1) * QT], lh[:, c, :], h2[0][:, c, quad * QT:(quad + 1) * QT],
                                            ALU.subtract).then_inc(h_split, 1)
                    if st < 2:
                        attention_slots(v, h, st, slot)
                        base = h * HALF + (st * STAGE + 160)
                        for b in range(HT):
                            add_output(base + b, b, b % RING)
                        v.wait_ge(evacuated, base + (HT + RING))
                    else:
                        mlp_slots(v, h, mlp_slot)
                        v.wait_ge(evacuated, h * HALF + (HALF + RING))

        @block.tensor
        def _(pe):
            def ring_wait(idx):
                pe.wait_ge(evacuated, idx + 1)

            def slot(S):
                st = S.st
                cols = slice(S.quad * QT, (S.quad + 1) * QT)

                def project(k):
                    ring_wait(S.ring + k)
                    if k < 4:
                        hd = k // 2
                        w, x = (wq, h2) if k % 2 == 0 else (wk, c2)
                        if k % 2 == 0:
                            pe.wait_ge(wq_split, S.gq * 2 + (hd + 1))
                        else:
                            pe.wait_ge(wk_split, S.gk + 1)
                        for c in range(EC):
                            ins = mm3(pe, ps[:, k % RING, :], [t[:, c, hd * P:(hd + 1) * P] for t in w],
                                      [t[:, c, cols] for t in x], c == 0, c == EC - 1)
                    else:
                        pe.wait_ge(wv_split, S.gk + 2)
                        for b in range(2):
                            t0 = S.quad * QT + ((k - 4) * 2 + b) * L
                            for c in range(EC):
                                ins = mm3(pe, ps[:, k % RING, b * 256:(b + 1) * 256], [t[:, c, t0:t0 + L] for t in c2],
                                          [t[:, c, :] for t in wv], c == 0, c == EC - 1)
                    ins.then_inc(ring_full, 1)

                def scores(hd):
                    if hd == 0:
                        pe.wait_ge(evacuated, S.projected + RING)
                    pe.wait_ge(exp_done, S.n * 2 + (hd - 1))
                    for b in range(4):
                        o = (b % 2) * KW
                        ins = mm3(pe, ps[:, BANK_SC + b // 2, o:o + KW], [t[:, b * L:(b + 1) * L] for t in qT[hd]],
                                  [t[:, b, :] for t in kT[hd]], True, True)
                    ins.then_inc(sc_full, 1)

                def transpose(hd):
                    pe.wait_ge(norm_done, S.n * 2 + (hd - 1))
                    for b in range(4):
                        ins = pe.transpose(ps[:, BANK_TR + hd, b * L:(b + 1) * L], pr[hd][:, b, 0:L], ident[:])
                    ins.then_inc(tr_full, 1)

                def context(hd):
                    pe.wait_ge(pt_split, S.n * 2 + (hd - 1))
                    pe.wait_ge(ct_split, S.n * 2 + (hd - 1))
                    for b in range(4):
                        ins = mm3(pe, ps[:, BANK_PV, b * L:(b + 1) * L], [t[:, b, hd * P:(hd + 1) * P] for t in vT],
                                  [t[:, b * L:(b + 1) * L] for t in pT[hd]], True, True)
                    ins.then_inc(pv_full, 1)

                def outputs():
                    pe.wait_ge(ct_split, S.n * 2 + 1)
                    for b in range(4):
                        ring_wait(S.out0 + b)
                        for hd in range(2):
                            ins = mm3(pe, ps[:, b % RING, :], [t[:, b * L:(b + 1) * L] for t in cT[hd]],
                                      [t[:, hd, :] for t in wo], hd == 0, hd == 1)
                        ins.then_inc(ring_full, 1)

                if S.attn:
                    scores(0)
                if S.proj:
                    project(0)
                if S.attn:
                    scores(1)
                if S.proj:
                    project(1)
                if S.attn:
                    transpose(0)
                if S.proj:
                    project(2)
                if S.attn:
                    transpose(1)
                    context(0)
                if S.proj:
                    project(3)
                if S.attn:
                    context(1)
                if S.proj:
                    project(4)
                    project(5)
                    if S.quad == 1:
                        pe.wait_ge(wo_split, S.gq + 2)
                        pe.wait_ge(db_ready, S.gk + 1)
                        for hd in range(2):
                            for i, (a, b) in enumerate(((0, 0), (0, 1), (1, 0))):
                                pe.matmul(ps[0:NH, BANK_BV, :], db[a][:, hd, :], wo[b][:, hd, :],
                                          start=isinstance(S.g, int) and hd == 0 and i == 0, stop=False, skip_group_check=True)
                if S.attn:
                    outputs()

            def mlp_slot(S):
                if S.proj:
                    for k in range(2):
                        pe.wait_ge(wq_split, S.gq * 2 + (k + 1))
                        if S.outp:
                            pe.wait_ge(gelu_ready, S.n * 2 + (k - 1))
                        for c in range(EC):
                            ins = mm3(pe, ps[:, BANK_SC + k, :], [t[:, c, k * P:(k + 1) * P] for t in wq],
                                      [t[:, c, S.quad * QT:(S.quad + 1) * QT] for t in h2], c == 0, c == EC - 1)
                        ins.then_inc(fc1_full, 1)
                if S.outp:
                    pe.wait_ge(u_split, S.n * 2 + 2)
                    pe.wait_ge(wo_split, (S.gq + 2) if S.quad == 1 else (S.gq + 1))
                    for b in range(4):
                        ring_wait(S.out0 + b)
                        for k in range(2):
                            ins = mm3(pe, ps[:, b % RING, :], [t[:, b * L:(b + 1) * L] for t in S.u_last[k]],
                                      [t[:, k, :] for t in wo], k == 0, k == 1)
                        ins.then_inc(ring_full, 1)

            pe.wait_ge(const_in, 64)
            with pe.Fori(0, 2) as h:
                for st in range(3):
                    for quad in range(2):
                        r = (h * 3 + st) * 2 + quad
                        if quad == 1:
                            pe.wait_ge(lh_ready, r * 4)
                        for b in range(4):
                            pe.wait_ge(xn0_ready, r * 4 + (b + 1))
                            for c in range(EC):
                                ins = pe.transpose(ps[:, c, b * P:(b + 1) * P], lt[:, b, c * P:(c + 1) * P], ident[:])
                        ins.then_inc(lnT_full, 1)
                    pe.wait_ge(h_split, (h * 3 + st) * 8 + 8)
                    if st == 0:
                        pe.wait_ge(c_split, h * 2 + 2)
                        pe.wait_ge(ready, 6)
                    if st < 2:
                        attention_slots(pe, h, st, slot)
                        for b in range(HT):
                            ins = pe.transpose(ps[0:NH, BANK_TR + b // 4, (b % 4) * P:(b % 4 + 1) * P], pb[:, b, :], ident[:])
                        ins.then_inc(pbT_full, 1)
                        pe.wait_ge(pbT_ready, h * 2 + (st + 1))
                        base = h * HALF + (st * STAGE + 160)
                        for b in range(HT):
                            ring_wait(base + b)
                            pe.matmul(ps[:, b % RING, :], pbT[:, b * P:(b + 1) * P], bvs[:], start=True, stop=True).then_inc(ring_full, 1)
                    else:
                        mlp_slots(pe, h, mlp_slot)


def build(nc, io, out):
    x2 = nc.dram_tensor("x2_dram", (B, L, E), F32, kind="Internal").ap()
    time_mix(nc, io, x2)
    x3 = nc.dram_tensor("x3_dram", (B, L, E), F32, kind="Internal").ap()
    channel_mix(nc, io, x2, x3)
    cross_attend(nc, io, x3, out)


def vec_table(a):
    return np.ascontiguousarray(a.reshape(-1, EC, P).transpose(2, 0, 1).reshape(P, -1))


def w_tiles(w, m):
    k, n = w.shape
    return np.ascontiguousarray(w.reshape(k // P, P, n // m, m).transpose(2, 1, 0, 3))


def layouts(i):
    a = {}
    p = "L0_xattn_"
    a["x"] = i["x"]
    ctx = i["ctx_2048"]
    vecs = [i[p + n] for n in ("ln1_w", "ln1_b", "ln2_w", "ln2_b", "maa_x")] + [i[p + "maa_stack"][m] for m in range(5)]
    vecs += [i[p + "time_decay"], i[p + "faaaa"].reshape(E), i[p + "gn_w"], i[p + "gn_b"], i[p + "ffn_maa_k"], i[p + "ffn_maa_r"]]
    vecs += [i["L1_xattn_" + n] for n in ("ln1_scale", "ln1_offset", "ln2_scale", "ln2_offset", "ln_mlp_scale", "ln_mlp_offset")]
    a["vec"] = vec_table(np.stack(vecs))
    a["ident"] = np.eye(P, dtype=np.float32)
    same = np.kron(np.eye(8, dtype=np.float32), np.ones((HS, HS), np.float32))
    a["head_sum"] = same
    a["head_mean"] = same / HS
    a["head_mean4"] = np.tile(np.kron(np.eye(8, dtype=np.float32), np.ones((HS, 1), np.float32)), (1, 4)) / HS
    unpack = np.zeros((P, EC, P), np.float32)
    for c in range(EC):
        for h in range(8):
            unpack[32 * c + h, c, h * HS:(h + 1) * HS] = 1
    a["unpack"] = unpack
    pick = np.zeros((P, P + HS - 1), np.float32)
    pick[np.arange(P), np.arange(P) // HS * HS + HS - 1] = 1
    a["pick_k"] = pick
    spread = np.zeros((P, HS, P), np.float32)
    for d in range(HS):
        spread[:, d, :] = same * (np.arange(P)[:, None] % HS == d)
    a["spread_v"] = spread.reshape(P, HS * P)
    a["prev1"] = np.ascontiguousarray(ctx[:, 1, :].reshape(B, EC, P).transpose(2, 1, 0))
    a["prev0"] = np.ascontiguousarray(ctx[:, 0, :].reshape(B, EC, P).transpose(2, 1, 0))
    a["s0"] = np.ascontiguousarray(ctx[:, 2:2 + HS, :].reshape(NQ, 4, EC, P, HS).transpose(0, 3, 2, 4, 1))
    a["l0w"] = np.stack([w_tiles(i[p + n].T, E)[0] for n in ("Wr", "Wk", "Wv", "Wg", "Wo", "ffn_Wk", "ffn_Wr", "ffn_Wv")])
    a["lora1"] = w_tiles(i[p + "maa_w1"], 160)[0]
    a["dec1"] = w_tiles(i[p + "decay_w1"], 64)[0]
    a["lora2"] = i[p + "maa_w2"].reshape(160, E)
    a["dec2"] = i[p + "decay_w2"]
    p = "L1_xattn_"
    a["ctxT"] = ctx.reshape(B * L, EC, P).transpose(2, 1, 0)
    a["head_vec"] = np.stack([i[p + n + s].reshape(NH, KD) for s in "12" for n in ("bq", "bk", "bv", "bias_k", "bias_v")]
                             + [i[p + "b_fc1"].reshape(NH, P)]).transpose(2, 0, 1).reshape(P, -1)
    a["bo"] = np.broadcast_to(np.stack([i[p + "bo1"], i[p + "bo2"], i[p + "b_fc2"]]), (P, 3, E))
    q = [w_tiles(i[p + n], 256) for n in ("wq1", "wq2", "w_fc1")]
    a["wq"] = np.concatenate(q + [q[0][0:1]])
    k = [w_tiles(i[p + n], 256) for n in ("wk1", "wk2")]
    a["wk"] = np.concatenate(k + [k[0][0:1]])
    a["wv"] = np.concatenate([w_tiles(i[p + n], 256) for n in ("wv1", "wv2")])
    a["wo"] = np.concatenate([i[p + n].reshape(NH // 2, 2, P, E).transpose(0, 2, 1, 3) for n in ("wo1", "wo2", "w_fc2")])
    return {k: np.ascontiguousarray(v) for k, v in a.items()}


def kernel(**inputs):
    import concourse.bacc as _bacc
    from concourse.bass_utils import run_bass_kernel_spmd as _run

    nc = _bacc.Bacc("TRN2", target_bir_lowering=False, num_devices=1)
    arrays = layouts({k: np.asarray(v) for k, v in inputs.items()})
    io = {n: nc.dram_tensor(f"in_{n}", a.shape, mybir.dt.from_np(a.dtype), kind="ExternalInput").ap() for n, a in arrays.items()}
    out = nc.dram_tensor("out_dram", (B, L, E), F32, kind="ExternalOutput").ap()
    build(nc, io, out)
    r = _run(nc, [{f"in_{n}": a for n, a in arrays.items()}], core_ids=[0])
    return r.results[0]["out_dram"]
```

```python
from contextlib import ExitStack

import numpy as np
import concourse.bass as bass
from concourse import mybir

ALU = mybir.AluOpType
ACT = mybir.ActivationFunctionType
AX = mybir.AxisListType.X
F32 = mybir.dt.float32
FR = mybir.dt.float32r

P = 128
B, L, E = 16, 128, 512
EC = E // P
NQ = B // 4
QT = 4 * L
HS = 16
EPS = 1e-5
NH, KD = 16, 128
F = 2048
SCALE = float(KD) ** -0.5
LORA = 32

VEC_NAMES = ["ln1_w", "ln1_b", "ln2_w", "ln2_b", "maa_x", "stack0", "stack1", "stack2", "stack3", "stack4",
             "time_decay", "faaaa", "gn_w", "gn_b", "ffn_maa_k", "ffn_maa_r",
             "s1", "o1", "s2", "o2", "s3", "o3"]
VEC = {n: i * EC for i, n in enumerate(VEC_NAMES)}
NV = len(VEC_NAMES) * EC


class Steps:

    def __init__(self, engine, sem, base=0):
        self.engine, self.sem, self.base, self.n = engine, sem, base, 0

    def link(self, instruction):
        self.n += 1
        instruction.then_inc(self.sem, 1)
        self.engine.wait_ge(self.sem, self.base + self.n)


def mm3(pe, out, lhs, rhs, first, last):
    pe.matmul(out, lhs[0], rhs[0], start=first, stop=False)
    pe.matmul(out, lhs[0], rhs[1], start=False, stop=False)
    return pe.matmul(out, lhs[1], rhs[0], start=False, stop=last)


def layernorm_stats(v, x4, stats, mv, rstd, bn_done, stats_ready, n):
    for b in range(4):
        v.bn_stats(stats[:, b, :], x4[:, b, :]).then_inc(bn_done, 1)
    v.wait_ge(bn_done, n * 4 + 4)
    v.memset(rstd[:, :], 1.0)
    for b in range(4):
        ins = v.bn_aggr(mv[:, b, :], stats[:, b, :])
    ins.then_inc(stats_ready, 1)


def layernorm_dve(v, x4, xn4, stats, mv, std, rstd, bn_done, stats_ready, std_ready, xn0_ready, n, link):
    layernorm_stats(v, x4, stats, mv, rstd, bn_done, stats_ready, n)
    v.wait_ge(std_ready, n + 1)
    link(v.reciprocal(rstd[:, :], std[:, :]))
    for b in range(4):
        v.tensor_scalar(xn4[:, b, :], x4[:, b, :], mv[:, b, 0:1], rstd[:, b:b + 1], ALU.subtract,
                        ALU.mult).then_inc(xn0_ready, 1)


def time_mix(nc, io, x2):
    J = 6
    MIX = [None, 1, 3, 0, 2, 4]
    HALVES = 32
    with ExitStack() as ctx:
        def sb(n, s, d=F32):
            return ctx.enter_context(nc.sbuf_tensor("tm_" + n, s, d))

        def ps(n, s):
            return ctx.enter_context(nc.psum_tensor("tm_" + n, s, F32))

        def sem(n):
            return ctx.enter_context(nc.semaphore("tm_" + n))

        vec = sb("vec", [P, NV])
        ident = sb("ident", [P, P])
        head_sum = sb("head_sum", [P, P])
        head_mean = sb("head_mean", [P, P])
        head_mean4 = sb("head_mean4", [P, 32])
        unpack = sb("unpack", [P, EC, P])
        pick_k = sb("pick_k", [P, P + HS - 1])
        spread_v = sb("spread_v", [P, HS, P], FR)
        prev = sb("prev", [P, EC, B])
        eps = sb("eps", [P, 1])
        rest = sb("rest", [1, 1])
        w_hi = sb("w_hi", [P, 5, EC, E], FR)
        w_lo = sb("w_lo", [P, 5, EC, E], FR)
        lora1 = (sb("lora1_hi", [P, EC, 160], FR), sb("lora1_lo", [P, EC, 160], FR))
        dec1 = (sb("dec1_hi", [P, EC, 64], FR), sb("dec1_lo", [P, EC, 64], FR))
        lora2 = sb("lora2", [P, E])
        lora2e = sb("lora2e", [LORA, E])
        dec2 = sb("dec2", [64, E])
        xq = sb("xq", [P, 4, E])
        stats = sb("stats", [P, 4, 6])
        mv = sb("mv", [P, 4, 2])
        std = sb("std", [P, 4])
        rstd = sb("rstd", [P, 4])
        s0 = sb("s0", [P, EC, HS, 4])
        xn = sb("xn", [P, EC, 4, L + 1])
        sx = sb("sx", [P, EC, QT])
        xf = sb("xf", [P, EC, QT])
        x_hi = sb("x_hi", [P, EC, QT], FR)
        x_lo = sb("x_lo", [P, EC, QT], FR)
        h5 = sb("h5", [P, QT])
        h5e = sb("h5e", [LORA, QT])
        dh = sb("dh", [64, QT])
        ew = sb("ew", [P, QT])
        wd = sb("wd", [P, EC, 4, L])
        rr = sb("rr", [P, EC, QT])
        kk = sb("kk", [P, EC, 4, L + 1])
        vv = sb("vv", [P, EC, 4, L + 1])
        gg = sb("gg", [P, EC, QT])
        pj = [ps("pj0", [P, QT]), ps("pj1", [P, QT])]
        mx = [ps("mx0", [P, QT]), ps("mx1", [P, QT])]
        vb = ps("vb", [P, 4, QT])

        first_in, const_in, small_in = sem("first_in"), sem("const_in"), sem("small_in")
        rr_in, gg_in, w_hi_ready, w_ready = sem("rr_in"), sem("gg_in"), sem("w_hi_ready"), sem("w_ready")
        x_in, s0_in, res_in, x2_out, quad_done = sem("x_in"), sem("s0_in"), sem("res_in"), sem("x2_out"), sem("quad_done")
        bn_done = sem("bn_done")
        stats_ready, std_ready, xn0_ready = sem("stats_ready"), sem("std_ready"), sem("xn0_ready")
        xnT_full, xn_ready, prev_ready = sem("xnT_full"), sem("xn_ready"), sem("prev_ready")
        xf_ready, hi_ready, split_ready, x_used = sem("xf_ready"), sem("hi_ready"), sem("split_ready"), sem("x_used")
        pj_full, pj_free, mx_full, mx_free = sem("pj_full"), sem("pj_free"), sem("mx_full"), sem("mx_free")
        f_full, f_free = sem("f_full"), sem("f_free")
        ew_ready = sem("ew_ready")
        dve_step, v_hi_ready, v_split_ready = sem("dve_step"), sem("v_hi_ready"), sem("v_split_ready")
        ruk_ready, bonus_full, bonus_used = sem("ruk_ready"), sem("bonus_full"), sem("bonus_used")
        vb_full, s0_set, kv_ready, scanned = sem("vb_full"), sem("s0_set"), sem("kv_ready"), sem("scanned")
        rs_ready, rs_used, acc_full, att_ready = sem("rs_ready"), sem("rs_used"), sem("acc_full"), sem("att_ready")
        mean_full, cent_ready, sq_ready, var_full = sem("mean_full"), sem("cent_ready"), sem("sq_ready"), sem("var_full")
        gstd_ready, grstd_ready, unpacked = sem("gstd_ready"), sem("grstd_ready"), sem("unpacked")
        y_ready, y_hi_ready, y_split_ready, wo_full = sem("y_ready"), sem("y_hi_ready"), sem("y_split_ready"), sem("wo_full")
        ready, ln_step = sem("ready"), sem("ln_step")

        xn_flat = xn[:, :, :, :].rearrange("p a b c -> p (a b c)")[:, 0:4 * QT].rearrange("p (a b) -> p a b", a=4)
        state = [xn_flat[:, 0:2, :], xn_flat[:, 2:4, :]]
        prod = [sx[:, 0:2, :], sx[:, 2:4, :], xf[:, 0:2, :], xf[:, 2:4, :]]
        wo_bank = [mx[0], mx[1], pj[0], pj[1]]
        raw_spread = rr[:].rearrange("p a b -> p (a b)")
        raw_lora1 = sx[:, 0:2, :].rearrange("p a b -> p (a b)")[:, 0:640].rearrange("p (c m) -> p c m", c=EC)
        raw_dec1 = sx[:, 2, 0:256].rearrange("p (c m) -> p c m", c=EC)
        DVE_STEPS = 4 + 8 + 3
        FIRST = (("vec", vec), ("ident", ident), ("prev1", prev))
        CONSTS = (("head_sum", head_sum), ("head_mean", head_mean), ("head_mean4", head_mean4),
                  ("unpack", unpack), ("pick_k", pick_k), ("dec2", dec2))
        N_CONST = 16 * (len(CONSTS) + 2)
        block = ctx.enter_context(nc.Block())

        def quad3(ap):
            return ap.rearrange("p (b t) -> p b t", b=4)

        def x_used_wait(engine, q, j, c):
            if c < EC - 1:
                engine.wait_ge(x_used, q * (J * 3) + (j * 3 + c + 1))
            elif j == 0:
                engine.wait_ge(pj_full, q * 7 + 2)
            elif j == 1:
                engine.wait_ge(pj_full, q * 7 + 3)
            else:
                engine.wait_ge(f_full, q * 16 + (j - 1) * 4)

        @block.sync
        def _(sp):
            sp.dma_start(xq[:], io["x"][0:4].rearrange("b t e -> t b e")).then_inc(x_in, 16)
            for name, tile in FIRST:
                sp.dma_start(tile[:], io[name]).then_inc(first_in, 16)
            sp.dma_start(raw_lora1, io["lora1"]).then_inc(small_in, 16)
            sp.dma_start(raw_dec1, io["dec1"]).then_inc(small_in, 16)
            sp.dma_start(lora2[:], io["lora2"][0:P, :]).then_inc(const_in, 16)
            sp.dma_start(lora2e[:], io["lora2"][P:160, :]).then_inc(const_in, 16)
            for name, tile in CONSTS:
                sp.dma_start(tile[:], io[name]).then_inc(const_in, 16)
            sp.dma_start(rr[:], io["l0w"][0]).then_inc(rr_in, 16)
            sp.dma_start(gg[:], io["l0w"][1]).then_inc(gg_in, 16)
            sp.wait_ge(w_ready, 3)
            sp.dma_start(raw_spread, io["spread_v"]).then_inc(rr_in, 16)
            for j in range(2, 5):
                sp.wait_ge(w_ready, 2 + j)
                sp.dma_start(gg[:], io["l0w"][j]).then_inc(gg_in, 16)

            def quad(q, last):
                if not isinstance(q, int) or q > 0:
                    sp.wait_ge(scanned, q * (2 * HALVES))
                sp.dma_start(s0[:], io["s0"][bass.ds(q, 1)].rearrange("a p c d b -> (a p) c d b")).then_inc(s0_in, 16)
                sp.wait_ge(xn0_ready, q * 4 + 4)
                sp.dma_start(xq[:], io["x"][bass.ds(0 if last else q * 4 + 4, 4)].rearrange("b t e -> t b e")).then_inc(x_in, 16)
                sp.wait_ge(acc_full, q * 4 + 4)
                sp.dma_start(rr[:], io["x"][bass.ds(q * 4, 4)].rearrange("b t e -> t b e")).then_inc(res_in, 16)
                sp.wait_ge(quad_done, q + 1)
                sp.dma_start(x2[bass.ds(q * 4, 4)].rearrange("b t e -> t b e"), rr[:]).then_inc(x2_out, 16)

            quad(0, False)
            with sp.Fori(1, NQ - 1) as q:
                quad(q, False)
            quad(NQ - 1, True)
            sp.wait_ge(x2_out, NQ * 16 + 16)

        @block.gpsimd
        def _(gp):
            gp.memset(eps[:], EPS).then_inc(ready, 1)
            gp.memset(wd[:], 0.0).then_inc(ready, 1)
            gp.memset(kk[:, :, :, 0:1], 1.0).then_inc(ready, 1)
            gp.memset(vv[:, :, :, 0:1], 0.0).then_inc(ready, 1)
            gp.memset(rest[:], 0.0).then_inc(x2_out, 16)
            with gp.Fori(0, NQ) as q:
                for t in range(HALVES):
                    if t >= 4:
                        gp.wait_ge(rs_used, q * HALVES + (t - 3))
                    gp.wait_ge(scanned, q * (2 * HALVES) + 2 * (t + 1))
                    g = t // 8
                    gp.tensor_tensor(prod[t % 4], state[t % 2], rr[:, g:g + 1, :].broadcast_to([P, 2, QT]), ALU.mult).then_inc(rs_ready, 1)

        @block.scalar
        def _(act):
            def split_w(j):
                if j == 0:
                    act.wait_ge(rr_in, 16)
                    raw = rr
                else:
                    act.wait_ge(gg_in, j * 16)
                    raw = gg
                act.activation(w_hi[:, j], raw[:], ACT.Copy).then_inc(w_hi_ready, 1)

            def roots(q):
                act.wait_ge(stats_ready, q + 1)
                act.activation(std[:, :], mv[:, :, 1], ACT.Sqrt, bias=eps[:]).then_inc(std_ready, 1)

            def quad(q, first):
                def hi(j, c):
                    act.wait_ge(xf_ready, q * (4 * J) + (4 * j + c + 1))
                    if j > 0:
                        x_used_wait(act, q, j - 1, c)
                    act.activation(x_hi[:, c, :], xf[:, c, :], ACT.Copy).then_inc(hi_ready, 1)

                def decay(f):
                    act.wait_ge(pj_full, q * 7 + (3 + f + 1))
                    if f > 0:
                        act.wait_ge(ew_ready, q * 4 + f)
                    col = VEC["time_decay"] + f
                    act.activation(ew[:], pj[(3 + f) % 2][:], ACT.Exp, bias=vec[:, col:col + 1]).then_inc(pj_free, 1)
                    act.wait_ge(pj_free, q * 7 + (3 + f + 1))
                    act.activation(wd[:, f, :, 1:L], quad3(ew[:])[:, :, 0:L - 1], ACT.Exp, scale=-1.0).then_inc(ew_ready, 1)

                def evacuate(j):
                    if j == 2:
                        act.wait_ge(x2_out, q * 16 + 16)
                    for f in range(EC):
                        act.wait_ge(f_full, q * 16 + ((j - 2) * 4 + f + 1))
                        if j == 2:
                            ins = act.activation(rr[:, f, :], vb[:, f, :], ACT.Copy)
                        elif j == 3:
                            ins = act.activation(kk[:, f, :, 1:L + 1], quad3(vb[:, f, :]), ACT.Copy)
                        elif j == 4:
                            ins = act.activation(vv[:, f, :, 1:L + 1], quad3(vb[:, f, :]), ACT.Copy)
                        else:
                            ins = act.activation(gg[:, f, :], vb[:, f, :], ACT.Silu)
                        ins.then_inc(f_free, 1)

                def normalised(c):
                    act.wait_ge(xnT_full, q * 4 + (c + 1))
                    act.activation(xn[:, c, :, 1:L + 1], quad3(vb[:, c, :]), ACT.Identity,
                                   bias=vec[:, VEC["ln1_b"] + c:VEC["ln1_b"] + c + 1],
                                   scale=vec[:, VEC["ln1_w"] + c:VEC["ln1_w"] + c + 1]).then_inc(xn_ready, 1)

                normalised(0)
                normalised(1)
                hi(0, 0)
                normalised(2)
                hi(0, 1)
                normalised(3)
                hi(0, 2)
                hi(0, 3)
                for k, tile in ((0, h5), (1, h5e)):
                    act.wait_ge(pj_full, q * 7 + (k + 1))
                    act.activation(tile[:], pj[k][0:tile.shape[0], :], ACT.Tanh).then_inc(pj_free, 1)
                for c in range(EC):
                    hi(1, c)
                if first:
                    act.wait_ge(rr_in, 32)
                    act.activation(spread_v[:].rearrange("p a b -> p (a b)"), raw_spread, ACT.Copy).then_inc(w_hi_ready, 1)
                    split_w(1)
                for c in range(3):
                    hi(2, c)
                act.wait_ge(pj_full, q * 7 + 3)
                act.activation(dh[:], pj[0][0:64, :], ACT.Tanh).then_inc(pj_free, 1)
                hi(2, 3)
                if first:
                    split_w(2)
                for j in range(2, J):
                    for c in range(3):
                        if j + 1 < J:
                            hi(j + 1, c)
                        if j == 2:
                            decay(c)
                    evacuate(j)
                    if j + 1 < J:
                        hi(j + 1, 3)
                    if j == 2:
                        decay(3)
                    if first and j + 1 < J - 1:
                        split_w(j + 1)
                act.wait_ge(f_free, q * 16 + 16)
                for c in range(EC):
                    act.activation(quad3(x_hi[:, c, :]), vv[:, c, :, 0:L], ACT.Copy).then_inc(v_hi_ready, 1)
                act.wait_ge(s0_in, q * 16 + 16)
                for t in range(HALVES):
                    act.wait_ge(vb_full, q * HALVES + (t + 1))
                    d = 2 * (t % 8)
                    act.activation(vb[:, 2 * (t % 2):2 * (t % 2) + 2, 0:QT:L], s0[:, t // 8, d:d + 2, :], ACT.Copy).then_inc(s0_set, 1)
                for c in range(EC):
                    act.wait_ge(cent_ready, q * 4 + (c + 1))
                    act.activation(quad3(xf[:, c, :]), vv[:, c, :, 1:L + 1], ACT.Square).then_inc(sq_ready, 1)
                act.wait_ge(var_full, q + 1)
                act.activation(ew[:], mx[0][:], ACT.Sqrt, bias=eps[:]).then_inc(gstd_ready, 1)
                for c in range(EC):
                    act.wait_ge(y_ready, q * 4 + (c + 1))
                    act.activation(x_hi[:, c, :], xf[:, c, :], ACT.Copy).then_inc(y_hi_ready, 1)
                roots(q + 1)

            act.wait_ge(small_in, 32)
            act.activation(lora1[0][:], raw_lora1, ACT.Copy).then_inc(w_hi_ready, 1)
            act.activation(dec1[0][:], raw_dec1, ACT.Copy).then_inc(w_hi_ready, 1)
            act.wait_ge(ready, 4)
            roots(0)
            split_w(0)
            act.wait_ge(first_in, 16 * len(FIRST))
            quad(0, True)
            with act.Fori(1, NQ) as q:
                quad(q, False)

        @block.vector
        def _(v):
            def split_w(j):
                v.wait_ge(w_hi_ready, 3 if j == 0 else 4 + j)
                v.tensor_tensor(w_lo[:, j], (gg if j else rr)[:], w_hi[:, j], ALU.subtract).then_inc(w_ready, 1)

            def norm(q):
                def link(ins):
                    ins.then_inc(ln_step, 1)
                    v.wait_ge(ln_step, q + 1)

                v.wait_ge(x_in, q * 16 + 16)
                layernorm_dve(v, xq, xf, stats, mv, std, rstd, bn_done, stats_ready, std_ready, xn0_ready, q, link)

            def quad(q, first):
                steps = Steps(v, dve_step, q * DVE_STEPS)
                link = steps.link
                v.tensor_copy(xn[:, :, :, 0], prev[:, :, bass.ds(q * 4, 4)]).then_inc(prev_ready, 1)
                v.wait_ge(prev_ready, q + 1)
                def lo(j, c):
                    v.wait_ge(hi_ready, q * (4 * J) + (4 * j + c + 1))
                    v.tensor_tensor(x_lo[:, c, :], xf[:, c, :], x_hi[:, c, :], ALU.subtract).then_inc(split_ready, 1)

                for c in range(EC):
                    v.wait_ge(xn_ready, q * 4 + (c + 1))
                    link(v.tensor_tensor(quad3(sx[:, c, :]), xn[:, c, :, 0:L], xn[:, c, :, 1:L + 1], ALU.subtract))
                    if c == 0:
                        v.wait_ge(xnT_full, q * 4 + 4)
                    m = VEC["maa_x"] + c
                    v.scalar_tensor_tensor(out=quad3(xf[:, c, :]), in0=quad3(sx[:, c, :]), scalar=vec[:, m:m + 1],
                                           in1=xn[:, c, :, 1:L + 1], op0=ALU.mult, op1=ALU.add).then_inc(xf_ready, 1)
                    if c > 0:
                        lo(0, c - 1)
                lo(0, EC - 1)
                for j in range(1, J):
                    for c in range(EC):
                        s = VEC["stack%d" % MIX[j]] + c
                        n = (j - 1) * 4 + c
                        v.wait_ge(split_ready, q * (4 * J) + (4 * (j - 1) + c + 1))
                        v.wait_ge(mx_full, q * 20 + (n + 1))
                        v.scalar_tensor_tensor(out=xf[:, c, :], in0=mx[n % 2][:], scalar=vec[:, s:s + 1],
                                               in1=sx[:, c, :], op0=ALU.add, op1=ALU.mult).then_inc(mx_free, 1)
                        if c > 0:
                            lo(j, c - 1)
                        v.wait_ge(mx_free, q * 20 + (n + 1))
                        v.tensor_tensor(quad3(xf[:, c, :]), quad3(xf[:, c, :]), xn[:, c, :, 1:L + 1], ALU.add).then_inc(xf_ready, 1)
                    lo(j, EC - 1)
                    if first and j < J - 1:
                        split_w(j)
                v.wait_ge(f_free, q * 16 + 8)
                for c in range(EC):
                    u = VEC["faaaa"] + c
                    v.scalar_tensor_tensor(out=quad3(sx[:, c, :]), in0=quad3(rr[:, c, :]), scalar=vec[:, u:u + 1],
                                           in1=kk[:, c, :, 1:L + 1], op0=ALU.mult, op1=ALU.mult).then_inc(ruk_ready, 1)
                for c in range(EC):
                    v.wait_ge(v_hi_ready, q * 4 + (c + 1))
                    v.tensor_tensor(quad3(x_lo[:, c, :]), vv[:, c, :, 0:L], quad3(x_hi[:, c, :]), ALU.subtract).then_inc(v_split_ready, 1)
                v.wait_ge(v_split_ready, q * 4 + 4)
                for c in range(EC):
                    v.wait_ge(bonus_full, q * 4 + (c + 1))
                    v.tensor_tensor(vv[:, c, :, 1:L + 1], quad3(pj[c % 2][:]), vv[:, c, :, 1:L + 1], ALU.mult).then_inc(bonus_used, 1)
                v.wait_ge(bonus_used, q * 4 + 4)

                def add_bonus(g):
                    v.wait_ge(acc_full, q * 4 + (g + 1))
                    v.tensor_tensor(vv[:, g, :, 1:L + 1], quad3(mx[g % 2][:]), vv[:, g, :, 1:L + 1], ALU.add).then_inc(att_ready, 1)

                for t in range(HALVES):
                    g = t // 8
                    pair = vb[:, 2 * (t % 2):2 * (t % 2) + 2, :]
                    pair4 = pair.rearrange("p d (b t) -> p d b t", b=4)
                    v.wait_ge(s0_set, q * HALVES + (t + 1))
                    v.tensor_tensor(pair4, pair4, kk[:, g:g + 1, :, 0:L].broadcast_to([P, 2, 4, L]), ALU.mult).then_inc(kv_ready, 1)
                    if t >= 2:
                        v.wait_ge(rs_ready, q * HALVES + (t - 1))
                    v.wait_ge(kv_ready, q * HALVES + (t + 1))
                    for d in range(2):
                        v.tensor_tensor_scan(state[t % 2][:, d, :], wd[:, g].rearrange("p b t -> p (b t)"), pair[:, d, :], 0.0,
                                             ALU.mult, ALU.add).then_inc(scanned, 1)
                    if t % 8 == 2 and t > 8:
                        add_bonus(g - 1)
                add_bonus(3)
                v.wait_ge(att_ready, q * 4 + 4)
                for c in range(EC):
                    v.wait_ge(mean_full, q * 4 + (c + 1))
                    v.tensor_tensor(vv[:, c, :, 1:L + 1], vv[:, c, :, 1:L + 1], quad3(pj[c % 2][:]), ALU.subtract).then_inc(cent_ready, 1)
                v.wait_ge(gstd_ready, q + 1)
                v.reciprocal(ew[:], ew[:]).then_inc(grstd_ready, 1)
                for c in range(EC):
                    v.wait_ge(unpacked, q * 4 + (c + 1))
                    link(v.tensor_tensor(quad3(xf[:, c, :]), vv[:, c, :, 1:L + 1], quad3(vb[:, c, :]), ALU.mult))
                    w, b_ = VEC["gn_w"] + c, VEC["gn_b"] + c
                    link(v.tensor_scalar(xf[:, c, :], xf[:, c, :], vec[:, w:w + 1], vec[:, b_:b_ + 1], ALU.mult, ALU.add))
                    v.tensor_tensor(xf[:, c, :], xf[:, c, :], gg[:, c, :], ALU.mult).then_inc(y_ready, 1)
                    if c > 0:
                        v.wait_ge(y_hi_ready, q * 4 + c)
                        v.tensor_tensor(x_lo[:, c - 1, :], xf[:, c - 1, :], x_hi[:, c - 1, :], ALU.subtract).then_inc(y_split_ready, 1)
                v.wait_ge(y_hi_ready, q * 4 + EC)
                v.tensor_tensor(x_lo[:, EC - 1, :], xf[:, EC - 1, :], x_hi[:, EC - 1, :], ALU.subtract).then_inc(y_split_ready, 1)
                v.wait_ge(y_split_ready, q * 4 + EC)
                norm(q + 1)
                v.wait_ge(res_in, q * 16 + 16)
                for b in range(4):
                    v.wait_ge(wo_full, q * 4 + (b + 1))
                    ins = v.tensor_tensor(rr[:, b, :], rr[:, b, :], wo_bank[b][:], ALU.add)
                    if b < 3:
                        link(ins)
                ins.then_inc(quad_done, 1)
                assert steps.n == DVE_STEPS

            v.wait_ge(ready, 4)
            norm(0)
            v.wait_ge(w_hi_ready, 2)
            v.tensor_tensor(lora1[1][:], raw_lora1, lora1[0][:], ALU.subtract).then_inc(w_ready, 1)
            v.tensor_tensor(dec1[1][:], raw_dec1, dec1[0][:], ALU.subtract).then_inc(w_ready, 1)
            split_w(0)
            v.wait_ge(first_in, 16 * len(FIRST))
            v.wait_ge(w_ready, 3)
            quad(0, True)
            with v.Fori(1, NQ) as q:
                quad(q, False)

        @block.tensor
        def _(pe):
            def quad(q, first):
                def mix(j, c):
                    if j >= J:
                        return
                    m, n = MIX[j], (j - 1) * 4 + c
                    if n >= 2:
                        pe.wait_ge(mx_free, q * 20 + (n - 1))
                    if m < 4:
                        lhs, rhs = lora2[32 * m:32 * m + 32, c * P:(c + 1) * P], h5[32 * m:32 * m + 32, :]
                    else:
                        lhs, rhs = lora2e[:, c * P:(c + 1) * P], h5e[:]
                    pe.matmul(mx[n % 2][:], lhs, rhs, start=True, stop=True).then_inc(mx_full, 1)

                def stage(j, c):
                    start, last = c == 0, c == EC - 1
                    if first and start:
                        pe.wait_ge(w_ready, 2 if j < 2 else j + 1)
                    pe.wait_ge(split_ready, q * (4 * J) + (4 * j + c + 1))
                    x = (x_hi[:, c, :], x_lo[:, c, :])
                    if j == 0:
                        for k, rows in ((0, P), (1, LORA)):
                            ins = mm3(pe, pj[k][0:rows, :], [t[:, c, k * P:k * P + rows] for t in lora1], x, start, last)
                            if last:
                                ins.then_inc(pj_full, 1)
                    elif j == 1:
                        if start:
                            pe.wait_ge(pj_free, q * 7 + 1)
                        ins = mm3(pe, pj[0][0:64, :], [t[:, c, :] for t in dec1], x, start, last)
                        if last:
                            ins.then_inc(pj_full, 1)
                    else:
                        for f in range(EC):
                            if start and j > 2:
                                pe.wait_ge(f_free, q * 16 + ((j - 3) * 4 + f + 1))
                            ins = mm3(pe, vb[:, f, :], [t[:, j - 2, c, f * P:(f + 1) * P] for t in (w_hi, w_lo)], x, start, last)
                            if last:
                                ins.then_inc(f_full, 1)
                    if not last:
                        ins.then_inc(x_used, 1)

                def decay(f):
                    pe.wait_ge(pj_free, q * 7 + (3 if f == 0 else 3 + f - 1))
                    pe.matmul(pj[(3 + f) % 2][:], dec2[:, f * P:(f + 1) * P], dh[:], start=True, stop=True).then_inc(pj_full, 1)

                for b in range(4):
                    pe.wait_ge(xn0_ready, q * 4 + (b + 1))
                    for c in range(EC):
                        ins = pe.transpose(vb[:, c, b * P:(b + 1) * P], xf[:, b, c * P:(c + 1) * P], ident[:])
                        if b == 3:
                            ins.then_inc(xnT_full, 1)
                if first:
                    pe.wait_ge(const_in, N_CONST)
                for c in range(EC):
                    stage(0, c)
                pe.wait_ge(pj_free, q * 7 + 1)
                for c in range(EC):
                    mix(1, c)
                for j in range(1, J):
                    if MIX[j + 1 if j + 1 < J else j] == 4:
                        pe.wait_ge(pj_free, q * 7 + 2)
                    mix(j + 1, 0)
                    mix(j + 1, 1)
                    stage(j, 0)
                    if j == 2:
                        decay(0)
                    mix(j + 1, 2)
                    stage(j, 1)
                    if j == 2:
                        decay(1)
                    mix(j + 1, 3)
                    for c in (2, 3):
                        stage(j, c)
                        if j == 2:
                            decay(c)
                for c in range(EC):
                    pe.wait_ge(ruk_ready, q * 4 + (c + 1))
                    if c < 2:
                        pe.wait_ge(pj_free, q * 7 + 7)
                    else:
                        pe.wait_ge(bonus_used, q * 4 + (c - 1))
                    pe.matmul(pj[c % 2][:], head_sum[:], sx[:, c, :], start=True, stop=True).then_inc(bonus_full, 1)

                def spread(t):
                    if t >= HALVES:
                        return
                    g = t // 8
                    pe.wait_ge(v_split_ready, q * 4 + (g + 1))
                    if t >= 2:
                        pe.wait_ge(scanned, q * (2 * HALVES) + 2 * (t - 1))
                    for e in range(2):
                        d = 2 * (t % 8) + e
                        pe.matmul(vb[:, 2 * (t % 2) + e, :], spread_v[:, d, :], x_hi[:, g, :], start=True, stop=False)
                        ins = pe.matmul(vb[:, 2 * (t % 2) + e, :], spread_v[:, d, :], x_lo[:, g, :], start=False, stop=True)
                    ins.then_inc(vb_full, 1)

                def accumulate(t):
                    g = t // 8
                    if t % 8 == 0 and g >= 2:
                        pe.wait_ge(att_ready, q * 4 + (g - 1))
                    pe.wait_ge(rs_ready, q * HALVES + (t + 1))
                    for e in range(2):
                        d = 2 * (t % 8) + e
                        ins = pe.matmul(mx[g % 2][:], pick_k[:, HS - 1 - d:HS - 1 - d + P], prod[t % 4][:, e, :], start=d == 0, stop=d == 15)
                    ins.then_inc(rs_used, 1)
                    if t % 8 == 7:
                        pe.wait_ge(rs_used, q * HALVES + (t + 1))
                        pe.nop().then_inc(acc_full, 1)

                pe.wait_ge(f_free, q * 16 + 16)
                if first:
                    pe.wait_ge(w_hi_ready, 4)
                    pe.wait_ge(w_ready, 7)
                spread(0)
                spread(1)
                for t in range(HALVES):
                    spread(t + 2)
                    if t >= 1:
                        accumulate(t - 1)
                accumulate(HALVES - 1)
                for c in range(EC):
                    pe.wait_ge(att_ready, q * 4 + (c + 1))
                    if c >= 2:
                        pe.wait_ge(cent_ready, q * 4 + (c - 1))
                    pe.matmul(pj[c % 2][:], head_mean[:], vv[:, c, :, 1:L + 1], start=True, stop=True).then_inc(mean_full, 1)
                for c in range(EC):
                    pe.wait_ge(sq_ready, q * 4 + (c + 1))
                    ins = pe.matmul(mx[0][32 * c:32 * c + 32, :], head_mean4[:], xf[:, c, :], start=True, stop=True)
                ins.then_inc(var_full, 1)
                pe.wait_ge(grstd_ready, q + 1)
                for c in range(EC):
                    pe.matmul(vb[:, c, :], unpack[:, c, :], ew[:], start=True, stop=True).then_inc(unpacked, 1)
                for c in range(EC):
                    pe.wait_ge(y_split_ready, q * 4 + (c + 1))
                    for b in range(4):
                        ins = mm3(pe, wo_bank[b][:], (x_hi[:, c, b * P:(b + 1) * P], x_lo[:, c, b * P:(b + 1) * P]),
                                  (w_hi[:, 4, c, :], w_lo[:, 4, c, :]), c == 0, c == EC - 1)
                        if c == EC - 1:
                            ins.then_inc(wo_full, 1)

            pe.wait_ge(first_in, 16 * len(FIRST))
            quad(0, True)
            with pe.Fori(1, NQ) as q:
                quad(q, False)

def channel_mix(nc, io, x2, x3):
    with ExitStack() as ctx:
        def sb(n, s, d=F32):
            return ctx.enter_context(nc.sbuf_tensor("cm_" + n, s, d))

        def ps(n, s):
            return ctx.enter_context(nc.psum_tensor("cm_" + n, s, F32))

        def sem(n):
            return ctx.enter_context(nc.semaphore("cm_" + n))

        vec = sb("vec", [P, NV])
        ident = sb("ident", [P, P])
        prev = sb("prev", [P, EC, B])
        eps = sb("eps", [P, 1])
        rest = sb("rest", [1, 1])
        w_hi = sb("w_hi", [P, 3, EC, E], FR)
        w_lo = sb("w_lo", [P, 3, EC, E], FR)
        xq = sb("xq", [P, 4, E])
        xres = sb("xres", [P, 4, E])
        stats = sb("stats", [P, 4, 6])
        mv = sb("mv", [P, 4, 2])
        std = sb("std", [P, 4])
        rstd = sb("rstd", [P, 4])
        lnx = sb("lnx", [P, 4, E])
        xn = sb("xn", [P, EC, 4, L + 1])
        sx = sb("sx", [P, EC, QT])
        xf = [sb("xk", [P, EC, QT]), sb("xr", [P, EC, QT])]
        x_hi = [sb("xk_hi", [P, EC, QT], FR), sb("xr_hi", [P, EC, QT], FR)]
        x_lo = [sb("xk_lo", [P, EC, QT], FR), sb("xr_lo", [P, EC, QT], FR)]
        relu = sb("relu", [P, EC, QT])
        k2_hi = sb("k2_hi", [P, EC, QT], FR)
        k2_lo = sb("k2_lo", [P, EC, QT], FR)
        gate = sb("gate", [P, 4, E])
        gy = sb("gy", [P, 4, E])
        tr = ps("tr", [P, 4, QT])
        mm = ps("mm", [P, 4, QT])

        const_in, w_in, w_hi_ready, w_ready = sem("const_in"), [sem("w_in%d" % j) for j in range(3)], sem("w_hi_ready"), sem("w_ready")
        x_in, res_in, x3_out, added, ready = sem("x_in"), sem("res_in"), sem("x3_out"), sem("added"), sem("ready")
        bn_done, stats_ready, std_ready, xn0_ready = sem("bn_done"), sem("stats_ready"), sem("std_ready"), sem("xn0_ready")
        ln_step, xnT_full, xn_ready, prev_ready = sem("ln_step"), sem("xnT_full"), sem("xn_ready"), sem("prev_ready")
        sx_ready, xf_ready, hi_ready, split_ready = sem("sx_ready"), sem("xf_ready"), sem("hi_ready"), sem("split_ready")
        k_full, r_full, y_full, relu_ready = sem("k_full"), sem("r_full"), sem("y_full"), sem("relu_ready")
        k2_ready, k2_hi_ready, k2_split_ready = sem("k2_ready"), sem("k2_hi_ready"), sem("k2_split_ready")
        gate_ready, gated = sem("gate_ready"), sem("gated")
        raw = [gate, relu, gy]
        block = ctx.enter_context(nc.Block())


        @block.sync
        def _(sp):
            sp.dma_start(xq[:], x2[0:4].rearrange("b t e -> t b e")).then_inc(x_in, 16)
            for tile, name in ((vec, "vec"), (ident, "ident"), (prev, "prev0")):
                sp.dma_start(tile[:], io[name]).then_inc(const_in, 16)
            for j in range(3):
                sp.dma_start(raw[j][:], io["l0w"][5 + j]).then_inc(w_in[j], 16)

            def load_and_store(q, more):
                if more:
                    sp.wait_ge(xn0_ready, q * 4 + 4)
                    sp.dma_start(xq[:], x2[bass.ds(q * 4 + 4, 4)].rearrange("b t e -> t b e")).then_inc(x_in, 16)
                sp.wait_ge(x3_out, q * 16 + 16)
                sp.dma_start(xres[:], x2[bass.ds(q * 4, 4)].rearrange("b t e -> t b e")).then_inc(res_in, 16)
                sp.wait_ge(added, q * 4 + 4)
                sp.dma_start(x3[bass.ds(q * 4, 4)].rearrange("b t e -> t b e"), xres[:]).then_inc(x3_out, 16)

            with sp.Fori(0, NQ - 1) as q:
                load_and_store(q, True)
            load_and_store(NQ - 1, False)
            sp.wait_ge(x3_out, NQ * 16 + 16)

        @block.gpsimd
        def _(gp):
            gp.memset(eps[:], EPS).then_inc(ready, 1)
            gp.memset(rest[:], 0.0).then_inc(x3_out, 16)

        @block.scalar
        def _(act):
            def split_w(j):
                act.wait_ge(w_in[j], 16)
                act.activation(w_hi[:, j], raw[j][:], ACT.Copy).then_inc(w_hi_ready, 1)

            def roots(q):
                act.wait_ge(stats_ready, q + 1)
                act.activation(std[:, :], mv[:, :, 1], ACT.Sqrt, bias=eps[:]).then_inc(std_ready, 1)

            def normalised(q):
                act.wait_ge(xnT_full, q + 1)
                for c in range(EC):
                    act.activation(xn[:, c, :, 1:L + 1], tr[:, c, :].rearrange("p (b t) -> p b t", b=4), ACT.Identity,
                                   bias=vec[:, VEC["ln2_b"] + c:VEC["ln2_b"] + c + 1],
                                   scale=vec[:, VEC["ln2_w"] + c:VEC["ln2_w"] + c + 1]).then_inc(xn_ready, 1)

            def mix_hi(q, j):
                for c in range(EC):
                    act.wait_ge(xf_ready, q * 8 + (4 * j + c + 1))
                    act.activation(x_hi[j][:, c, :], xf[j][:, c, :], ACT.Copy).then_inc(hi_ready, 1)

            def square(q):
                for c in range(EC):
                    act.wait_ge(k_full, q * 4 + (c + 1))
                    act.activation(relu[:, c, :], mm[:, c, :], ACT.Relu).then_inc(relu_ready, 1)
                for c in range(EC):
                    act.wait_ge(k2_ready, q * 4 + (c + 1))
                    act.activation(k2_hi[:, c, :], xf[0][:, c, :], ACT.Copy).then_inc(k2_hi_ready, 1)

            def gates(q):
                for b in range(4):
                    act.wait_ge(r_full, q * 4 + (b + 1))
                    act.activation(gate[:, b, :], tr[:, b, :], ACT.Sigmoid).then_inc(gate_ready, 1)

            split_w(0)
            act.wait_ge(ready, 1)
            roots(0)
            act.wait_ge(const_in, 48)
            normalised(0)
            mix_hi(0, 0)
            split_w(1)
            mix_hi(0, 1)
            split_w(2)
            act.wait_ge(w_ready, 3)
            with act.Fori(0, NQ - 1) as q:
                roots(q + 1)
                square(q)
                gates(q)
                normalised(q + 1)
                mix_hi(q + 1, 0)
                mix_hi(q + 1, 1)
            square(NQ - 1)
            gates(NQ - 1)

        @block.vector
        def _(v):
            def split_w(j):
                v.wait_ge(w_hi_ready, j + 1)
                v.tensor_tensor(w_lo[:, j], raw[j][:], w_hi[:, j], ALU.subtract).then_inc(w_ready, 1)

            def link(q):
                def step(ins):
                    ins.then_inc(ln_step, 1)
                    v.wait_ge(ln_step, q + 1)
                return step

            def norm(q):
                v.wait_ge(x_in, q * 16 + 16)
                layernorm_dve(v, xq, lnx, stats, mv, std, rstd, bn_done, stats_ready, std_ready, xn0_ready, q, link(q))

            def shift(q):
                v.tensor_copy(xn[:, :, :, 0], prev[:, :, bass.ds(q * 4, 4)]).then_inc(prev_ready, 1)
                v.wait_ge(prev_ready, q + 1)
                for c in range(EC):
                    v.wait_ge(xn_ready, q * 4 + (c + 1))
                    v.tensor_tensor(sx[:, c, :].rearrange("p (b t) -> p b t", b=4), xn[:, c, :, 0:L],
                                    xn[:, c, :, 1:L + 1], ALU.subtract).then_inc(sx_ready, 1)

            def mix(q, j, name):
                for c in range(EC):
                    v.wait_ge(sx_ready, q * 4 + (c + 1))
                    m = VEC[name] + c
                    v.scalar_tensor_tensor(out=xf[j][:, c, :].rearrange("p (b t) -> p b t", b=4),
                                           in0=sx[:, c, :].rearrange("p (b t) -> p b t", b=4), scalar=vec[:, m:m + 1],
                                           in1=xn[:, c, :, 1:L + 1], op0=ALU.mult, op1=ALU.add).then_inc(xf_ready, 1)
                for c in range(EC):
                    v.wait_ge(hi_ready, q * 8 + (4 * j + c + 1))
                    v.tensor_tensor(x_lo[j][:, c, :], xf[j][:, c, :], x_hi[j][:, c, :], ALU.subtract).then_inc(split_ready, 1)

            def square(q):
                for c in range(EC):
                    v.wait_ge(relu_ready, q * 4 + (c + 1))
                    v.tensor_tensor(xf[0][:, c, :], relu[:, c, :], relu[:, c, :], ALU.mult).then_inc(k2_ready, 1)
                for c in range(EC):
                    v.wait_ge(k2_hi_ready, q * 4 + (c + 1))
                    v.tensor_tensor(k2_lo[:, c, :], xf[0][:, c, :], k2_hi[:, c, :], ALU.subtract).then_inc(k2_split_ready, 1)

            def add(q):
                v.wait_ge(res_in, q * 16 + 16)
                for b in range(4):
                    v.wait_ge(gate_ready, q * 4 + (b + 1))
                    v.wait_ge(y_full, q * 4 + (b + 1))
                    v.tensor_tensor(gy[:, b, :], gate[:, b, :], mm[:, b, :], ALU.mult).then_inc(gated, 1)
                    v.wait_ge(gated, q * 4 + (b + 1))
                    v.tensor_tensor(xres[:, b, :], xres[:, b, :], gy[:, b, :], ALU.add).then_inc(added, 1)

            v.memset(std[:], 1.0)
            norm(0)
            split_w(0)
            v.wait_ge(const_in, 48)
            shift(0)
            mix(0, 0, "ffn_maa_k")
            split_w(1)
            mix(0, 1, "ffn_maa_r")
            split_w(2)
            with v.Fori(0, NQ - 1) as q:
                v.wait_ge(xnT_full, q + 1)
                norm(q + 1)
                square(q)
                shift(q + 1)
                v.wait_ge(k2_split_ready, q * 4 + 4)
                mix(q + 1, 0, "ffn_maa_k")
                add(q)
                mix(q + 1, 1, "ffn_maa_r")
            square(NQ - 1)
            add(NQ - 1)

        @block.tensor
        def _(pe):
            def transpose(q):
                for b in range(4):
                    pe.wait_ge(xn0_ready, q * 4 + (b + 1))
                    for c in range(EC):
                        ins = pe.transpose(tr[:, c, b * P:(b + 1) * P], lnx[:, b, c * P:(c + 1) * P], ident[:])
                ins.then_inc(xnT_full, 1)

            def keys(q, read=None):
                for f in range(EC):
                    if read is not None:
                        pe.wait_ge(gated, read + (f + 1))
                    for c in range(EC):
                        pe.wait_ge(split_ready, q * 8 + (c + 1))
                        ins = mm3(pe, mm[:, f, :], (w_hi[:, 0, c, f * P:(f + 1) * P], w_lo[:, 0, c, f * P:(f + 1) * P]),
                                  (x_hi[0][:, c, :], x_lo[0][:, c, :]), c == 0, c == EC - 1)
                    ins.then_inc(k_full, 1)

            def receptances(q):
                for b in range(4):
                    for c in range(EC):
                        pe.wait_ge(split_ready, q * 8 + (4 + c + 1))
                        ins = mm3(pe, tr[:, b, :], (x_hi[1][:, c, b * P:(b + 1) * P], x_lo[1][:, c, b * P:(b + 1) * P]),
                                  (w_hi[:, 1, c, :], w_lo[:, 1, c, :]), c == 0, c == EC - 1)
                    ins.then_inc(r_full, 1)

            def values(q):
                for b in range(4):
                    for c in range(EC):
                        pe.wait_ge(k2_split_ready, q * 4 + (c + 1 if b == 0 else 4))
                        ins = mm3(pe, mm[:, b, :], (k2_hi[:, c, b * P:(b + 1) * P], k2_lo[:, c, b * P:(b + 1) * P]),
                                  (w_hi[:, 2, c, :], w_lo[:, 2, c, :]), c == 0, c == EC - 1)
                    ins.then_inc(y_full, 1)

            pe.wait_ge(const_in, 48)
            transpose(0)
            pe.wait_ge(xn_ready, 4)
            pe.wait_ge(w_ready, 1)
            keys(0)
            with pe.Fori(0, NQ - 1) as q:
                pe.wait_ge(w_ready, 2)
                receptances(q)
                pe.wait_ge(gate_ready, q * 4 + 4)
                transpose(q + 1)
                pe.wait_ge(w_ready, 3)
                values(q)
                keys(q + 1, q * 4)
            receptances(NQ - 1)
            values(NQ - 1)


def cross_attend(nc, io, x3, out):
    HT = 8
    G = NH // 2
    RING = 2
    STAGE = 6 * 16 + 4 * 16 + HT + 2
    HALF = 2 * STAGE + 4 * 16
    KW = L + 2
    BANK_TR, BANK_SC, BANK_PV, BANK_BV = 2, 4, 6, 7
    LN_BANKS = (2, 3, 6, 7)
    ORDER = (0, 1, 2, 3, 4, 5)
    ORDER_FIRST = (1, 3, 4, 5, 0, 2)
    HV = {"bq": 0, "bk": 1, "bv": 2, "bias_k": 3, "bias_v": 4}
    with ExitStack() as ctx:
        def sb(n, s, d=F32):
            return ctx.enter_context(nc.sbuf_tensor("ca_" + n, s, d))

        def two(n, s):
            return (sb(n + "_hi", s, FR), sb(n + "_lo", s, FR))

        def sem(n):
            return ctx.enter_context(nc.semaphore("ca_" + n))

        vec = sb("vec", [P, NV])
        hv = sb("hv", [P, 11 * NH])
        ident = sb("ident", [P, P])
        eps = sb("eps", [P, 1])
        bo = sb("bo", [P, 3, E])
        bias_k = two("bias_k", [P, 2 * NH])
        c2 = two("ctx", [P, EC, HT * L])
        h2 = two("h", [P, EC, HT * L])
        xres = sb("xres", [P, HT, E])
        lt = sb("lt", [P, 4, E])
        lh = sb("lh", [P, EC, QT])
        stats = sb("stats", [P, 4, 6])
        mv = sb("mv", [P, 4, 2])
        std = sb("std", [P, 4])
        rstd = sb("rstd", [P, 4])
        sq, sk, sv = sb("sq", [P, EC, 256]), sb("sk", [P, EC, 256]), sb("sv", [P, EC, 256])
        so = sb("so", [P, 2, E])
        gelu = sk[:].rearrange("p (k a) m -> p k (a m)", k=2)
        wq, wk, wv = two("wq", [P, EC, 256]), two("wk", [P, EC, 256]), two("wv", [P, EC, 256])
        wo = two("wo", [P, 2, E])
        qT = [two("q%d" % i, [P, QT]) for i in range(2)]
        kT = [two("k%d" % i, [P, 4, KW]) for i in range(2)]
        vT = two("v", [P, 4, 256])
        pr = [sb("pr%d" % i, [P, 4, KW]) for i in range(2)]
        pT = [two("pt%d" % i, [P, QT]) for i in range(2)]
        cT = [two("ct%d" % i, [P, QT]) for i in range(2)]
        mxs = [sb("mx%d" % i, [P, 4]) for i in range(2)]
        nbs = [sb("nb%d" % i, [P, 4]) for i in range(2)]
        sms = [sb("sm%d" % i, [P, 4]) for i in range(2)]
        rss = [sb("rs%d" % i, [P, 4]) for i in range(2)]
        pb = sb("pb", [P, HT, NH])
        dbias = sb("dbias", [P, NH, NH])
        db = two("db", [P, 2, NH])
        bvs = sb("bvs", [NH, E])
        pbT = sb("pbT", [NH, HT * L])
        ps = ctx.enter_context(nc.psum_tensor("ca_ps", [P, 8, QT], F32))

        const_in, ready, bk_hi, bk_split = sem("const_in"), sem("ready"), sem("bk_hi"), sem("bk_split")
        x_in, c_in, out_done = [[sem("%s%d" % (n, quad)) for quad in range(2)] for n in ("x_in", "c_in", "out_done")]
        c_hi, c_split = sem("c_hi"), sem("c_split")
        wq_in, wk_in, wv_in, wo_in = sem("wq_in"), sem("wk_in"), sem("wv_in"), sem("wo_in")
        wq_hi, wk_hi, wv_hi, wo_hi = sem("wq_hi"), sem("wk_hi"), sem("wv_hi"), sem("wo_hi")
        wq_split, wk_split, wv_split, wo_split = sem("wq_split"), sem("wk_split"), sem("wv_split"), sem("wo_split")
        bn_done, stats_ready, std_ready, xn0_ready = sem("bn_done"), sem("stats_ready"), sem("std_ready"), sem("xn0_ready")
        ln_step, lnT_full, lh_ready, h_hi, h_split = sem("ln_step"), sem("lnT_full"), sem("lh_ready"), sem("h_hi"), sem("h_split")
        lh_act, bo_in = sem("lh_act"), sem("bo_in")
        bo_added, dbias_ready = sem("bo_added"), sem("dbias_ready")
        ring_full, evacuated, p_hi = sem("ring_full"), sem("evacuated"), sem("p_hi")
        sc_full, mx_done, max_done, exp_done = sem("sc_full"), sem("mx_done"), sem("max_done"), sem("exp_done")
        rs_done, norm_done = sem("rs_done"), sem("norm_done")
        tr_full, pt_hi, pt_split = sem("tr_full"), sem("pt_hi"), sem("pt_split")
        pv_full, ct_hi, ct_split = sem("pv_full"), sem("ct_hi"), sem("ct_split")
        act_waited = sem("act_waited")
        db_hi, db_ready, bvs_ready = sem("db_hi"), sem("db_ready"), sem("bvs_ready")
        fc1_full, gelu_ready, u_hi, u_split = sem("fc1_full"), sem("gelu_ready"), sem("u_hi"), sem("u_split")

        class Slot:

            def __init__(self, h, st, g, quad, proj=True, attn=True):
                self.h, self.st, self.g, self.quad, self.proj, self.attn = h, st, g, quad, proj, attn
                s = g * 2 + quad
                self.s = s
                self.n = h * 32 + (st * 16 + s)
                self.gu = g if quad else g - 1
                self.qu = 1 - quad
                self.ring = h * HALF + (st * STAGE + s * 10 - (4 if attn else 0))
                self.projected = self.ring - (0 if isinstance(g, int) and s <= 1 else 4)
                self.out0 = self.ring + (6 if proj else 5)
                self.odd = 0 if proj else 1
                self.order = ORDER if attn else ORDER_FIRST
                self.gq = h * 24 + (st * 8 + g)
                self.gk = h * 16 + (st * 8 + g)

        def attention_slots(engine, h, st, first_slot, slot, last_slot):
            first_slot(Slot(h, st, 0, 0, attn=False))
            slot(Slot(h, st, 0, 1))
            with engine.Fori(1, G) as g:
                slot(Slot(h, st, g, 0))
                slot(Slot(h, st, g, 1))
            last_slot(Slot(h, st, G, 0, proj=False))

        class MlpSlot:
            def __init__(self, h, g, quad, proj=True, outp=True):
                self.h, self.g, self.quad, self.proj, self.outp = h, g, quad, proj, outp
                s = g * 2 + quad
                self.n = h * 16 + s
                self.out0 = h * HALF + (2 * STAGE + s * 4 - 4)
                self.gq = h * 24 + (16 + g)
                self.u = pT if quad == 0 else cT
                self.u_last = cT if quad == 0 else pT

        def mlp_slots(engine, h, slot, second_norm, next_ctx):
            slot(MlpSlot(h, 0, 0, outp=False))
            second_norm()
            slot(MlpSlot(h, 0, 1))
            next_ctx(0)
            with engine.Fori(1, G) as g:
                slot(MlpSlot(h, g, 0))
                slot(MlpSlot(h, g, 1))
            next_ctx(1)
            slot(MlpSlot(h, G, 0, proj=False))

        def wait_apart(act):
            act.sem_inc(act_waited, 1)

        def head_col(st, kind, g, hd):
            return hv[:, bass.ds(g * 2 + ((st * 5 + HV[kind]) * NH + hd), 1)]

        block = ctx.enter_context(nc.Block())

        @block.sync
        def _(sp):
            sp.dma_start(lh[:], io["ctxT"][:, :, 0:QT]).then_inc(c_in[0], 16)
            sp.dma_start(sk[:], io["wk"][0]).then_inc(wk_in, 16)
            for tile, name in ((vec, "vec"), (ident, "ident"), (hv, "head_vec")):
                sp.dma_start(tile[:], io[name]).then_inc(const_in, 16)
            sp.dma_start(sv[:], io["wv"][0]).then_inc(wv_in, 16)
            sp.dma_start(lt[:], io["ctxT"][:, :, QT:2 * QT]).then_inc(c_in[1], 16)
            sp.dma_start(sq[:], io["wq"][0]).then_inc(wq_in, 16)
            sp.dma_start(bo[:], io["bo"]).then_inc(bo_in, 16)
            with sp.Fori(0, 2) as h:
                for quad in range(2):
                    sp.wait_ge(out_done[quad], h * 16 + 16)
                    sp.dma_start(xres[:, quad * 4:quad * 4 + 4, :],
                                 x3[bass.ds(h * HT + quad * 4, 4)].rearrange("b t e -> t b e")).then_inc(x_in[quad], 16)
                for st in range(2):
                    with sp.Fori(0, G) as g:
                        gq, gk = h * 24 + (st * 8 + g), h * 16 + (st * 8 + g)
                        sp.wait_ge(wv_split, gk + 1)
                        sp.dma_start(sv[:], io["wv"][bass.ds(g + (st * 8 + 1), 1)].rearrange("a p c m -> (a p) c m")).then_inc(wv_in, 16)
                        sp.wait_ge(wo_split, gq + 1)
                        sp.dma_start(so[:], io["wo"][bass.ds(g + st * 8, 1)].rearrange("a p c m -> (a p) c m")).then_inc(wo_in, 16)
                        sp.wait_ge(wq_split, (gq + 1) * 2)
                        sp.dma_start(sq[:], io["wq"][bass.ds(g + (st * 8 + 1), 1)].rearrange("a p c m -> (a p) c m")).then_inc(wq_in, 16)
                        sp.wait_ge(wk_split, gk + 1)
                        sp.dma_start(sk[:], io["wk"][bass.ds(g + (st * 8 + 1), 1)].rearrange("a p c m -> (a p) c m")).then_inc(wk_in, 16)

                def mlp_weights(g):
                    gq = h * 24 + (16 + g)
                    sp.wait_ge(wo_split, gq + 1)
                    sp.dma_start(so[:], io["wo"][bass.ds(g + 16, 1)].rearrange("a p c m -> (a p) c m")).then_inc(wo_in, 16)
                    sp.wait_ge(wq_split, (gq + 1) * 2)
                    sp.dma_start(sq[:], io["wq"][bass.ds(g + 17, 1)].rearrange("a p c m -> (a p) c m")).then_inc(wq_in, 16)

                def other_ctx(quad):
                    sp.dma_start(lh[:], io["ctxT"][:, :, bass.ds(h * (-HT * L) + (HT * L + quad * QT), QT)]).then_inc(c_in[quad], 16)

                mlp_weights(0)
                sp.wait_ge(h_split, h * 24 + 24)
                other_ctx(0)
                mlp_weights(1)
                sp.wait_ge(c_split, h * 2 + 3)
                other_ctx(1)
                with sp.Fori(2, G) as g:
                    mlp_weights(g)
                for quad in range(2):
                    sp.wait_ge(evacuated, h * HALF + (HALF + RING - 4 * (1 - quad)))
                    sp.dma_start(out[bass.ds(h * HT + quad * 4, 4)].rearrange("b t e -> t b e"),
                                 xres[:, quad * 4:quad * 4 + 4, :]).then_inc(out_done[quad], 16)
            for quad in range(2):
                sp.wait_ge(out_done[quad], 3 * 16)

        @block.gpsimd
        def _(gp):
            gp.memset(eps[:], EPS).then_inc(ready, 1)
            gp.memset(dbias[:], 0.0).then_inc(ready, 1)
            for hd in range(2):
                gp.memset(kT[hd][0][:, :, L + 1:KW].bitcast(F32), 0.0).then_inc(ready, 1)
                gp.memset(kT[hd][1][:, :, L + 1:KW].bitcast(F32), 0.0).then_inc(ready, 1)
            for s, n in ((out_done[0], 16), (out_done[1], 16), (wo_split, 1), (evacuated, RING), (exp_done, 1),
                         (ct_split, 1), (tr_full, 2)):
                gp.memset(pb[0:1, 0, 0:1], 0.0).then_inc(s, n)
                gp.drain()
            gp.wait_ge(bo_in, 16)
            with gp.Fori(0, 2) as h:
                for st in range(3):
                    for quad in range(2):
                        gp.wait_ge(xn0_ready, (h * 3 + st) * 8 + (quad * 4 + 4))
                        for b in range(quad * 4, quad * 4 + 4):
                            ins = gp.tensor_tensor(xres[:, b, :], xres[:, b, :], bo[:, st, :], ALU.add)
                        ins.then_inc(bo_added, 1)

        @block.scalar
        def _(act):
            def split_q(gq, k):
                act.wait_ge(wq_in, (gq + 1) * 16)
                act.activation(wq[0][:, :, k * P:(k + 1) * P], sq[:, :, k * P:(k + 1) * P], ACT.Copy).then_inc(wq_hi, 1)

            def split_one(w, raw, w_in, w_hi, g):
                act.wait_ge(w_in, (g + 1) * 16)
                act.activation(w[0][:], raw[:], ACT.Copy).then_inc(w_hi, 1)

            def project_hi(S, i):
                k = S.order[i]
                act.wait_ge(ring_full, S.ring + (i + 1))
                src = ps[:, i % RING, :]
                if k >= 4:
                    act.activation(vT[0][:, (k - 4) * 2:(k - 4) * 2 + 2, :].rearrange("p b m -> p (b m)"), src, ACT.Copy).then_inc(p_hi, 1)
                    return
                hd = k // 2
                wait_apart(act)
                if k % 2 == 0:
                    act.activation(qT[hd][0][:], src, ACT.Identity, bias=head_col(S.st, "bq", S.g, hd)).then_inc(p_hi, 1)
                else:
                    act.activation(kT[hd][0][:, :, 0:L], src.rearrange("p (b t) -> p b t", b=4), ACT.Identity,
                                   bias=head_col(S.st, "bk", S.g, hd)).then_inc(p_hi, 1)

            def exps(S, hd):
                act.wait_ge(max_done, S.n * 2 + (hd - 1))
                act.wait_ge(tr_full, S.n * 2 + (hd - 1))
                for b in range(4):
                    o = (b % 2) * KW
                    ins = act.activation(pr[hd][:, b, 0:L + 1], ps[:, BANK_SC + b // 2, o:o + L + 1], ACT.Exp,
                                         bias=nbs[hd][:, b:b + 1], scale=SCALE, accum_out=sms[hd][:, b:b + 1])
                ins.then_inc(exp_done, 1)

            def probs_hi(S, hd):
                act.wait_ge(tr_full, S.n * 2 + (hd - 1 + 2))
                act.activation(pT[hd][0][:], ps[:, BANK_TR + hd, :], ACT.Copy).then_inc(pt_hi, 1)

            def context_hi(S, hd):
                act.wait_ge(pv_full, S.n * 2 + (hd - 1))
                wait_apart(act)
                act.activation(cT[hd][0][:], ps[:, BANK_PV, :], ACT.Identity, bias=head_col(S.st, "bv", S.gu, hd)).then_inc(ct_hi, 1)

            def roots(j, quad):
                act.wait_ge(stats_ready, j * 2 + (quad + 1))
                act.activation(std[:, :], mv[:, :, 1], ACT.Sqrt, bias=eps[:]).then_inc(std_ready, 1)

            def h_his(st, j, quad):
                act.wait_ge(lnT_full, j * 2 + (quad + 1))
                if quad == 1:
                    act.wait_ge(h_split, j * 8 + 4)
                for c in (2, 3):
                    w, b_ = VEC["s%d" % (st + 1)] + c, VEC["o%d" % (st + 1)] + c
                    act.activation(lh[:, c, :], ps[:, LN_BANKS[c], :], ACT.Identity, bias=vec[:, b_:b_ + 1],
                                   scale=vec[:, w:w + 1]).then_inc(lh_act, 1)
                for c in range(EC):
                    if c < 2:
                        act.wait_ge(lh_ready, j * 4 + (quad * 2 + c + 1))
                    else:
                        act.wait_ge(lh_act, j * 4 + (quad * 2 + c - 1))
                    act.activation(h2[0][:, c, quad * QT:(quad + 1) * QT], lh[:, c, :], ACT.Copy).then_inc(h_hi, 1)

            def ctx_hi(quad, tile, n):
                act.wait_ge(c_in[quad], n * 16 + 16)
                act.activation(c2[0][:, :, quad * QT:(quad + 1) * QT], tile[:], ACT.Copy).then_inc(c_hi, 1)

            def first_slot(S):
                j = S.h * 3 + S.st
                if S.st > 0:
                    h_his(S.st, j, 0)
                project_hi(S, 0)
                split_one(wv, sv, wv_in, wv_hi, S.gk)
                project_hi(S, 1)
                if S.st > 0:
                    roots(j, 1)
                project_hi(S, 2)
                project_hi(S, 3)
                if S.st == 0:
                    roots(j, 0)
                    roots(j, 1)
                    h_his(S.st, j, 0)
                project_hi(S, 4)
                h_his(S.st, j, 1)
                project_hi(S, 5)

            def last_slot(S):
                act.wait_ge(ring_full, S.ring)
                exps(S, 0)
                act.activation(bvs[:], ps[0:NH, BANK_BV, :], ACT.Copy).then_inc(bvs_ready, 1)
                exps(S, 1)
                probs_hi(S, 0)
                probs_hi(S, 1)
                roots(S.h * 3 + (S.st + 1), 0)
                context_hi(S, 0)
                context_hi(S, 1)

            def slot(S):
                act.wait_ge(ring_full, S.ring)
                exps(S, 0)
                project_hi(S, 0)
                if S.quad == 0:
                    split_one(wv, sv, wv_in, wv_hi, S.gk)
                else:
                    split_one(wo, so, wo_in, wo_hi, S.gq)
                exps(S, 1)
                project_hi(S, 1)
                probs_hi(S, 0)
                project_hi(S, 2)
                if S.quad == 1:
                    split_q(S.gq + 1, 0)
                probs_hi(S, 1)
                context_hi(S, 0)
                project_hi(S, 3)
                if S.quad == 1:
                    split_q(S.gq + 1, 1)
                context_hi(S, 1)
                project_hi(S, 4)
                if S.quad == 1:
                    split_one(wk, sk, wk_in, wk_hi, S.gk + 1)
                project_hi(S, 5)

            def mlp_slot(S):
                if S.outp:
                    act.wait_ge(ring_full, S.out0)
                if S.proj and S.quad == 1:
                    split_one(wo, so, wo_in, wo_hi, S.gq)
                if S.proj:
                    for k in range(2):
                        act.wait_ge(fc1_full, S.n * 2 + (k + 1))
                        act.wait_ge(u_split, S.n * 2 + (k + 1))
                        wait_apart(act)
                        act.activation(gelu[:, k, :], ps[:, BANK_SC + k, :], ACT.Gelu,
                                       bias=hv[:, bass.ds(S.g * 2 + (10 * NH + k), 1)]).then_inc(gelu_ready, 1)
                        if S.quad == 1:
                            split_q(S.gq + 1, k)
                        act.wait_ge(gelu_ready, S.n * 2 + (k + 1))
                        act.activation(S.u[k][0][:], gelu[:, k, :], ACT.Copy).then_inc(u_hi, 1)

            split_one(wk, sk, wk_in, wk_hi, 0)
            ctx_hi(0, lh, 0)
            act.wait_ge(const_in, 48)
            act.activation(bias_k[0][:].rearrange("p (s h) -> p s h", s=2),
                           hv[:, 0:10 * NH].rearrange("p (s k h) -> p s k h", s=2, k=5)[:, :, HV["bias_k"], :], ACT.Copy).then_inc(bk_hi, 1)
            act.wait_ge(ready, 6)
            ctx_hi(1, lt, 0)
            split_q(0, 0)
            split_q(0, 1)
            with act.Fori(0, 2) as h:
                for st in range(2):
                    attention_slots(act, h, st, first_slot, slot, last_slot)
                h_his(2, h * 3 + 2, 0)
                roots(h * 3 + 2, 1)
                mlp_slots(act, h, mlp_slot, lambda: h_his(2, h * 3 + 2, 1), lambda quad: ctx_hi(quad, lh, h + 1))

        @block.vector
        def _(v):
            def split_q(gq, k):
                v.wait_ge(wq_hi, gq * 2 + (k + 1))
                v.tensor_tensor(wq[1][:, :, k * P:(k + 1) * P], sq[:, :, k * P:(k + 1) * P], wq[0][:, :, k * P:(k + 1) * P],
                                ALU.subtract).then_inc(wq_split, 1)

            def split_one(w, raw, w_hi, w_split, g):
                v.wait_ge(w_hi, g + 1)
                v.tensor_tensor(w[1][:], raw[:], w[0][:], ALU.subtract).then_inc(w_split, 1)

            def add_output(idx, b, bank):
                v.wait_ge(ring_full, idx + 1)
                v.tensor_tensor(xres[:, b, :], xres[:, b, :], ps[:, bank, :], ALU.add).then_inc(evacuated, 1)

            def project_lo(S, i):
                k = S.order[i]
                v.wait_ge(p_hi, S.n * 6 + (i + 1))
                src = ps[:, i % RING, :]
                if k >= 4:
                    tiles = [t[:, (k - 4) * 2:(k - 4) * 2 + 2, :].rearrange("p b m -> p (b m)") for t in vT]
                    v.tensor_tensor(tiles[1], src, tiles[0], ALU.subtract).then_inc(evacuated, 1)
                    return
                hd = k // 2
                if k % 2 == 0:
                    v.scalar_tensor_tensor(out=qT[hd][1][:], in0=src, scalar=head_col(S.st, "bq", S.g, hd),
                                           in1=qT[hd][0][:], op0=ALU.add, op1=ALU.subtract).then_inc(evacuated, 1)
                else:
                    for t in range(2):
                        v.tensor_scalar(kT[hd][t][:, :, L:L + 1],
                                        bias_k[t][:, bass.ds(S.g * 2 + (S.st * NH + hd), 1)].rearrange("p (a b) -> p a b", b=1).broadcast_to([P, 4, 1]),
                                        1.0, None, ALU.mult)
                    v.scalar_tensor_tensor(out=kT[hd][1][:, :, 0:L], in0=src.rearrange("p (b t) -> p b t", b=4),
                                           scalar=head_col(S.st, "bk", S.g, hd), in1=kT[hd][0][:, :, 0:L],
                                           op0=ALU.add, op1=ALU.subtract).then_inc(evacuated, 1)

            def row_max(S, hd):
                v.wait_ge(sc_full, S.n * 2 + (hd - 1))
                sc = ps[:, BANK_SC:BANK_SC + 2, 0:2 * KW].rearrange("p a (b k) -> p a b k", b=2)[:, :, :, 0:L + 1]
                v.tensor_reduce(mxs[hd][:].rearrange("p (a b) -> p a b", a=2), sc, AX, ALU.max).then_inc(mx_done, 1)
                v.wait_ge(mx_done, S.n * 2 + (hd - 1))
                v.tensor_scalar(nbs[hd][:], mxs[hd][:], -SCALE, None, ALU.mult).then_inc(max_done, 1)

            def normalise(S, hd):
                v.wait_ge(exp_done, S.n * 2 + (hd - 1 + 1))
                v.reciprocal(rss[hd][:], sms[hd][:]).then_inc(rs_done, 1)
                v.wait_ge(rs_done, S.n * 2 + (hd - 1))
                v.tensor_tensor(pr[hd][:, :, 0:L + 1], pr[hd][:, :, 0:L + 1],
                                rss[hd][:].rearrange("p (a b) -> p a b", b=1).broadcast_to([P, 4, L + 1]), ALU.mult).then_inc(norm_done, 1)
                v.wait_ge(norm_done, S.n * 2 + (hd - 1))
                v.tensor_scalar(pb[:, S.qu * 4:S.qu * 4 + 4, bass.ds(S.gu * 2 + hd, 1)], pr[hd][:, :, L:L + 1], 1.0, None,
                                ALU.mult)

            def probs_lo(S, hd):
                v.wait_ge(pt_hi, S.n * 2 + (hd - 1))
                v.tensor_tensor(pT[hd][1][:], ps[:, BANK_TR + hd, :], pT[hd][0][:], ALU.subtract).then_inc(pt_split, 1)

            def context_lo(S, hd):
                v.wait_ge(ct_hi, S.n * 2 + (hd - 1))
                v.scalar_tensor_tensor(out=cT[hd][1][:], in0=ps[:, BANK_PV, :], scalar=head_col(S.st, "bv", S.gu, hd),
                                       in1=cT[hd][0][:], op0=ALU.add, op1=ALU.subtract).then_inc(ct_split, 1)

            def ln_stats(j, quad):
                layernorm_stats(v, xres[:, quad * 4:quad * 4 + 4, :], stats, mv, rstd, bn_done, stats_ready, j * 2 + quad)

            def ln_roots(j, quad):
                v.wait_ge(std_ready, j * 2 + (quad + 1))
                v.reciprocal(rstd[:, :], std[:, :]).then_inc(ln_step, 1)
                v.wait_ge(ln_step, j * 2 + (quad + 1))

            def ln_apply(quad, b):
                v.tensor_scalar(lt[:, b, :], xres[:, quad * 4 + b, :], mv[:, b, 0:1], rstd[:, b:b + 1], ALU.subtract,
                                ALU.mult).then_inc(xn0_ready, 1)

            def h_los(st, j, quad):
                v.wait_ge(lnT_full, j * 2 + (quad + 1))
                if quad == 1:
                    v.wait_ge(h_split, j * 8 + 4)
                for c in (0, 1):
                    w, b_ = VEC["s%d" % (st + 1)] + c, VEC["o%d" % (st + 1)] + c
                    v.tensor_scalar(lh[:, c, :], ps[:, LN_BANKS[c], :], vec[:, w:w + 1], vec[:, b_:b_ + 1], ALU.mult, ALU.add).then_inc(lh_ready, 1)
                for c in range(EC):
                    v.wait_ge(h_hi, j * 8 + (quad * 4 + c + 1))
                    v.tensor_tensor(h2[1][:, c, quad * QT:(quad + 1) * QT], lh[:, c, :], h2[0][:, c, quad * QT:(quad + 1) * QT],
                                    ALU.subtract).then_inc(h_split, 1)

            def ln_second(j):
                ln_roots(j, 1)
                v.wait_ge(lnT_full, j * 2 + 1)
                for b in range(4):
                    ln_apply(1, b)

            def ctx_lo(quad, tile, n):
                v.wait_ge(c_hi, n * 2 + (quad + 1))
                v.tensor_tensor(c2[1][:, :, quad * QT:(quad + 1) * QT], tile[:], c2[0][:, :, quad * QT:(quad + 1) * QT],
                                ALU.subtract).then_inc(c_split, 1)

            def first_slot(S):
                h, st = S.h, S.st
                j = h * 3 + st
                col = (st * 5 + HV["bias_v"]) * NH, (st * 5 + HV["bv"]) * NH
                v.tensor_tensor(dbias[:].rearrange("p a b -> p (a b)")[:, 0:NH * NH:NH + 1], hv[:, col[0]:col[0] + NH],
                                hv[:, col[1]:col[1] + NH], ALU.subtract).then_inc(dbias_ready, 1)
                v.wait_ge(dbias_ready, h * 2 + (st + 1))
                if st > 0:
                    h_los(st, j, 0)
                project_lo(S, 0)
                split_one(wv, sv, wv_hi, wv_split, S.gk)
                project_lo(S, 1)
                if st > 0:
                    ln_stats(j, 1)
                project_lo(S, 2)
                project_lo(S, 3)
                if st == 0:
                    v.wait_ge(x_in[0], h * 16 + 16)
                    ln_stats(j, 0)
                    ln_roots(j, 0)
                    for b in range(4):
                        ln_apply(0, b)
                    v.wait_ge(x_in[1], h * 16 + 16)
                    ln_stats(j, 1)
                    h_los(st, j, 0)
                ln_second(j)
                project_lo(S, 4)
                h_los(st, j, 1)
                project_lo(S, 5)

            def last_slot(S):
                j = S.h * 3 + (S.st + 1)

                def bias_weights(quad):
                    idx = S.ring + quad * 9
                    v.wait_ge(ring_full, idx + 1)
                    v.tensor_scalar(pbT[:, quad * QT:(quad + 1) * QT], ps[0:NH, quad, :], 1.0, None, ALU.mult).then_inc(evacuated, 1)

                row_max(S, 0)
                normalise(S, 0)
                bias_weights(0)
                row_max(S, 1)
                probs_lo(S, 0)
                for b in range(4):
                    add_output(S.ring + (1 + b), b, (1 + b) % RING)
                    if b == 1:
                        normalise(S, 1)
                v.wait_ge(evacuated, S.ring + (5 + RING))
                ln_stats(j, 0)
                probs_lo(S, 1)
                context_lo(S, 0)
                context_lo(S, 1)
                ln_roots(j, 0)
                for b in range(4):
                    add_output(S.out0 + b, 4 + b, (S.odd + b) % RING)
                    ln_apply(0, b)
                bias_weights(1)
                for b in range(4):
                    add_output(S.ring + (10 + b), 4 + b, b % RING)
                v.wait_ge(evacuated, S.ring + (14 + RING))

            def slot(S):
                row_max(S, 0)
                normalise(S, 0)
                project_lo(S, 0)
                row_max(S, 1)
                if S.quad == 0:
                    split_one(wv, sv, wv_hi, wv_split, S.gk)
                else:
                    split_one(wo, so, wo_hi, wo_split, S.gq)
                    v.tensor_scalar(db[0][:], dbias[:, bass.ds(S.g * 2, 2), :], 1.0, None, ALU.mult).then_inc(db_hi, 1)
                    v.wait_ge(db_hi, S.gk + 1)
                    v.tensor_tensor(db[1][:], dbias[:, bass.ds(S.g * 2, 2), :], db[0][:], ALU.subtract).then_inc(db_ready, 1)
                normalise(S, 1)
                project_lo(S, 1)
                probs_lo(S, 0)
                project_lo(S, 2)
                if S.quad == 1:
                    split_q(S.gq + 1, 0)
                probs_lo(S, 1)
                context_lo(S, 0)
                project_lo(S, 3)
                if S.quad == 1:
                    split_q(S.gq + 1, 1)
                context_lo(S, 1)
                project_lo(S, 4)
                if S.quad == 1:
                    split_one(wk, sk, wk_hi, wk_split, S.gk + 1)
                project_lo(S, 5)
                v.wait_ge(bo_added, (S.h * 3 + S.st) * 2 + (S.qu + 1))
                for b in range(4):
                    add_output(S.out0 + b, S.qu * 4 + b, b % RING)

            def mlp_slot(S):
                def activation_lo(k):
                    if S.quad == 1:
                        split_q(S.gq + 1, k)
                    v.wait_ge(u_hi, S.n * 2 + (k + 1))
                    v.tensor_tensor(S.u[k][1][:], gelu[:, k, :], S.u[k][0][:], ALU.subtract).then_inc(u_split, 1)

                def add(b):
                    add_output(S.out0 + b, (1 - S.quad) * 4 + b, b % RING)

                if S.proj and S.quad == 1:
                    split_one(wo, so, wo_hi, wo_split, S.gq)
                if S.proj:
                    activation_lo(0)
                if S.outp:
                    v.wait_ge(bo_added, (S.h * 3 + 2) * 2 + (2 - S.quad))
                    add(0)
                if S.proj:
                    activation_lo(1)
                if S.outp:
                    for b in range(1, 4):
                        add(b)

            split_one(wk, sk, wk_hi, wk_split, 0)
            ctx_lo(0, lh, 0)
            v.wait_ge(bk_hi, 1)
            v.tensor_tensor(bias_k[1][:].rearrange("p (s h) -> p s h", s=2),
                            hv[:, 0:10 * NH].rearrange("p (s k h) -> p s k h", s=2, k=5)[:, :, HV["bias_k"], :],
                            bias_k[0][:].rearrange("p (s h) -> p s h", s=2), ALU.subtract).then_inc(bk_split, 1)
            v.memset(std[:], 1.0).then_inc(u_split, 2)
            v.wait_ge(bk_split, 1)
            v.wait_ge(ready, 6)
            ctx_lo(1, lt, 0)
            split_q(0, 0)
            split_q(0, 1)
            v.wait_ge(c_split, 2)
            with v.Fori(0, 2) as h:
                for st in range(2):
                    attention_slots(v, h, st, first_slot, slot, last_slot)
                j = h * 3 + 2
                h_los(2, j, 0)
                ln_stats(j, 1)
                ln_second(j)
                mlp_slots(v, h, mlp_slot, lambda: h_los(2, j, 1), lambda quad: ctx_lo(quad, lh, h + 1))

        @block.tensor
        def _(pe):
            def ring_wait(idx):
                pe.wait_ge(evacuated, idx + 1)


            def project(S, i, h_count=None):
                k, bank = S.order[i], i % RING
                ring_wait(S.ring + i)
                if k < 4:
                    hd = k // 2
                    w, x = (wq, h2) if k % 2 == 0 else (wk, c2)
                    if k % 2 == 0:
                        pe.wait_ge(wq_split, S.gq * 2 + (hd + 1))
                    else:
                        pe.wait_ge(wk_split, S.gk + 1)
                    for c in range(EC):
                        if h_count is not None:
                            pe.wait_ge(h_split, h_count + (c + 1))
                        ins = mm3(pe, ps[:, bank, :], [t[:, c, hd * P:(hd + 1) * P] for t in w],
                                  [t[:, c, S.quad * QT:(S.quad + 1) * QT] for t in x], c == 0, c == EC - 1)
                else:
                    pe.wait_ge(wv_split, S.gk + 1)
                    for b in range(2):
                        t0 = S.quad * QT + ((k - 4) * 2 + b) * L
                        for c in range(EC):
                            ins = mm3(pe, ps[:, bank, b * 256:(b + 1) * 256], [t[:, c, t0:t0 + L] for t in c2],
                                      [t[:, c, :] for t in wv], c == 0, c == EC - 1)
                ins.then_inc(ring_full, 1)

            def scores(S, hd):
                late = isinstance(S.g, int) and S.g == 0
                if hd == 0 or late:
                    pe.wait_ge(evacuated, S.projected + (RING - 1 if late and hd == 0 else RING))
                pe.wait_ge(exp_done, S.n * 2 + (hd - 1))
                for b in range(4):
                    o = (b % 2) * KW
                    ins = mm3(pe, ps[:, BANK_SC + b // 2, o:o + KW], [t[:, b * L:(b + 1) * L] for t in qT[hd]],
                              [t[:, b, :] for t in kT[hd]], True, True)
                ins.then_inc(sc_full, 1)

            def transpose(S, hd):
                pe.wait_ge(norm_done, S.n * 2 + (hd - 1))
                for b in range(4):
                    ins = pe.transpose(ps[:, BANK_TR + hd, b * L:(b + 1) * L], pr[hd][:, b, 0:L], ident[:])
                ins.then_inc(tr_full, 1)

            def context(S, hd):
                pe.wait_ge(pt_split, S.n * 2 + (hd - 1))
                pe.wait_ge(ct_split, S.n * 2 + (hd - 1))
                for b in range(4):
                    ins = mm3(pe, ps[:, BANK_PV, b * L:(b + 1) * L], [t[:, b, hd * P:(hd + 1) * P] for t in vT],
                              [t[:, b * L:(b + 1) * L] for t in pT[hd]], True, True)
                ins.then_inc(pv_full, 1)

            def outputs(S):
                pe.wait_ge(ct_split, S.n * 2 + 1)
                for b in range(4):
                    ring_wait(S.out0 + b)
                    for hd in range(2):
                        ins = mm3(pe, ps[:, (S.odd + b) % RING, :], [t[:, b * L:(b + 1) * L] for t in cT[hd]],
                                  [t[:, hd, :] for t in wo], hd == 0, hd == 1)
                    ins.then_inc(ring_full, 1)

            def bias_rows(S):
                pe.wait_ge(wo_split, S.gq + 2)
                pe.wait_ge(db_ready, S.gk + 1)
                for hd in range(2):
                    for i, (a, b) in enumerate(((0, 0), (0, 1), (1, 0))):
                        pe.matmul(ps[0:NH, BANK_BV, :], db[a][:, hd, :], wo[b][:, hd, :],
                                  start=isinstance(S.g, int) and hd == 0 and i == 0, stop=False, skip_group_check=True)

            def ln_transpose(j, quad):
                for b in range(4):
                    pe.wait_ge(xn0_ready, j * 8 + (quad * 4 + b + 1))
                    for c in range(EC):
                        ins = pe.transpose(ps[:, LN_BANKS[c], b * P:(b + 1) * P], lt[:, b, c * P:(c + 1) * P], ident[:])
                ins.then_inc(lnT_full, 1)

            def first_slot(S):
                j = S.h * 3 + S.st
                if S.st == 0:
                    pe.wait_ge(c_split, S.h * 2 + 1)
                else:
                    ln_transpose(j, 0)
                for i in range(4):
                    project(S, i)
                if S.st == 0:
                    ln_transpose(j, 0)
                project(S, 4, j * 8)
                ln_transpose(j, 1)
                project(S, 5)
                if S.st == 0:
                    pe.wait_ge(c_split, S.h * 2 + 2)

            def last_slot(S):
                def bias_weights(quad):
                    idx = S.ring + quad * 9
                    ring_wait(idx)
                    for b in range(4):
                        ins = pe.transpose(ps[0:NH, quad, b * P:(b + 1) * P], pb[:, quad * 4 + b, :], ident[:])
                    ins.then_inc(ring_full, 1)

                def bias_outputs(quad):
                    idx = S.ring + (quad * 9 + 1)
                    pe.wait_ge(evacuated, idx + RING)
                    for b in range(4):
                        ring_wait(idx + b)
                        pe.matmul(ps[:, (1 + quad + b) % RING, :], pbT[:, (quad * 4 + b) * P:(quad * 4 + b + 1) * P], bvs[:],
                                  start=True, stop=True).then_inc(ring_full, 1)

                scores(S, 0)
                bias_weights(0)
                scores(S, 1)
                transpose(S, 0)
                pe.wait_ge(bvs_ready, S.h * 2 + (S.st + 1))
                bias_outputs(0)
                transpose(S, 1)
                context(S, 0)
                context(S, 1)
                outputs(S)
                bias_weights(1)
                bias_outputs(1)

            def slot(S):
                first = isinstance(S.g, int)
                scores(S, 0)
                project(S, 0, (S.h * 3 + S.st) * 8 + 4 if first else None)
                scores(S, 1)
                project(S, 1)
                transpose(S, 0)
                project(S, 2)
                transpose(S, 1)
                context(S, 0)
                project(S, 3)
                context(S, 1)
                project(S, 4)
                project(S, 5)
                if S.quad == 1:
                    bias_rows(S)
                outputs(S)

            def mlp_slot(S):
                if S.proj:
                    for k in range(2):
                        pe.wait_ge(wq_split, S.gq * 2 + (k + 1))
                        if S.outp:
                            pe.wait_ge(gelu_ready, S.n * 2 + (k - 1))
                        for c in range(EC):
                            if isinstance(S.g, int) and S.g == 0 and k == 0:
                                pe.wait_ge(h_split, (S.h * 3 + 2) * 8 + (S.quad * 4 + c + 1))
                            ins = mm3(pe, ps[:, BANK_SC + k, :], [t[:, c, k * P:(k + 1) * P] for t in wq],
                                      [t[:, c, S.quad * QT:(S.quad + 1) * QT] for t in h2], c == 0, c == EC - 1)
                        ins.then_inc(fc1_full, 1)
                if S.outp:
                    pe.wait_ge(u_split, S.n * 2 + 2)
                    pe.wait_ge(wo_split, (S.gq + 2) if S.quad == 1 else (S.gq + 1))
                    for b in range(4):
                        ring_wait(S.out0 + b)
                        for k in range(2):
                            ins = mm3(pe, ps[:, b % RING, :], [t[:, b * L:(b + 1) * L] for t in S.u_last[k]],
                                      [t[:, k, :] for t in wo], k == 0, k == 1)
                        ins.then_inc(ring_full, 1)

            pe.wait_ge(const_in, 48)
            pe.wait_ge(ready, 6)
            with pe.Fori(0, 2) as h:
                for st in range(2):
                    attention_slots(pe, h, st, first_slot, slot, last_slot)
                j = h * 3 + 2
                ln_transpose(j, 0)
                mlp_slots(pe, h, mlp_slot, lambda: ln_transpose(j, 1), lambda quad: None)


def build(nc, io, out):
    x2 = nc.dram_tensor("x2_dram", (B, L, E), F32, kind="Internal").ap()
    time_mix(nc, io, x2)
    x3 = nc.dram_tensor("x3_dram", (B, L, E), F32, kind="Internal").ap()
    channel_mix(nc, io, x2, x3)
    cross_attend(nc, io, x3, out)


def vec_table(a):
    return np.ascontiguousarray(a.reshape(-1, EC, P).transpose(2, 0, 1).reshape(P, -1))


def w_tiles(w, m):
    k, n = w.shape
    return np.ascontiguousarray(w.reshape(k // P, P, n // m, m).transpose(2, 1, 0, 3))


def layouts(i):
    a = {}
    p = "L0_xattn_"
    a["x"] = i["x"]
    ctx = i["ctx_2048"]
    vecs = [i[p + n] for n in ("ln1_w", "ln1_b", "ln2_w", "ln2_b", "maa_x")] + [i[p + "maa_stack"][m] for m in range(5)]
    vecs += [i[p + "time_decay"], i[p + "faaaa"].reshape(E), i[p + "gn_w"], i[p + "gn_b"], i[p + "ffn_maa_k"], i[p + "ffn_maa_r"]]
    vecs += [i["L1_xattn_" + n] for n in ("ln1_scale", "ln1_offset", "ln2_scale", "ln2_offset", "ln_mlp_scale", "ln_mlp_offset")]
    a["vec"] = vec_table(np.stack(vecs))
    a["ident"] = np.eye(P, dtype=np.float32)
    same = np.kron(np.eye(8, dtype=np.float32), np.ones((HS, HS), np.float32))
    a["head_sum"] = same
    a["head_mean"] = same / HS
    a["head_mean4"] = np.tile(np.kron(np.eye(8, dtype=np.float32), np.ones((HS, 1), np.float32)), (1, 4)) / HS
    unpack = np.zeros((P, EC, P), np.float32)
    for c in range(EC):
        for h in range(8):
            unpack[32 * c + h, c, h * HS:(h + 1) * HS] = 1
    a["unpack"] = unpack
    pick = np.zeros((P, P + HS - 1), np.float32)
    pick[np.arange(P), np.arange(P) // HS * HS + HS - 1] = 1
    a["pick_k"] = pick
    spread = np.zeros((P, HS, P), np.float32)
    for d in range(HS):
        spread[:, d, :] = same * (np.arange(P)[:, None] % HS == d)
    a["spread_v"] = spread.reshape(P, HS * P)
    a["prev1"] = np.ascontiguousarray(ctx[:, 1, :].reshape(B, EC, P).transpose(2, 1, 0))
    a["prev0"] = np.ascontiguousarray(ctx[:, 0, :].reshape(B, EC, P).transpose(2, 1, 0))
    a["s0"] = np.ascontiguousarray(ctx[:, 2:2 + HS, :].reshape(NQ, 4, EC, P, HS).transpose(0, 3, 2, 4, 1))
    a["l0w"] = np.stack([w_tiles(i[p + n].T, E)[0] for n in ("Wr", "Wk", "Wv", "Wg", "Wo", "ffn_Wk", "ffn_Wr", "ffn_Wv")])
    a["lora1"] = w_tiles(i[p + "maa_w1"], 160)[0]
    a["dec1"] = w_tiles(i[p + "decay_w1"], 64)[0]
    a["lora2"] = i[p + "maa_w2"].reshape(160, E)
    a["dec2"] = i[p + "decay_w2"]
    p = "L1_xattn_"
    a["ctxT"] = ctx.reshape(B * L, EC, P).transpose(2, 1, 0)
    a["head_vec"] = np.stack([i[p + n + s].reshape(NH, KD) for s in "12" for n in ("bq", "bk", "bv", "bias_k", "bias_v")]
                             + [i[p + "b_fc1"].reshape(NH, P)]).transpose(2, 0, 1).reshape(P, -1)
    a["bo"] = np.broadcast_to(np.stack([i[p + "bo1"], i[p + "bo2"], i[p + "b_fc2"]]), (P, 3, E))
    q = [w_tiles(i[p + n], 256) for n in ("wq1", "wq2", "w_fc1")]
    a["wq"] = np.concatenate(q + [q[0][0:1]])
    k = [w_tiles(i[p + n], 256) for n in ("wk1", "wk2")]
    a["wk"] = np.concatenate(k + [k[0][0:1]])
    v = [w_tiles(i[p + n], 256) for n in ("wv1", "wv2")]
    a["wv"] = np.concatenate(v + [v[0][0:1]])
    a["wo"] = np.concatenate([i[p + n].reshape(NH // 2, 2, P, E).transpose(0, 2, 1, 3) for n in ("wo1", "wo2", "w_fc2")])
    return {k: np.ascontiguousarray(v) for k, v in a.items()}


def kernel(**inputs):
    import concourse.bacc as _bacc
    from concourse.bass_utils import run_bass_kernel_spmd as _run

    nc = _bacc.Bacc("TRN2", target_bir_lowering=False, num_devices=1)
    arrays = layouts({k: np.asarray(v) for k, v in inputs.items()})
    io = {n: nc.dram_tensor(f"in_{n}", a.shape, mybir.dt.from_np(a.dtype), kind="ExternalInput").ap() for n, a in arrays.items()}
    out = nc.dram_tensor("out_dram", (B, L, E), F32, kind="ExternalOutput").ap()
    build(nc, io, out)
    r = _run(nc, [{f"in_{n}": a for n, a in arrays.items()}], core_ids=[0])
    return r.results[0]["out_dram"]
```
